# Optimizing a Trainium2 kernel written in Bass

```python
import numpy as np
import jax
import jax.numpy as jnp

def _softmax(x, axis=-1):
    return jax.nn.softmax(x, axis=axis)

def _gelu(x):
    return jax.nn.gelu(x, approximate=True)

def _silu(x):
    return jax.nn.silu(x)

def _sigmoid(x):
    return jax.nn.sigmoid(x)

def _layernorm(x, axis=-1, eps=1e-05):
    m = jnp.mean(x, axis=axis, keepdims=True)
    v = jnp.var(x, axis=axis, keepdims=True)
    return (x - m) / jnp.sqrt(v + eps)

def _scatter_add(tgt, idx, src, axis=0):
    return tgt.at[idx].add(src)

def _segment_sum(src, seg, n):
    return jax.ops.segment_sum(src, seg, n)
kernel_name = 'mk_macaron_d1_jaxref_r4_d6c1f9'

def setup_inputs(seed: int=0):
    np.random.seed(seed)
    _w = jnp.asarray

    def _L0_attn_setup():
        import jax, jax.numpy as jnp
        import numpy as np
        D_MODEL = 256
        EXPAND = 2
        D_INNER = D_MODEL * EXPAND
        D_STATE = 16
        FFN_HIDDEN = (D_MODEL * 4 * 2 // 3 + 63) // 64 * 64
        EPS = 1e-06

        def rmsnorm(x, w):
            return x * jax.lax.rsqrt(jnp.mean(x * x, axis=-1, keepdims=True) + EPS) * w

        def selective_scan(z, dt_w, dt_b, x_proj_w, A_log, Dp):
            dt = jax.nn.softplus(jnp.einsum('bld,ed->ble', z, dt_w) + dt_b)
            BC = jnp.einsum('bld,nd->bln', z, x_proj_w)
            Bm, Cm = (BC[..., :D_STATE], BC[..., D_STATE:])
            A = -jnp.exp(A_log)
            dA = jnp.exp(dt[..., None] * A)
            dBz = (dt * z)[..., None] * Bm[:, :, None, :]

            def combine(e1, e2):
                a1, b1 = e1
                a2, b2 = e2
                return (a1 * a2, a2 * b1 + b2)
            _, h = jax.lax.associative_scan(combine, (dA, dBz), axis=1)
            y = jnp.einsum('bldn,bln->bld', h, Cm) + z * Dp
            return y
        key = jax.random.key(seed)
        ks = jax.random.split(key, 12)
        s = 0.02
        inp = {'x': jax.random.normal(ks[0], (2, 256, D_MODEL), dtype=jnp.float32), 'norm1_w': jnp.ones((D_MODEL,), jnp.float32), 'in_proj_w': jax.random.normal(ks[1], (D_INNER, D_MODEL), jnp.float32) * s, 'gate_proj_w': jax.random.normal(ks[2], (D_INNER, D_MODEL), jnp.float32) * s, 'dt_w': jax.random.normal(ks[3], (D_INNER, D_INNER), jnp.float32) * s, 'dt_b': jnp.full((D_INNER,), -2.0, jnp.float32), 'x_proj_w': jax.random.normal(ks[4], (2 * D_STATE, D_INNER), jnp.float32) * s, 'A_log': jnp.broadcast_to(jnp.log(jnp.arange(1, D_STATE + 1, dtype=jnp.float32)), (D_INNER, D_STATE)).copy(), 'Dp': jnp.ones((D_INNER,), jnp.float32), 'out_proj_w': jax.random.normal(ks[5], (D_MODEL, D_INNER), jnp.float32) * s, 'ffn_norm_w': jnp.ones((D_MODEL,), jnp.float32), 'ffn_gate_w': jax.random.normal(ks[6], (FFN_HIDDEN, D_MODEL), jnp.float32) * s, 'ffn_up_w': jax.random.normal(ks[7], (FFN_HIDDEN, D_MODEL), jnp.float32) * s, 'ffn_down_w': jax.random.normal(ks[8], (D_MODEL, FFN_HIDDEN), jnp.float32) * s}
        return inp
    _L0_attn_in = _L0_attn_setup()

    def _L0_ffn_setup():
        import jax, jax.numpy as jnp
        import numpy as np
        D, H, E, K, S = (256, 512, 8, 2, 1)
        B, L = (4, 512)
        key = jax.random.key(seed)
        ks = jax.random.split(key, 9)
        std = 0.02
        return {'x': jax.random.normal(ks[0], (B, L, D), dtype=jnp.float32), 'router_w': jax.random.normal(ks[1], (E, D), dtype=jnp.float32) * std, 'experts_bias': jnp.zeros((E,), dtype=jnp.float32), 'w1': jax.random.normal(ks[2], (E, D, H), dtype=jnp.float32) * std, 'w3': jax.random.normal(ks[3], (E, D, H), dtype=jnp.float32) * std, 'w2': jax.random.normal(ks[4], (E, H, D), dtype=jnp.float32) * std, 'sw1': jax.random.normal(ks[5], (S, D, H), dtype=jnp.float32) * std, 'sw3': jax.random.normal(ks[6], (S, D, H), dtype=jnp.float32) * std, 'sw2': jax.random.normal(ks[7], (S, H, D), dtype=jnp.float32) * std}
    _L0_ffn_in = _L0_ffn_setup()
    _d = {'L0_attn_x': _L0_attn_in['x'], 'L0_attn_norm1_w': _L0_attn_in['norm1_w'], 'L0_attn_in_proj_w': _L0_attn_in['in_proj_w'], 'L0_attn_gate_proj_w': _L0_attn_in['gate_proj_w'], 'L0_attn_dt_w': _L0_attn_in['dt_w'], 'L0_attn_dt_b': _L0_attn_in['dt_b'], 'L0_attn_x_proj_w': _L0_attn_in['x_proj_w'], 'L0_attn_A_log': _L0_attn_in['A_log'], 'L0_attn_Dp': _L0_attn_in['Dp'], 'L0_attn_out_proj_w': _L0_attn_in['out_proj_w'], 'L0_attn_ffn_norm_w': _L0_attn_in['ffn_norm_w'], 'L0_attn_ffn_gate_w': _L0_attn_in['ffn_gate_w'], 'L0_attn_ffn_up_w': _L0_attn_in['ffn_up_w'], 'L0_attn_ffn_down_w': _L0_attn_in['ffn_down_w'], 'L0_ffn_router_w': _L0_ffn_in['router_w'], 'L0_ffn_experts_bias': _L0_ffn_in['experts_bias'], 'L0_ffn_w1': _L0_ffn_in['w1'], 'L0_ffn_w3': _L0_ffn_in['w3'], 'L0_ffn_w2': _L0_ffn_in['w2'], 'L0_ffn_sw1': _L0_ffn_in['sw1'], 'L0_ffn_sw3': _L0_ffn_in['sw3'], 'L0_ffn_sw2': _L0_ffn_in['sw2']}
    _x0 = _d['L0_attn_x']
    _d['L0_attn_x'] = jax.random.normal(jax.random.fold_in(jax.random.key(seed), 1), (1, 4096, 256), dtype=_x0.dtype)
    del _x0
    return _d

def reference(L0_attn_x, L0_attn_norm1_w, L0_attn_in_proj_w, L0_attn_gate_proj_w, L0_attn_dt_w, L0_attn_dt_b, L0_attn_x_proj_w, L0_attn_A_log, L0_attn_Dp, L0_attn_out_proj_w, L0_attn_ffn_norm_w, L0_attn_ffn_gate_w, L0_attn_ffn_up_w, L0_attn_ffn_down_w, L0_ffn_router_w, L0_ffn_experts_bias, L0_ffn_w1, L0_ffn_w3, L0_ffn_w2, L0_ffn_sw1, L0_ffn_sw3, L0_ffn_sw2):

    def _L0_attn_ref(x, norm1_w, in_proj_w, gate_proj_w, dt_w, dt_b, x_proj_w, A_log, Dp, out_proj_w, ffn_norm_w, ffn_gate_w, ffn_up_w, ffn_down_w):
        import jax, jax.numpy as jnp
        import numpy as np
        D_MODEL = 256
        EXPAND = 2
        D_INNER = D_MODEL * EXPAND
        D_STATE = 16
        FFN_HIDDEN = (D_MODEL * 4 * 2 // 3 + 63) // 64 * 64
        EPS = 1e-06

        def rmsnorm(x, w):
            return x * jax.lax.rsqrt(jnp.mean(x * x, axis=-1, keepdims=True) + EPS) * w

        def selective_scan(z, dt_w, dt_b, x_proj_w, A_log, Dp):
            dt = jax.nn.softplus(jnp.einsum('bld,ed->ble', z, dt_w) + dt_b)
            BC = jnp.einsum('bld,nd->bln', z, x_proj_w)
            Bm, Cm = (BC[..., :D_STATE], BC[..., D_STATE:])
            A = -jnp.exp(A_log)
            dA = jnp.exp(dt[..., None] * A)
            dBz = (dt * z)[..., None] * Bm[:, :, None, :]

            def combine(e1, e2):
                a1, b1 = e1
                a2, b2 = e2
                return (a1 * a2, a2 * b1 + b2)
            _, h = jax.lax.associative_scan(combine, (dA, dBz), axis=1)
            y = jnp.einsum('bldn,bln->bld', h, Cm) + z * Dp
            return y
        residual = x
        h = rmsnorm(x, norm1_w)
        z = jnp.einsum('bld,ed->ble', h, in_proj_w)
        gate = jax.nn.sigmoid(jnp.einsum('bld,ed->ble', h, gate_proj_w))
        z = z * gate
        ssm_out = selective_scan(z, dt_w, dt_b, x_proj_w, A_log, Dp)
        x = residual + jnp.einsum('ble,de->bld', ssm_out, out_proj_w)
        hn = rmsnorm(x, ffn_norm_w)
        ff = jnp.einsum('blh,dh->bld', jax.nn.silu(jnp.einsum('bld,hd->blh', hn, ffn_gate_w)) * jnp.einsum('bld,hd->blh', hn, ffn_up_w), ffn_down_w)
        return x + ff

    def _L0_ffn_ref(x, router_w, experts_bias, w1, w3, w2, sw1, sw3, sw2):
        import jax, jax.numpy as jnp
        import numpy as np
        D, H, E, K, S = (256, 512, 8, 2, 1)
        B, L = (4, 512)
        b, l, d = x.shape
        xf = x.reshape(-1, d)
        sg = jnp.einsum('td,sdh->tsh', xf, sw1)
        su = jnp.einsum('td,sdh->tsh', xf, sw3)
        shared_out = jnp.einsum('tsh,shd->td', jax.nn.silu(sg) * su, sw2)
        logits = xf @ router_w.T + experts_bias
        rw, sel = jax.lax.top_k(logits, K)
        rw = jax.nn.softmax(rw.astype(jnp.float32), axis=-1).astype(x.dtype)
        cw = (jax.nn.one_hot(sel, E, dtype=x.dtype) * rw[..., None]).sum(axis=1)
        g = jnp.einsum('td,edh->teh', xf, w1)
        u = jnp.einsum('td,edh->teh', xf, w3)
        eo = jax.nn.silu(g) * u
        moe_out = jnp.einsum('te,teh,ehd->td', cw, eo, w2)
        return (moe_out + shared_out).reshape(b, l, d)
    x = L0_attn_x
    x = x + 0.5 * _L0_ffn_ref(_layernorm(x, axis=-1), L0_ffn_router_w, L0_ffn_experts_bias, L0_ffn_w1, L0_ffn_w3, L0_ffn_w2, L0_ffn_sw1, L0_ffn_sw3, L0_ffn_sw2)
    x = x + _L0_attn_ref(_layernorm(x, axis=-1), L0_attn_norm1_w, L0_attn_in_proj_w, L0_attn_gate_proj_w, L0_attn_dt_w, L0_attn_dt_b, L0_attn_x_proj_w, L0_attn_A_log, L0_attn_Dp, L0_attn_out_proj_w, L0_attn_ffn_norm_w, L0_attn_ffn_gate_w, L0_attn_ffn_up_w, L0_attn_ffn_down_w)
    x = x + 0.5 * _L0_ffn_ref(_layernorm(x, axis=-1), L0_ffn_router_w, L0_ffn_experts_bias, L0_ffn_w1, L0_ffn_w3, L0_ffn_w2, L0_ffn_sw1, L0_ffn_sw3, L0_ffn_sw2)
    return x

_drawn_inputs = setup_inputs


def setup_inputs(seed=0):
    import zlib

    import numpy as np

    out = dict(_drawn_inputs(seed))
    spreads = {'L0_attn_norm1_w': (1.0, 0.6),
     'L0_attn_dt_b': (-2.0, 0.6),
     'L0_attn_Dp': (1.0, 0.6),
     'L0_attn_ffn_norm_w': (1.0, 0.6),
     'L0_ffn_experts_bias': (0.0, 0.8)}
    factors = {'L0_attn_gate_proj_w': 8.0,
     'L0_attn_dt_w': 8.0,
     'L0_attn_x_proj_w': 8.0,
     'L0_attn_A_log': 8.0,
     'L0_attn_ffn_gate_w': 3.714,
     'L0_attn_ffn_up_w': 3.665,
     'L0_attn_ffn_down_w': 3.657,
     'L0_ffn_router_w': 5.224,
     'L0_ffn_w1': 4.489,
     'L0_ffn_w3': 4.444,
     'L0_ffn_w2': 4.438,
     'L0_ffn_sw1': 3.187,
     'L0_ffn_sw3': 3.134,
     'L0_ffn_sw2': 3.153}
    for name, (base, spread) in spreads.items():
        noise = np.random.default_rng([zlib.crc32(name.encode()), seed]).standard_normal(out[name].shape)
        drawn = base * np.exp(spread * noise) if base else spread * noise
        out[name] = jnp.asarray(drawn.astype(out[name].dtype))
    for name, factor in factors.items():
        out[name] = (out[name] * factor).astype(out[name].dtype)
    return out
```

```python
from contextlib import ExitStack, contextmanager

import numpy as np

import concourse.bass as bass
from concourse import mybir

F32 = mybir.dt.float32
I32 = mybir.dt.int32
ALU = mybir.AluOpType
ACT = mybir.ActivationFunctionType
X = mybir.AxisListType.X

P = 128
T = 4096
D = 256
DC = D // P
TT = T // P

E = 8
K = 2
H = 512
HC = H // P
SHARED = E
UP = DC * H
EXPERT = 2 * UP + HC * D
SLOT_TILES = K * T // P + E - 1
SLOTS = SLOT_TILES * P
ROW = D + 2
ID, WEIGHT = D, D + 1
LN_EPS = 1e-5
RMS_EPS = 1e-6
RG = 2
GROUPS = TT // RG

C_IDENT = 0
C_TRI = C_IDENT + P
C_ONES = C_TRI + P
C_TOKEN = C_ONES + P
C_START = C_TOKEN + TT
C_TILE = C_START + TT
C_RANK = C_TILE + SLOT_TILES
C_FILL = C_RANK + E
CONSTS = C_FILL + ROW


def constants():
    c = np.zeros((P, CONSTS), np.float32)
    p = np.arange(P)
    c[:, C_IDENT:C_IDENT + P] = np.eye(P)
    c[:, C_TRI:C_TRI + P] = p[:, None] < p[None, :]
    c[:, C_ONES:C_ONES + P] = 1.0
    c[:, C_TOKEN:C_TOKEN + TT] = np.arange(TT)[None, :] * P + p[:, None]
    c[:, C_START:C_START + TT] = np.arange(TT) * P
    c[:, C_TILE:C_TILE + SLOT_TILES] = np.arange(SLOT_TILES)
    c[:, C_RANK:C_RANK + E] = E - np.arange(E)
    c[:, C_FILL + ID] = T + p
    return c


def wait(eng, sem, value):
    if not isinstance(value, int) or value > 0:
        eng.wait_ge(sem, value)


@contextmanager
def phase(nc):
    sems = []

    def new(name):
        sems.append(nc.alloc_semaphore(name=name))
        return sems[-1]
    yield new
    nc.clear_and_free_semaphores(sems)
    nc.all_engine_barrier()


def moe(nc, tag, src, dst, slots, weights, consts, const, W, later=()):
    ident = const[:, C_IDENT:C_IDENT + P]
    ones = const[:, C_ONES:C_ONES + P]
    src_g = src[0:T, :].rearrange("(g t p) d -> g p t d", t=RG, p=P)
    src_t = src[0:T, :].rearrange("(t p) d -> t p d", p=P)
    dst_t = dst.rearrange("(t p) d -> t p d", p=P)
    slots_t = slots.rearrange("(t p) d -> t p d", p=P)

    with phase(nc) as new, ExitStack() as ctx:
        def sb(name, shape, dt=F32):
            return ctx.enter_context(nc.sbuf_tensor(f"{tag}_{name}", shape, dt))

        def pb(name):
            return ctx.enter_context(nc.psum_tensor(f"{tag}_{name}", [P, 512], F32))

        def sem(name):
            return new(f"{tag}_{name}")

        bias = sb("bias", [P, E])
        router = sb("router", [P, DC, E])
        rows = sb("rows", [P, TT, ROW])
        xin = sb("xin", [P, 2, RG, D])
        xnb = sb("xnb", [P, 2, RG, D])
        xTr = sb("xTr", [P, DC, RG * P])
        stats = sb("stats", [P, 2, RG, 6])
        mv = sb("mv", [P, 2, RG, 2])
        ve = sb("ve", [P, 2, RG])
        rstd = sb("rstd", [P, 2, RG])
        nhalf = sb("nhalf", [P, RG])
        L = sb("L", [P, TT, E])
        scratch = sb("scratch", [P, TT, E])
        oh1 = sb("oh1", [P, TT, E])
        oh2 = sb("oh2", [P, TT, E])
        incl = sb("incl", [P, TT, E])
        cmp = sb("cmp", [P, E, TT])
        m1 = sb("m1", [P, TT])
        m2 = sb("m2", [P, TT])
        r1 = sb("r1", [P, TT])
        ex = sb("ex", [P, TT])
        w0 = sb("w0", [P, TT])
        w1 = sb("w1", [P, TT])
        posf = sb("posf", [P, 2, TT])
        pos = sb("pos", [P, 2, TT], I32)
        tiles = sb("tiles", [P, E])
        tend = sb("tend", [P, E])
        base = sb("base", [P, E])
        tile_cmp = sb("tile_cmp", [1, SLOT_TILES, E])
        tile_sum = sb("tile_sum", [1, SLOT_TILES])
        tile_expert = sb("tile_expert", [1, SLOT_TILES], I32)
        xs = sb("xs", [P, 2, ROW])
        xres = sb("xres", [P, 2, D])
        xT = sb("xT", [P, DC * P])
        sg = sb("sg", [P, H])
        hs = sb("hs", [P, H])
        hT = sb("hT", [P, HC * P])
        ys = sb("ys", [P, 2, D])
        ids = sb("ids", [P, 2, 1], I32)
        wt = sb("wt", [P, 2, 1])

        pX = pb("pX")
        pL = pb("pL")
        pG = pb("pG")
        pU = pb("pU")
        pH = pb("pH")
        pY = pb("pY")

        s_const = sem("const")
        s_bias = sem("bias")
        s_w = [sem(f"w{e}") for e in range(E + 1)]
        s_fill = sem("fill")
        s_spare = sem("spare")
        s_xin = [sem(f"xin{q}") for q in range(2)]
        s_nhalf = sem("nhalf")
        s_bns = sem("bns")
        s_bna = sem("bna")
        s_ve = sem("ve")
        s_rs = sem("rs")
        s_norm = sem("norm")
        s_tr = sem("tr")
        s_xTr = sem("xTr")
        s_lg = sem("lg")
        s_L = sem("L")
        s_row = sem("row")
        s_chain = sem("chain")
        s_diff = sem("diff")
        s_ex = sem("ex")
        s_oh = sem("oh")
        s_prefix = sem("prefix")
        s_pos = sem("pos")
        s_map = sem("map")
        s_colw = sem("colw")
        s_scat = sem("scat")
        s_sent = sem("sent")

        block = ctx.enter_context(nc.Block())

        def pipe(name):
            names = ("xs", "xt", "xT", "g", "u", "sg", "h", "ht", "hT", "y", "ys", "used", "xsf")
            d = {n: sem(f"{name}_{n}") for n in names}
            d["load"] = [sem(f"{name}_load{q}") for q in range(2)]
            d["store"] = [sem(f"{name}_store{q}") for q in range(2)]
            return d

        S = pipe("s")
        R = pipe("r")
        s_add = sem("add")

        def over_tiles(eng, n, step):
            step(0, 0)
            step(1, 1)
            pairs = (n - 3) // 2
            with eng.Fori(1, 1 + pairs) as j:
                step(j * 2, 0)
                step(j * 2 + 1, 1)
            for i in range(2 + 2 * pairs, n):
                step(i, i % 2)

        @block.sync
        def _(sp):
            sp.dma_start(const[:, :], consts).then_inc(s_const, 16)
            sp.dma_start(router[:, :, :], weights["router"]).then_inc(s_bias, 16)
            sp.dma_start(bias[:, :], weights["bias"].partition_broadcast(P)).then_inc(s_bias, 16)

            def load_group(g, q):
                wait(sp, s_norm, RG * (g - 1))
                sp.dma_start(xin[:, q, :, :], src_g[bass.ds(g, 1)].rearrange("a p t d -> p (a t) d")).then_inc(s_xin[q], 16)
            load_group(0, 0)
            load_group(1, 1)
            sp.dma_start(W[:, SHARED, :], weights["moe"][SHARED]).then_inc(s_w[SHARED], 16)
            with sp.Fori(1, GROUPS // 2) as j:
                load_group(j * 2, 0)
                load_group(j * 2 + 1, 1)

            def shared_load(i, q):
                wait(sp, S["ys"], i - 1)
                sp.dma_start(xres[:, q, :], src_t[bass.ds(i, 1)].rearrange("a p d -> p (a d)")).then_inc(S["load"][q], 16)

            def shared_store(i, q):
                sp.wait_ge(S["ys"], i + 1)
                sp.dma_start(dst_t[bass.ds(i, 1)].rearrange("a p d -> p (a d)"), ys[:, q, :]).then_inc(S["store"][q], 16)
            shared_load(0, 0)
            shared_load(1, 1)
            for e in range(E):
                sp.dma_start(W[:, e, :], weights["moe"][e]).then_inc(s_w[e], 16)
            for to, from_, s in later:
                sp.dma_start(to, from_).then_inc(s, 16)
            with sp.Fori(0, TT // 2 - 1) as j:
                shared_store(j * 2, 0)
                shared_load(j * 2 + 2, 0)
                shared_store(j * 2 + 1, 1)
                shared_load(j * 2 + 3, 1)
            shared_store(TT - 2, 0)
            shared_store(TT - 1, 1)

            sp.wait_ge(s_sent, 1)

            def slot_load(i, q):
                wait(sp, R["used"], i - 1)
                sp.dma_start(xs[:, q, :], slots_t[bass.ds(i, 1)].rearrange("a p d -> p (a d)")).then_inc(R["load"][q], 16)
            over_tiles(sp, SLOT_TILES, slot_load)

        @block.gpsimd
        def _(pool):
            pool.memset(nhalf[:, :], -0.5).then_inc(s_nhalf, 1)
            pool.wait_ge(s_nhalf, 1)

            def group(g, q):
                pool.wait_ge(s_ve, g + 1)
                nc.gpsimd.tensor_tensor(rstd[:, q, :], ve[:, q, :], nhalf[:, :], ALU.pow).then_inc(s_rs, 1)
                if not isinstance(g, int) or g > 1:
                    nc.gpsimd.tensor_copy(rows[:, bass.ds((g - 2) * RG, RG), 0:D], xnb[:, q, :, :]).then_inc(s_row, 1)
            over_tiles(pool, GROUPS, group)
            pool.wait_ge(s_norm, RG * GROUPS)
            for q in range(2):
                at = TT - (2 - q) * RG
                nc.gpsimd.tensor_copy(rows[:, at:at + RG, 0:D], xnb[:, q, :, :]).then_inc(s_row, 1)
            pool.wait_ge(s_const, 16)
            nc.gpsimd.tensor_copy(rows[:, :, ID:ID + 1], const[:, C_TOKEN:C_TOKEN + TT].unsqueeze(2)).then_inc(s_colw, 1)
            pool.wait_ge(s_fill, 16)
            pool.wait_ge(s_pos, 1)
            pool.wait_ge(s_row, GROUPS)
            for k in range(K):
                wait(pool, s_scat, 16 * TT * k)
                nc.gpsimd.tensor_copy(rows[:, :, WEIGHT:WEIGHT + 1], (w0, w1)[k][:, :].unsqueeze(2)).then_inc(s_colw, 1)
                pool.wait_ge(s_colw, 2 + k)
                for t in range(TT):
                    nc.gpsimd.indirect_dma_start(
                        out=slots, out_offset=bass.IndirectOffsetOnAxis(ap=pos[:, k, t:t + 1], axis=0),
                        in_=rows[:, t, :], in_offset=None).then_inc(s_scat, 16)
            pool.wait_ge(s_scat, 16 * TT * K)
            nc.gpsimd.memset(nhalf[:, 0:1], 0.0).then_inc(s_sent, 1)

            for q in range(2):
                pool.wait_ge(S["store"][q], 16 * TT // 2)
            pool.wait_ge(s_spare, 16)
            for i in range(SLOT_TILES):
                wait(pool, s_add, 16 * i)
                pool.wait_ge(R["ys"], i + 1)
                nc.gpsimd.indirect_dma_start(
                    out=dst, out_offset=bass.IndirectOffsetOnAxis(ap=ids[:, i % 2, :], axis=0),
                    in_=ys[:, i % 2, :], in_offset=None, compute_op=ALU.add).then_inc(s_add, 16)
            pool.wait_ge(s_add, 16 * SLOT_TILES)

        @block.scalar
        def _(act):
            act.wait_ge(s_const, 16)
            act.dma_start(slots_t.rearrange("t p d -> p t d"),
                          const[:, C_FILL:C_FILL + ROW].unsqueeze(1).broadcast_to([P, SLOT_TILES, ROW])).then_inc(s_fill, 16)
            act.dma_start(dst_t[TT], const[:, C_FILL:C_FILL + D]).then_inc(s_spare, 16)

            def group(g, q):
                act.wait_ge(s_tr, g + 1)
                wait(act, s_lg, g)
                nc.scalar.activation(xTr[:, :, :].rearrange("p c n -> p (c n)"), pX[:, :], ACT.Copy).then_inc(s_xTr, 1)
            over_tiles(act, GROUPS, group)
            act.wait_ge(s_diff, 1)
            nc.scalar.activation(ex[:, :], r1[:, :], ACT.Exp).then_inc(s_ex, 1)

            def silu_and_hT(Q, i):
                act.wait_ge(Q["g"], i + 1)
                wait(act, Q["h"], i)
                nc.scalar.activation(sg[:, :], pG[:, :], ACT.Silu).then_inc(Q["sg"], 1)
                act.wait_ge(Q["ht"], i + 1)
                nc.scalar.activation(hT[:, :], pH[:, :], ACT.Copy).then_inc(Q["hT"], 1)

            def shared_copy(i, q):
                wait(act, S["xt"], i - 1)
                nc.scalar.activation(xs[:, q, 0:D], rows[:, bass.ds(i, 1), 0:D].rearrange("p a d -> p (a d)"), ACT.Copy).then_inc(S["xs"], 1)

            def shared(i, q):
                if not isinstance(i, int) or i + 1 < TT:
                    shared_copy(i + 1, 1 - q)
                silu_and_hT(S, i)
            act.wait_ge(s_row, GROUPS)
            shared_copy(0, 0)
            over_tiles(act, TT, shared)
            over_tiles(act, SLOT_TILES, lambda i, q: silu_and_hT(R, i))

        @block.tensor
        def _(pe):
            pe.wait_ge(s_const, 16)
            pe.wait_ge(s_bias, 32)

            def group(g, q):
                pe.wait_ge(s_norm, RG * (g + 1))
                wait(pe, s_xTr, g)
                for c in range(DC):
                    for t in range(RG):
                        last = nc.tensor.transpose(pX[:, (c * RG + t) * P:(c * RG + t + 1) * P],
                                                   xnb[:, q, t, c * P:(c + 1) * P], ident)
                last.then_inc(s_tr, 1)
                pe.wait_ge(s_xTr, g + 1)
                wait(pe, s_L, g)
                for t in range(RG):
                    for c in range(DC):
                        last = nc.tensor.matmul(pL[:, t * E:(t + 1) * E], xTr[:, c, t * P:(t + 1) * P],
                                                router[:, c, :], start=(c == 0), stop=(c == DC - 1))
                last.then_inc(s_lg, 1)
            over_tiles(pe, GROUPS, group)

            def prefix():
                pe.wait_ge(s_oh, 1)
                chosen = scratch[:, :, :].rearrange("p t e -> p (t e)")
                nc.tensor.matmul(pL[:, 0:TT * E], const[:, C_TRI:C_TRI + P], chosen, start=True, stop=True)
                nc.tensor.matmul(pY[:, 0:TT * E], ones, chosen, start=True, stop=True).then_inc(s_prefix, 1)
            prefix()

            Wf = W[:, :, :].rearrange("p e n -> p (e n)")

            def expert(e, at, n):
                return Wf[:, bass.ds(e * EXPERT + at, n)]

            def turn_x(Q, q, ready, free):
                for s, v in ready:
                    pe.wait_ge(s, v)
                for s, v in free:
                    wait(pe, s, v)
                for c in range(DC):
                    last = nc.tensor.transpose(pX[:, c * P:(c + 1) * P], xs[:, q, c * P:(c + 1) * P], ident)
                last.then_inc(Q["xt"], 1)

            def up(Q, i, e):
                pe.wait_ge(Q["xT"], i + 1)
                wait(pe, Q["h"], i)
                for bank, at, s in ((pG, 0, "g"), (pU, UP, "u")):
                    for c in range(DC):
                        last = nc.tensor.matmul(bank[:, :], xT[:, c * P:(c + 1) * P], expert(e, at + c * H, H),
                                                start=(c == 0), stop=(c == DC - 1))
                    last.then_inc(Q[s], 1)

            def down(Q, i, e):
                pe.wait_ge(Q["hT"], i + 1)
                wait(pe, Q["ys"], i)
                for k in range(HC):
                    last = nc.tensor.matmul(pY[:, 0:D], hT[:, k * P:(k + 1) * P], expert(e, 2 * UP + k * D, D),
                                            start=(k == 0), stop=(k == HC - 1))
                last.then_inc(Q["y"], 1)

            def turn_h(Q, i):
                pe.wait_ge(Q["h"], i + 1)
                wait(pe, Q["hT"], i)
                for k in range(HC):
                    last = nc.tensor.transpose(pH[:, k * P:(k + 1) * P], hs[:, k * P:(k + 1) * P], ident)
                last.then_inc(Q["ht"], 1)

            pe.wait_ge(s_w[SHARED], 16)
            turn_x(S, 0, [(S["xs"], 1)], [])

            def shared(i, q):
                up(S, i, SHARED)
                if not isinstance(i, int) or i + 1 < TT:
                    turn_x(S, 1 - q, [(S["xs"], i + 2)], [(S["xT"], i + 1)])
                if not isinstance(i, int) or i > 0:
                    down(S, i - 1, SHARED)
                else:
                    pe.wait_ge(s_pos, 1)
                turn_h(S, i)
            over_tiles(pe, TT, shared)
            down(S, TT - 1, SHARED)

            for e in range(E):
                pe.wait_ge(s_w[e], 16)
            pe.wait_ge(s_map, 1)
            turn_x(R, 0, [(R["load"][0], 16)], [(S["xT"], TT)])

            def routed(i, q):
                e = pe.value_load(tile_expert[0:1, bass.ds(i, 1)], min_val=0, max_val=E - 1)
                if isinstance(i, int) and i == 0:
                    pe.wait_ge(S["ys"], TT)
                up(R, i, e)
                if not isinstance(i, int) or i + 1 < SLOT_TILES:
                    n = (i + 1 - (1 - q)) * 8 + 16
                    turn_x(R, 1 - q, [(R["load"][1 - q], n)], [(R["xT"], i + 1)])
                if not isinstance(i, int) or i > 0:
                    before = pe.value_load(tile_expert[0:1, bass.ds(i - 1, 1)], min_val=0, max_val=E - 1)
                    down(R, i - 1, before)
                turn_h(R, i)
            over_tiles(pe, SLOT_TILES, routed)
            down(R, SLOT_TILES - 1, pe.value_load(tile_expert[0:1, SLOT_TILES - 1:SLOT_TILES], min_val=0, max_val=E - 1))

        @block.vector
        def _(dve):
            def logits(g):
                dve.wait_ge(s_lg, g + 1)
                nc.vector.tensor_tensor(L[:, bass.ds(g * RG, RG), :], pL[:, 0:RG * E].rearrange("p (t e) -> p t e", e=E),
                                        bias[:, :].unsqueeze(1).broadcast_to([P, RG, E]), ALU.add).then_inc(s_L, 1)

            def statistics(g, q):
                dve.wait_ge(s_xin[q], (g - q) * 8 + 16)
                for t in range(RG):
                    nc.vector.bn_stats(stats[:, q, t, :], xin[:, q, t, :]).then_inc(s_bns, 1)

            def variance(g, q):
                for t in range(RG):
                    nc.vector.bn_aggr(mv[:, q, t, :], stats[:, q, t, :]).then_inc(s_bna, 1)
                dve.wait_ge(s_bna, RG * (g + 1))
                nc.vector.tensor_scalar(ve[:, q, :], mv[:, q, :, 1], LN_EPS, None, ALU.add).then_inc(s_ve, 1)

            def group(g, q):
                more = not isinstance(g, int) or g + 1 < GROUPS
                if more:
                    statistics(g + 1, 1 - q)
                    dve.wait_ge(s_bns, RG * (g + 2))
                    wait(dve, s_norm, RG * g)
                dve.wait_ge(s_rs, g + 1)
                wait(dve, s_row, g - 1)
                for t in range(RG):
                    nc.vector.tensor_scalar(xnb[:, q, t, :], xin[:, q, t, :], mv[:, q, t, 0:1], rstd[:, q, t:t + 1],
                                            ALU.subtract, ALU.mult).then_inc(s_norm, 1)
                if more:
                    variance(g + 1, 1 - q)
                if not isinstance(g, int) or g > 0:
                    logits(g - 1)
            dve.wait_ge(s_bias, 32)
            statistics(0, 0)
            dve.wait_ge(s_bns, RG)
            variance(0, 0)
            over_tiles(dve, GROUPS, group)
            logits(GROUPS - 1)
            dve.wait_ge(s_const, 16)

            chained = [0]

            def link(ins):
                chained[0] += 1
                ins.then_inc(s_chain, 1)
                dve.wait_ge(s_chain, chained[0])

            dve.wait_ge(s_L, GROUPS)
            v = nc.vector

            def per_tile(a):
                return a.unsqueeze(2).broadcast_to([P, TT, E])

            def per_expert(a):
                return a.unsqueeze(1).broadcast_to([P, TT, E])
            rank = per_expert(const[:, C_RANK:C_RANK + E])

            def first_of_max(m, onehot):
                link(v.tensor_reduce(m[:, :], L[:, :, :], X, ALU.max))
                link(v.tensor_tensor(scratch[:, :, :], L[:, :, :], per_tile(m[:, :]), ALU.is_equal))
                link(v.tensor_tensor(scratch[:, :, :], scratch[:, :, :], rank, ALU.mult))
                link(v.tensor_reduce(r1[:, :], scratch[:, :, :], X, ALU.max))
                link(v.tensor_tensor(onehot[:, :, :], scratch[:, :, :], per_tile(r1[:, :]), ALU.is_equal))
            first_of_max(m1, oh1)
            link(v.scalar_tensor_tensor(L[:, :, :], oh1[:, :, :], -3e38, L[:, :, :], op0=ALU.mult, op1=ALU.add))
            first_of_max(m2, oh2)
            v.tensor_tensor(scratch[:, :, :], oh1[:, :, :], oh2[:, :, :], ALU.add).then_inc(s_oh, 1)
            v.tensor_tensor(r1[:, :], m2[:, :], m1[:, :], ALU.subtract).then_inc(s_diff, 1)

            dve.wait_ge(s_prefix, 1)
            total = pY[:, 0:TT * E].rearrange("p (t e) -> p t e", e=E)
            within = pL[:, 0:TT * E].rearrange("p (t e) -> p t e", e=E)
            for e in range(E):
                last = v.tensor_tensor_scan(incl[:, :, e], ones[:, 0:TT], total[:, :, e], initial=0.0, op0=ALU.mult, op1=ALU.add)
                if e < E - 1:
                    last.then_inc(s_chain, 1)
                    chained[0] += 1
            link(last)
            count = incl[:, TT - 1, :]
            link(v.tensor_tensor(cmp[:, :, :], count.unsqueeze(2).broadcast_to([P, E, TT]),
                                 const[:, C_START:C_START + TT].unsqueeze(1).broadcast_to([P, E, TT]), ALU.is_gt))
            link(v.tensor_reduce(tiles[:, :], cmp[:, :, :], X, ALU.add))
            link(v.tensor_tensor_scan(tend[:, :], ones[:, 0:E], tiles[:, :], initial=0.0, op0=ALU.mult, op1=ALU.add))
            link(v.tensor_tensor(base[:, :], tend[:, :], tiles[:, :], ALU.subtract))
            link(v.tensor_tensor(incl[:, :, :], incl[:, :, :], total, ALU.subtract))
            link(v.tensor_tensor(incl[:, :, :], incl[:, :, :], within, ALU.add))
            link(v.scalar_tensor_tensor(incl[:, :, :], per_expert(base[:, :]), float(P), incl[:, :, :], op0=ALU.mult, op1=ALU.add))
            for k, onehot in enumerate((oh1, oh2)):
                link(v.tensor_tensor(onehot[:, :, :], onehot[:, :, :], incl[:, :, :], ALU.mult))
                link(v.tensor_reduce(posf[:, k, :], onehot[:, :, :], X, ALU.add))
            link(v.tensor_copy(pos[:, :, :], posf[:, :, :]))
            dve.wait_ge(s_ex, 1)
            link(v.tensor_scalar(m1[:, :], ex[:, :], 1.0, None, ALU.add))
            link(v.reciprocal(m2[:, :], m1[:, :]))
            link(v.tensor_scalar(w0[:, :], m2[:, :], 0.5, None, ALU.mult))
            v.tensor_tensor(w1[:, :], w0[:, :], ex[:, :], ALU.mult).then_inc(s_pos, 1)
            link(v.tensor_tensor(tile_cmp[:, :, :], tend[0:1, :].unsqueeze(1).broadcast_to([1, SLOT_TILES, E]),
                                 const[0:1, C_TILE:C_TILE + SLOT_TILES].unsqueeze(2).broadcast_to([1, SLOT_TILES, E]), ALU.is_le))
            link(v.tensor_reduce(tile_sum[:, :], tile_cmp[:, :, :], X, ALU.add))
            v.tensor_scalar(tile_expert[:, :], tile_sum[:, :], float(E - 1), None, ALU.min).then_inc(s_map, 1)

            def take_x(Q, i):
                dve.wait_ge(Q["xt"], i + 1)
                nc.vector.tensor_copy(xT[:, :], pX[:, 0:DC * P]).then_inc(Q["xT"], 1)

            def gate(Q, i):
                dve.wait_ge(Q["sg"], i + 1)
                dve.wait_ge(Q["u"], i + 1)
                nc.vector.tensor_tensor(hs[:, :], sg[:, :], pU[:, :], ALU.mult).then_inc(Q["h"], 1)

            def shared_sum(i, q):
                dve.wait_ge(S["y"], i + 1)
                dve.wait_ge(S["load"][q], (i - q) * 8 + 16)
                wait(dve, S["store"][q], (i - q) * 8)
                nc.vector.scalar_tensor_tensor(ys[:, q, :], pY[:, 0:D], 0.5, xres[:, q, :],
                                               op0=ALU.mult, op1=ALU.add).then_inc(S["ys"], 1)

            take_x(S, 0)

            def shared(i, q):
                gate(S, i)
                if not isinstance(i, int) or i + 1 < TT:
                    take_x(S, i + 1)
                if not isinstance(i, int) or i > 0:
                    shared_sum(i - 1, 1 - q)
            over_tiles(dve, TT, shared)
            shared_sum(TT - 1, (TT - 1) % 2)

            def take_row_ends(i, q):
                dve.wait_ge(R["load"][q], (i - q) * 8 + 16)
                wait(dve, s_add, (i - 1) * 16)
                nc.vector.tensor_copy(ids[:, q, :], xs[:, q, ID:ID + 1]).then_inc(R["xsf"], 1)
                nc.vector.tensor_copy(wt[:, q, :], xs[:, q, WEIGHT:WEIGHT + 1]).then_inc(R["used"], 1)

            def weigh(i, q):
                dve.wait_ge(R["y"], i + 1)
                dve.wait_ge(R["used"], i + 1)
                wait(dve, s_add, (i - 1) * 16)
                nc.vector.tensor_scalar(ys[:, q, :], pY[:, 0:D], wt[:, q, :], None, ALU.mult).then_inc(R["ys"], 1)

            for q in range(2):
                dve.wait_ge(S["store"][q], 16 * TT // 2)
            take_x(R, 0)

            def routed(i, q):
                gate(R, i)
                if not isinstance(i, int) or i + 1 < SLOT_TILES:
                    take_x(R, i + 1)
                take_row_ends(i, q)
                if not isinstance(i, int) or i > 0:
                    weigh(i - 1, 1 - q)
            over_tiles(dve, SLOT_TILES, routed)
            weigh(SLOT_TILES - 1, (SLOT_TILES - 1) % 2)


DI = 512
EB = DI // P
N = 16
F = 704
FB = -(-F // P)
CH = 512
CT = CH // P
CHUNKS = T // CH
UNITS = N * EB
F_LAST = F - (FB - 1) * P

MAMBA_WEIGHTS = {
    "in_w": [P, DC, DI], "gate_w": [P, DC, DI], "dt_w": [P, EB, DI], "bc_w": [P, EB, 2 * N],
    "out_w": [P, EB, D], "norm1": [P, DC], "norm2": [P, DC], "dt_b": [P, EB], "A_log": [P, EB * N], "Dp": [P, EB],
}
FFN_WEIGHTS = {"fg_w": [P, DC, F], "fu_w": [P, DC, F], "fd_w": [P, FB - 1, D], "fd_last": [F_LAST, D]}


def mamba(nc, src, dst, w, ffn, const, s_weights):
    ident = const[:, C_IDENT:C_IDENT + P]
    ones = const[:, C_ONES:C_ONES + P]
    src_c = src[0:T, :].rearrange("(c t p) d -> c p t d", t=CT, p=P)
    dst_c = dst[0:T, :].rearrange("(c t p) d -> c p t d", t=CT, p=P)

    with phase(nc) as new, ExitStack() as ctx:
        def sb(name, shape, dt=F32):
            return ctx.enter_context(nc.sbuf_tensor(f"b_{name}", shape, dt))

        def pb(name):
            return ctx.enter_context(nc.psum_tensor(f"b_{name}", [P, 512], F32))

        def sem(name):
            return new(f"b_{name}")

        w = dict(w, **{name: sb(name, shape) for name, shape in FFN_WEIGHTS.items()})
        xf = sb("xf", [P, CT, D])
        xb = sb("xb", [P, CT, D])
        yln = sb("yln", [P, 2, CT, D])
        hrow = sb("hrow", [P, CT, D])
        hT = sb("hT", [P, DC, CH])
        z = sb("z", [P, 2, EB, CH])
        dt = sb("dt", [P, 2, EB, CH])
        dtzT = sb("dtzT", [P, 2, CT, DI])
        BC = sb("BC", [P, 2, CT, 2 * N])
        acc = sb("acc", [P, CT, DI])
        xa = sb("xa", [P, CT, D])
        hnT = sb("hnT", [P, DC, CH])
        ff = sb("ff", [P, FB, CH])
        sB = sb("sB", [P, 2, CT, DI])
        dA = sb("dA", [P, 4, CH])
        h = sb("h", [P, 3, EB, CH])
        eF = sb("eF", [P, CH])
        eB = sb("eB", [P, CH])
        ea = sb("ea", [P, CH])
        el = sb("el", [P, CH])
        dtz = sb("dtz", [P, CH])
        state = sb("state", [P, UNITS])
        negA = sb("negA", [P, EB * N])
        stats = sb("stats", [P, CT, 6])
        mv = sb("mv", [P, CT, 2])
        ve = sb("ve", [P, CT])
        rstd = sb("rstd", [P, CT])
        sq = sb("sq", [P, 2, D])
        ssq = sb("ssq", [P, 2, CT])
        ms = sb("ms", [P, 2, CT])
        rr = sb("rr", [P, 2, CT])
        nhalf = sb("nhalf", [P, CT])

        pB = [pb(f"pB{i}") for i in range(2)]
        pH = [pb(f"pH{i}") for i in range(2)]
        pF = [pb(f"pF{i}") for i in range(2)]
        pK = [pb(f"pK{i}") for i in range(2)]
        F_USES = (2 + 2 * EB, 1 + 2 * EB)
        K_USES = 5 + FB

        s_ffn = sem("ffn")
        s_fld = sem("fld")
        s_bld = sem("bld")
        s_stored = sem("stored")
        s_init = sem("init")
        s_neg = sem("neg")
        s_bns = sem("bns")
        s_bna = sem("bna")
        s_ve = sem("ve")
        s_rstd = sem("rstd")
        s_y = sem("y")
        s_sq = [sem(f"sq{i}") for i in range(2)]
        s_ms = [sem(f"ms{i}") for i in range(2)]
        s_rr = [sem(f"rr{i}") for i in range(2)]
        s_hrow = sem("hrow")
        s_hT = sem("hT")
        s_eF = sem("eF")
        s_lnF = sem("lnF")
        s_sigF = sem("sigF")
        s_z = sem("z")
        s_BC = sem("BC")
        s_relu = sem("relu")
        s_ea0 = sem("ea0")
        s_ea = sem("ea")
        s_el = sem("el")
        s_p1 = sem("p1")
        s_p2 = sem("p2")
        s_p3 = sem("p3")
        s_dt = sem("dt")
        s_dtz = sem("dtz")
        s_dtzT = sem("dtzT")
        s_fullF = [sem(f"fullF{i}") for i in range(2)]
        s_fullK = [sem(f"fullK{i}") for i in range(2)]
        s_ssm = sem("ssm")
        s_xa = sem("xa")
        s_base = sem("base")
        s_hn = sem("hn")
        s_hnT = sem("hnT")
        s_eB = sem("eB")
        s_lnB = sem("lnB")
        s_sigB = sem("sigB")
        s_gu = sem("gu")
        s_ff = sem("ff")
        s_x2 = sem("x2")
        s_sB = sem("sB")
        s_dA = sem("dA")
        s_dB = sem("dB")
        s_scan = sem("scan")
        s_state = sem("state")
        s_ht = sem("ht")
        s_acc = sem("acc")

        block = ctx.enter_context(nc.Block())
        LAST = UNITS + 6

        def chunks(slots):
            def run(eng):
                slots(0, 0, True, False)
                with eng.Fori(0, CHUNKS // 2 - 1) as j:
                    slots(j * 2 + 1, 1, True, True)
                    slots(j * 2 + 2, 0, True, True)
                slots(CHUNKS - 1, 1, False, True)
            return run

        @block.sync
        def _(sp):
            def load(dst_rows, c, s):
                sp.dma_start(dst_rows, src_c[bass.ds(c, 1)].rearrange("a p t d -> p (a t) d")).then_inc(s, 16)

            def step(c):
                sp.wait_ge(s_y, CT * (c + 1))
                load(xf[:, :, :], c + 1, s_fld)
                sp.wait_ge(s_x2, 2 * c)
                sp.dma_start(dst_c[bass.ds(c - 1, 1)].rearrange("a p t d -> p (a t) d"), xb[:, :, :]).then_inc(s_stored, 16)
                sp.wait_ge(s_stored, 16 * c)
                load(xb[:, :, :], c, s_bld)
            load(xf[:, :, :], 0, s_fld)
            load(xb[:, :, :], 0, s_bld)
            for name in FFN_WEIGHTS:
                sp.dma_start(w[name][:], ffn[name]).then_inc(s_ffn, 16)
            sp.wait_ge(s_y, CT)
            load(xf[:, :, :], 1, s_fld)
            with sp.Fori(1, CHUNKS - 1) as c:
                step(c)
            for c in (CHUNKS - 1, CHUNKS):
                sp.wait_ge(s_x2, 2 * c)
                sp.dma_start(dst_c[c - 1], xb[:, :, :]).then_inc(s_stored, 16)
                sp.wait_ge(s_stored, 16 * c)
                if c < CHUNKS:
                    load(xb[:, :, :], c, s_bld)

        @block.gpsimd
        def _(pool):
            g = nc.gpsimd
            zero = const[:, C_FILL:C_FILL + 1]
            g.memset(nhalf[:, :], -0.5).then_inc(s_init, 1)
            g.memset(state[:, :], 0.0).then_inc(s_init, 1)
            pool.wait_ge(s_init, 2)

            def rms(side, c):
                pool.wait_ge(s_ms[side], c + 1)
                g.tensor_tensor(rr[:, side, :], ms[:, side, :], nhalf[:, :], ALU.pow).then_inc(s_rr[side], 1)

            def front(u, c, q):
                if u == 4:
                    pool.wait_ge(s_ve, c + 1)
                    g.tensor_tensor(rstd[:, :], ve[:, :], nhalf[:, :], ALU.pow).then_inc(s_rstd, 1)
                if u == 16:
                    rms(0, c)
                for b in range(EB):
                    if u == 43 + 4 * b:
                        n = c * EB + b + 1
                        pool.wait_ge(s_el, n)
                        wait(pool, s_fullF[0], (c * F_USES[0] + 5 + b + 1) if b else (c * F_USES[0]))
                        g.tensor_tensor(dt[:, q, b, :], dt[:, q, b, :], el[:, :], ALU.add).then_inc(s_p1, 1)
                        g.tensor_scalar(dtz[:, :], ea[:, :], 1.0, -1.0, ALU.add, ALU.add).then_inc(s_p2, 1)
                        pool.wait_ge(s_p2, n)
                        g.tensor_tensor(dtz[:, :], ea[:, :], dtz[:, :], ALU.subtract).then_inc(s_p3, 1)
                        pool.wait_ge(s_p3, n)
                        g.tensor_tensor(dt[:, q, b, :], dt[:, q, b, :], dtz[:, :], ALU.add).then_inc(s_dt, 1)
                        pool.wait_ge(s_dt, n)
                        pool.wait_ge(s_z, n)
                        g.tensor_tensor(dtz[:, :], dt[:, q, b, :], z[:, q, b, :], ALU.mult).then_inc(s_dtz, 1)

            def back(u, c, q):
                if u == 14:
                    pool.wait_ge(s_xa, 2 * (c + 1))
                    pool.wait_ge(s_bld, 16 * (c + 1))
                    g.tensor_tensor(xb[:, :, :], xb[:, :, :], xa[:, :, :], ALU.add).then_inc(s_base, 1)
                if u == 17:
                    rms(1, c)

            def slots(c, q, has_front, has_back):
                for u in range(LAST):
                    if u < UNITS:
                        n, k = u // EB, u % EB
                        pool.wait_ge(s_scan, c * UNITS + u + 1)
                        g.tensor_tensor(state[:, u:u + 1], h[:, n % 3, k, CH - 1:CH], zero, ALU.add).then_inc(s_state, 1)
                    if has_front:
                        front(u, c + 1, 1 - q)
                    if has_back:
                        back(u, c - 1, 1 - q)
            for u in range(LAST):
                front(u, 0, 0)
            chunks(slots)(pool)
            for u in range(LAST):
                back(u, CHUNKS - 1, 1)

        @block.scalar
        def _(act):
            a = nc.scalar
            act.preload_act_table_set("natural_log_exp_and_others")
            act.wait_ge(s_weights, 16 * len(MAMBA_WEIGHTS))
            a.activation(negA[:, :], w["A_log"][:, :], ACT.Exp).then_inc(s_neg, 1)
            act.wait_ge(s_neg, 1)
            a.activation(negA[:, :], negA[:, :], ACT.Copy, scale=-1.0).then_inc(s_neg, 1)
            act.wait_ge(s_neg, 2)

            def squares(side, rows, c):
                wait(act, s_ms[side], c)
                for t in range(CT):
                    wait(act, s_sq[side], c * CT + t)
                    a.activation(sq[:, side, :], rows(t), ACT.Square, accum_out=ssq[:, side, t:t + 1]).then_inc(s_sq[side], 1)

            def front(u, c, q):
                if u == 13:
                    act.wait_ge(s_y, CT * (c + 1))
                    squares(0, lambda t: yln[:, q, t, :], c)
                if u == 20:
                    for d in range(DC):
                        act.wait_ge(s_fullF[d], c * F_USES[d] + 1)
                        wait(act, s_fullF[1], c * F_USES[1])
                        a.activation(hT[:, d, :], pF[d][:, :], ACT.Copy, scale=w["norm1"][:, d:d + 1]).then_inc(s_hT, 1)
                for b in range(EB):
                    n = c * EB + b
                    if u == 23 + 4 * b:
                        act.wait_ge(s_fullF[1], c * F_USES[1] + 2 + b)
                        wait(act, s_z, n)
                        a.activation(eF[:, :], pF[1][:, :], ACT.Exp, scale=-1.0).then_inc(s_eF, 1)
                    if u == 24 + 4 * b:
                        act.wait_ge(s_eF, n + 1)
                        a.activation(eF[:, :], eF[:, :], ACT.Ln, bias=1.0).then_inc(s_lnF, 1)
                    if u == 25 + 4 * b:
                        act.wait_ge(s_lnF, n + 1)
                        a.activation(eF[:, :], eF[:, :], ACT.Exp, scale=-1.0).then_inc(s_sigF, 1)
                    if u == 42 + 4 * b:
                        act.wait_ge(s_fullF[1], c * F_USES[1] + 2 + EB + b)
                        wait(act, s_dt, n)
                        a.activation(dt[:, q, b, :], pF[1][:, :], ACT.Relu, bias=w["dt_b"][:, b:b + 1]).then_inc(s_relu, 1)
                        a.activation(ea[:, :], pF[1][:, :], ACT.Abs, bias=w["dt_b"][:, b:b + 1]).then_inc(s_ea0, 1)
                        act.wait_ge(s_ea0, n + 1)
                        a.activation(ea[:, :], ea[:, :], ACT.Exp, scale=-1.0).then_inc(s_ea, 1)
                        act.wait_ge(s_ea, n + 1)
                        a.activation(el[:, :], ea[:, :], ACT.Ln, bias=1.0).then_inc(s_el, 1)
                    if u == 48 + 4 * b:
                        act.wait_ge(s_fullF[0], c * F_USES[0] + 7 + b)
                        a.activation(dtzT[:, q, :, b * P:(b + 1) * P], pF[0][:, :].rearrange("p (t d) -> p t d", t=CT),
                                     ACT.Copy).then_inc(s_dtzT, 1)

            def back(u, c, q):
                if u == 14:
                    act.wait_ge(s_xa, 2 * (c + 1))
                    squares(1, lambda t: xa[:, t, :], c)
                if u == 22:
                    for d in range(DC):
                        act.wait_ge(s_fullK[d], c * K_USES + 4)
                        a.activation(hnT[:, d, :], pK[d][:, :], ACT.Copy, scale=w["norm2"][:, d:d + 1]).then_inc(s_hnT, 1)
                for b in range(FB):
                    m = P if b < FB - 1 else F_LAST
                    if u == 25 + 4 * b:
                        act.wait_ge(s_fullK[0], c * K_USES + 5 + b)
                        wait(act, s_gu, c * FB + b)
                        a.activation(eB[0:m, :], pK[0][0:m, :], ACT.Exp, scale=-1.0).then_inc(s_eB, 1)
                    if u == 26 + 4 * b:
                        act.wait_ge(s_eB, c * FB + b + 1)
                        a.activation(eB[0:m, :], eB[0:m, :], ACT.Ln, bias=1.0).then_inc(s_lnB, 1)
                    if u == 27 + 4 * b:
                        act.wait_ge(s_lnB, c * FB + b + 1)
                        a.activation(eB[0:m, :], eB[0:m, :], ACT.Exp, scale=-1.0).then_inc(s_sigB, 1)

            def scale_B(i, c, q):
                n, t = i // CT, i % CT
                wait(act, s_dB, c * UNITS + (n - 1) * EB if n >= 2 else c * UNITS)
                a.activation(sB[:, n % 2, t, :], dtzT[:, q, t, :], ACT.Copy, scale=BC[:, q, t, n:n + 1]).then_inc(s_sB, 1)

            def decay(u, c, q):
                n, k = u // EB, u % EB
                wait(act, s_scan, c * UNITS + u - 3 if u > 3 else c * UNITS)
                a.activation(dA[:, u % 4, :], dt[:, q, k, :], ACT.Exp, scale=negA[:, k * N + n:k * N + n + 1]).then_inc(s_dA, 1)

            def slots(c, q, has_front, has_back):
                act.wait_ge(s_dt, EB * (c + 1))
                act.wait_ge(s_dtzT, EB * (c + 1))
                act.wait_ge(s_BC, c + 1)
                for i in range(6):
                    scale_B(i, c, q)
                decay(0, c, q)
                decay(1, c, q)
                for u in range(LAST):
                    if u + 6 < UNITS:
                        scale_B(u + 6, c, q)
                    if u + 2 < UNITS:
                        decay(u + 2, c, q)
                    if has_front:
                        front(u, c + 1, 1 - q)
                    if has_back:
                        back(u, c - 1, 1 - q)
            for u in range(LAST):
                front(u, 0, 0)
            chunks(slots)(act)
            for u in range(LAST):
                back(u, CHUNKS - 1, 1)

        @block.tensor
        def _(pe):
            t_ = nc.tensor

            def turn(bank, parts):
                for i, part in enumerate(parts):
                    last = t_.transpose(bank[:, i * P:(i + 1) * P], part, ident)
                return last

            def front(u, c, q):
                if u == 19:
                    pe.wait_ge(s_hrow, CT * (c + 1))
                    for d in range(DC):
                        wait(pe, (s_dtzT, s_ea0)[d], EB * c)
                        turn(pF[d], [hrow[:, t, d * P:(d + 1) * P] for t in range(CT)]).then_inc(s_fullF[d], 1)
                for b in range(EB):
                    if u == 22 + 4 * b:
                        pe.wait_ge(s_hT, DC * (c + 1))
                        for bank, name in ((0, "in_w"), (1, "gate_w")):
                            wait(pe, (s_z, s_eF)[bank], c * EB + b)
                            for d in range(DC):
                                last = t_.matmul(pF[bank][:, :], w[name][:, d, b * P:(b + 1) * P], hT[:, d, :],
                                                 start=(d == 0), stop=(d == DC - 1))
                            last.then_inc(s_fullF[bank], 1)
                    if u == 40 + 4 * b:
                        pe.wait_ge(s_eF, EB * (c + 1))
                        wait(pe, s_ea0, c * EB + b)
                        for d in range(EB):
                            last = t_.matmul(pF[1][:, :], w["dt_w"][:, d, b * P:(b + 1) * P], z[:, q, d, :],
                                             start=(d == 0), stop=(d == EB - 1))
                        last.then_inc(s_fullF[1], 1)
                    if u == 47 + 4 * b:
                        pe.wait_ge(s_dtz, c * EB + b + 1)
                        pe.wait_ge(s_BC, c + 1)
                        wait(pe, s_dtzT, c * EB + b)
                        turn(pF[0], [dtz[:, t * P:(t + 1) * P] for t in range(CT)]).then_inc(s_fullF[0], 1)
                if u == 39:
                    pe.wait_ge(s_z, EB * (c + 1))
                    for t in range(CT):
                        for d in range(EB):
                            last = t_.matmul(pF[0][:, t * 2 * N:(t + 1) * 2 * N], z[:, q, d, t * P:(t + 1) * P],
                                             w["bc_w"][:, d, :], start=(d == 0), stop=(d == EB - 1))
                    last.then_inc(s_fullF[0], 1)

            def back(u, c, q):
                for b in range(EB):
                    if u == b:
                        pe.wait_ge(s_acc, UNITS * (c + 1))
                        wait(pe, s_x2, 2 * c)
                        wait(pe, s_ssm, c * EB + max(b - 1, 0))
                        turn(pK[b % 2], [acc[:, t, b * P:(b + 1) * P] for t in range(CT)]).then_inc(s_fullK[b % 2], 1)
                for i in range(2):
                    if u == 6 + i:
                        pe.wait_ge(s_ssm, EB * (c + 1))
                        for t in range(2 * i, 2 * i + 2):
                            for d in range(EB):
                                last = t_.matmul(pK[i][:, (t % 2) * D:(t % 2 + 1) * D], z[:, q, d, t * P:(t + 1) * P],
                                                 w["out_w"][:, d, :], start=(d == 0), stop=(d == EB - 1))
                        last.then_inc(s_fullK[i], 1)
                    if u == 50 + 4 * i:
                        pe.wait_ge(s_ff, FB * (c + 1))
                        for t in range(2 * i, 2 * i + 2):
                            for b in range(FB):
                                m = P if b < FB - 1 else F_LAST
                                rhs = w["fd_w"][:, b, :] if b < FB - 1 else w["fd_last"][:, :]
                                last = t_.matmul(pK[i][:, (t % 2) * D:(t % 2 + 1) * D], ff[0:m, b, t * P:(t + 1) * P],
                                                 rhs, start=(b == 0), stop=(b == FB - 1))
                        last.then_inc(s_fullK[i], 1)
                if u == 21:
                    pe.wait_ge(s_hn, CT * (c + 1))
                    for d in range(DC):
                        turn(pK[d], [xa[:, t, d * P:(d + 1) * P] for t in range(CT)]).then_inc(s_fullK[d], 1)
                for b in range(FB):
                    if u == 24 + 4 * b:
                        m = P if b < FB - 1 else F_LAST
                        pe.wait_ge(s_hnT, DC * (c + 1))
                        for bank, name in ((0, "fg_w"), (1, "fu_w")):
                            wait(pe, (s_gu, s_ff)[bank], c * FB + b)
                            for d in range(DC):
                                last = t_.matmul(pK[bank][0:m, :], w[name][:, d, b * P:b * P + m], hnT[:, d, :],
                                                 start=(d == 0), stop=(d == DC - 1))
                            last.then_inc(s_fullK[bank], 1)

            def input_of_scan(u, c):
                n, k = u // EB, u % EB
                pe.wait_ge(s_sB, c * UNITS + (n + 1) * CT)
                wait(pe, s_scan, c * UNITS + u - 1 if u > 1 else c * UNITS)
                turn(pB[u % 2], [sB[:, n % 2, t, k * P:(k + 1) * P] for t in range(CT)]).then_inc(s_dB, 1)

            def states(v, c):
                n, t = v // CT, v % CT
                pe.wait_ge(s_scan, c * UNITS + (n + 1) * EB)
                wait(pe, s_acc, c * UNITS + v - 1 if v > 1 else c * UNITS)
                turn(pH[v % 2], [h[:, n % 3, k, t * P:(t + 1) * P] for k in range(EB)]).then_inc(s_ht, 1)

            def slots(c, q, has_front, has_back):
                input_of_scan(0, c)
                for u in range(LAST):
                    if u + 1 < UNITS:
                        input_of_scan(u + 1, c)
                    if has_front:
                        front(u, c + 1, 1 - q)
                    if has_back:
                        back(u, c - 1, 1 - q)
                    if 0 <= u - 5 < UNITS:
                        states(u - 5, c)
            pe.wait_ge(s_weights, 16 * len(MAMBA_WEIGHTS))
            for u in range(LAST):
                front(u, 0, 0)
            pe.wait_ge(s_ffn, 16 * len(FFN_WEIGHTS))
            chunks(slots)(pe)
            for u in range(LAST):
                back(u, CHUNKS - 1, 1)

        @block.vector
        def _(dve):
            v_ = nc.vector
            dve.wait_ge(s_weights, 16 * len(MAMBA_WEIGHTS))
            dve.wait_ge(s_init, 2)

            def mean_square(side, c):
                dve.wait_ge(s_sq[side], CT * (c + 1))
                v_.tensor_scalar(ms[:, side, :], ssq[:, side, :], 1.0 / D, RMS_EPS, ALU.mult, ALU.add).then_inc(s_ms[side], 1)

            def front(u, c, q):
                if u == 2:
                    dve.wait_ge(s_fld, 16 * (c + 1))
                    for t in range(CT):
                        v_.bn_stats(stats[:, t, :], xf[:, t, :]).then_inc(s_bns, 1)
                if u == 3:
                    if isinstance(c, int):
                        dve.wait_ge(s_bns, CT * (c + 1))
                    for t in range(CT):
                        v_.bn_aggr(mv[:, t, :], stats[:, t, :]).then_inc(s_bna, 1)
                    dve.wait_ge(s_bna, CT * (c + 1))
                    v_.tensor_scalar(ve[:, :], mv[:, :, 1], LN_EPS, None, ALU.add).then_inc(s_ve, 1)
                if u == 11:
                    dve.wait_ge(s_rstd, c + 1)
                    for t in range(CT):
                        v_.tensor_scalar(yln[:, q, t, :], xf[:, t, :], mv[:, t, 0:1], rstd[:, t:t + 1],
                                         ALU.subtract, ALU.mult).then_inc(s_y, 1)
                if u == 15:
                    mean_square(0, c)
                if u == 18:
                    dve.wait_ge(s_rr[0], c + 1)
                    wait(dve, s_hT, DC * c)
                    for t in range(CT):
                        v_.tensor_scalar(hrow[:, t, :], yln[:, q, t, :], rr[:, 0, t:t + 1], None, ALU.mult).then_inc(s_hrow, 1)
                for b in range(EB):
                    if u == 26 + 4 * b:
                        dve.wait_ge(s_sigF, c * EB + b + 1)
                        dve.wait_ge(s_fullF[0], c * F_USES[0] + 2 + b)
                        v_.tensor_tensor(z[:, q, b, :], eF[:, :], pF[0][:, :], ALU.mult).then_inc(s_z, 1)
                if u == 41:
                    dve.wait_ge(s_fullF[0], c * F_USES[0] + 6)
                    v_.tensor_copy(BC[:, q, :, :], pF[0][:, 0:CT * 2 * N].rearrange("p (t n) -> p t n", t=CT)).then_inc(s_BC, 1)

            def back(u, c, q):
                for b in range(EB):
                    if u == b + 1:
                        dve.wait_ge(s_fullK[b % 2], c * K_USES + b // 2 + 1)
                        v_.scalar_tensor_tensor(z[:, q, b, :], z[:, q, b, :], w["Dp"][:, b:b + 1], pK[b % 2][:, :],
                                                op0=ALU.mult, op1=ALU.add).then_inc(s_ssm, 1)
                for i in range(2):
                    if u == 8 + i:
                        dve.wait_ge(s_fullK[i], c * K_USES + 3)
                        v_.tensor_tensor(xa[:, 2 * i:2 * i + 2, :], yln[:, q, 2 * i:2 * i + 2, :],
                                         pK[i][:, :].rearrange("p (t d) -> p t d", t=2), ALU.add).then_inc(s_xa, 1)
                    if u == 53 + 4 * i:
                        dve.wait_ge(s_fullK[i], c * K_USES + 5 + FB)
                        v_.tensor_tensor(xb[:, 2 * i:2 * i + 2, :], xb[:, 2 * i:2 * i + 2, :],
                                         pK[i][:, :].rearrange("p (t d) -> p t d", t=2), ALU.add).then_inc(s_x2, 1)
                if u == 16:
                    mean_square(1, c)
                if u == 20:
                    dve.wait_ge(s_rr[1], c + 1)
                    dve.wait_ge(s_base, c + 1)
                    for t in range(CT):
                        v_.tensor_scalar(xa[:, t, :], xa[:, t, :], rr[:, 1, t:t + 1], None, ALU.mult).then_inc(s_hn, 1)
                for b in range(FB):
                    if u == 28 + 4 * b:
                        m = P if b < FB - 1 else F_LAST
                        n = c * FB + b + 1
                        dve.wait_ge(s_sigB, n)
                        v_.tensor_tensor(ff[0:m, b, :], eB[0:m, :], pK[0][0:m, :], ALU.mult).then_inc(s_gu, 1)
                        dve.wait_ge(s_gu, n)
                        dve.wait_ge(s_fullK[1], c * K_USES + 5 + b)
                        v_.tensor_tensor(ff[0:m, b, :], ff[0:m, b, :], pK[1][0:m, :], ALU.mult).then_inc(s_ff, 1)

            def scan(u, c, q):
                n, k = u // EB, u % EB
                dve.wait_ge(s_dA, c * UNITS + u + 1)
                dve.wait_ge(s_dB, c * UNITS + u + 1)
                wait(dve, s_state, c * UNITS if u < 3 * EB else c * UNITS + u - 3 * EB + 1)
                wait(dve, s_ht, c * UNITS if n < 3 else c * UNITS + (n - 2) * CT)
                v_.tensor_tensor_scan(h[:, n % 3, k, :], dA[:, u % 4, :], pB[u % 2][:, :], initial=state[:, u:u + 1],
                                      op0=ALU.mult, op1=ALU.add).then_inc(s_scan, 1)

            def weigh(v, c, q):
                n, t = v // CT, v % CT
                dve.wait_ge(s_ht, c * UNITS + v + 1)
                C = BC[:, q, t, N + n:N + n + 1]
                if n == 0:
                    wait(dve, s_ssm, EB * c)
                    v_.tensor_scalar(acc[:, t, :], pH[v % 2][:, :], C, None, ALU.mult).then_inc(s_acc, 1)
                else:
                    dve.wait_ge(s_acc, c * UNITS + v - CT + 1)
                    v_.scalar_tensor_tensor(acc[:, t, :], pH[v % 2][:, :], C, acc[:, t, :],
                                            op0=ALU.mult, op1=ALU.add).then_inc(s_acc, 1)

            def slots(c, q, has_front, has_back):
                for u in range(LAST):
                    if has_front and u == 3:
                        dve.wait_ge(s_bns, CT * (c + 2))
                    if u < UNITS:
                        scan(u, c, q)
                    if has_back:
                        back(u, c - 1, 1 - q)
                    if 0 <= u - 6 < UNITS:
                        weigh(u - 6, c, q)
                    if has_front:
                        front(u, c + 1, 1 - q)
            for u in range(LAST):
                front(u, 0, 0)
            chunks(slots)(dve)
            for u in range(LAST):
                back(u, CHUNKS - 1, 1)


def macaron(nc, x, moe_w, router, bias, consts, *rest):
    out = rest[-1]
    mamba_w = dict(zip([*MAMBA_WEIGHTS, *FFN_WEIGHTS], rest))
    moe_weights = {"moe": moe_w, "router": router, "bias": bias}
    x1 = nc.dram_tensor("x1", (T + P, D), F32, kind="Internal").ap()
    x2 = nc.dram_tensor("x2", (T, D), F32, kind="Internal").ap()
    x3 = nc.dram_tensor("x3", (T + P, D), F32, kind="Internal").ap()
    slots_a = nc.dram_tensor("slots_a", (SLOTS, ROW), F32, kind="Internal").ap()
    slots_c = nc.dram_tensor("slots_c", (SLOTS, ROW), F32, kind="Internal").ap()
    with ExitStack() as ctx:
        const = ctx.enter_context(nc.sbuf_tensor("const", [P, CONSTS], F32))
        w = {n: ctx.enter_context(nc.sbuf_tensor(f"w_{n}", s, F32)) for n, s in MAMBA_WEIGHTS.items()}
        s_weights = ctx.enter_context(nc.semaphore("weights"))
        s_out = ctx.enter_context(nc.semaphore("out"))
        with nc.sbuf_tensor("Wa", [P, E + 1, EXPERT], F32) as W:
            moe(nc, "a", x, x1, slots_a, moe_weights, consts, const, W,
                [(w[n][:], mamba_w[n], s_weights) for n in MAMBA_WEIGHTS])
        mamba(nc, x1, x2, w, mamba_w, const, s_weights)
        with nc.sbuf_tensor("Wc", [P, E + 1, EXPERT], F32) as W:
            moe(nc, "c", x2, x3, slots_c, moe_weights, consts, const, W)
        with nc.Block() as block:
            @block.sync
            def _(sp):
                sp.dma_start(out, x3[0:T, :]).then_inc(s_out, 16)
                sp.wait_ge(s_out, 16)


def layout(z):
    def blocks(w):
        return np.ascontiguousarray(w.reshape(w.shape[0] // P, P, -1).transpose(1, 0, 2))

    def turned(name):
        return np.ascontiguousarray(z[name].T)

    def expert(w1, w3, w2):
        return np.concatenate([blocks(w).reshape(P, -1) for w in (w1, w3, w2)], axis=1)
    f, a = "L0_ffn_", "L0_attn_"
    experts = [expert(z[f + "w1"][e], z[f + "w3"][e], z[f + "w2"][e]) for e in range(E)]
    experts.append(expert(z[f + "sw1"][0], z[f + "sw3"][0], z[f + "sw2"][0]))
    down = turned(a + "ffn_down_w")
    whole = (FB - 1) * P
    return {
        "x": z[a + "x"].reshape(T, D),
        "moe": np.stack(experts),
        "router": blocks(turned(f + "router_w")),
        "bias": z[f + "experts_bias"],
        "consts": constants(),
        "in_w": blocks(turned(a + "in_proj_w")),
        "gate_w": blocks(turned(a + "gate_proj_w")),
        "dt_w": blocks(turned(a + "dt_w")),
        "bc_w": blocks(turned(a + "x_proj_w")),
        "out_w": blocks(turned(a + "out_proj_w")),
        "norm1": z[a + "norm1_w"].reshape(DC, P).T,
        "norm2": z[a + "ffn_norm_w"].reshape(DC, P).T,
        "dt_b": z[a + "dt_b"].reshape(EB, P).T,
        "A_log": blocks(z[a + "A_log"]).reshape(P, EB * N),
        "Dp": z[a + "Dp"].reshape(EB, P).T,
        "fg_w": blocks(turned(a + "ffn_gate_w")),
        "fu_w": blocks(turned(a + "ffn_up_w")),
        "fd_w": blocks(down[:whole]),
        "fd_last": down[whole:],
    }


def kernel(**inputs):
    import concourse.bacc as _bacc
    from concourse.bass_utils import run_bass_kernel_spmd as _run

    nc = _bacc.Bacc("TRN2", target_bir_lowering=False, num_devices=1)
    arrays = {name: np.ascontiguousarray(a) for name, a in layout({n: np.asarray(v) for n, v in inputs.items()}).items()}
    args = [nc.dram_tensor(name, a.shape, mybir.dt.from_np(a.dtype), kind="ExternalInput").ap() for name, a in arrays.items()]
    args.append(nc.dram_tensor("out", (T, D), F32, kind="ExternalOutput").ap())
    macaron(nc, *args)
    r = _run(nc, [arrays], core_ids=[0])
    return r.results[0]["out"].reshape(1, T, D)
```

```python
from contextlib import ExitStack, contextmanager

import numpy as np

import concourse.bass as bass
from concourse import mybir

F32 = mybir.dt.float32
I32 = mybir.dt.int32
ALU = mybir.AluOpType
ACT = mybir.ActivationFunctionType
X = mybir.AxisListType.X

P = 128
T = 4096
D = 256
DC = D // P
TT = T // P

E = 8
K = 2
H = 512
HC = H // P
SHARED = E
UP = DC * H
EXPERT = 2 * UP + HC * D
SLOT_TILES = K * T // P + E - 1
SLOTS = SLOT_TILES * P
ENTRY = 2
ID, WEIGHT = 0, 1
LN_EPS = 1e-5
RMS_EPS = 1e-6
RG = 2
GROUPS = TT // RG
LAG = 4
ROUTING_TILES = 8
PREFIX_TILE = EXP_TILE = 2

C_IDENT = 0
C_TRI = C_IDENT + P
C_ONES = C_TRI + P
C_TOKEN = C_ONES + P
C_START = C_TOKEN + TT
C_TILE = C_START + TT
C_RANK = C_TILE + SLOT_TILES
C_FILL = C_RANK + E
C_ZERO = C_FILL + ENTRY
CONSTS = C_ZERO + D


def constants():
    c = np.zeros((P, CONSTS), np.float32)
    p = np.arange(P)
    c[:, C_IDENT:C_IDENT + P] = np.eye(P)
    c[:, C_TRI:C_TRI + P] = p[:, None] < p[None, :]
    c[:, C_ONES:C_ONES + P] = 1.0
    c[:, C_TOKEN:C_TOKEN + TT] = np.arange(TT)[None, :] * P + p[:, None]
    c[:, C_START:C_START + TT] = np.arange(TT) * P
    c[:, C_TILE:C_TILE + SLOT_TILES] = np.arange(SLOT_TILES)
    c[:, C_RANK:C_RANK + E] = E - np.arange(E)
    c[:, C_FILL + ID] = T + p
    return c


def wait(eng, sem, value):
    if not isinstance(value, int) or value > 0:
        eng.wait_ge(sem, value)


@contextmanager
def phase(nc):
    sems = []

    def new(name):
        sems.append(nc.alloc_semaphore(name=name))
        return sems[-1]
    yield new
    nc.clear_and_free_semaphores(sems)
    nc.all_engine_barrier()


def moe(nc, tag, src, dst, normed, slots, weights, consts, const, W, later=()):
    ident = const[:, C_IDENT:C_IDENT + P]
    ones = const[:, C_ONES:C_ONES + P]
    src_g = src[0:T, :].rearrange("(g t p) d -> g p t d", t=RG, p=P)
    src_t = src[0:T, :].rearrange("(t p) d -> t p d", p=P)
    dst_t = dst.rearrange("(t p) d -> t p d", p=P)
    normed_t = normed.rearrange("(t p) d -> t p d", p=P)
    normed_g = normed[0:T, :].rearrange("(g t p) d -> g p t d", t=RG, p=P)
    slots_p = slots.rearrange("(p t) d -> p t d", t=SLOT_TILES)

    with phase(nc) as new, ExitStack() as ctx:
        def sb(name, shape, dt=F32):
            return ctx.enter_context(nc.sbuf_tensor(f"{tag}_{name}", shape, dt))

        def pb(name):
            return ctx.enter_context(nc.psum_tensor(f"{tag}_{name}", [P, 512], F32))

        def sem(name):
            return new(f"{tag}_{name}")

        bias = sb("bias", [P, E])
        router = sb("router", [P, DC, E])
        x_all = sb("x_all", [P, TT, D])
        entries = sb("entries", [P, K, TT, ENTRY])
        xnb = sb("xnb", [P, 2, RG, D])
        xTr = sb("xTr", [P, 2, DC, RG * P])
        stats = sb("stats", [P, 2, RG, 6])
        mv = sb("mv", [P, 2, RG, 2])
        ve = sb("ve", [P, 2, RG])
        rstd = sb("rstd", [P, 2, RG])
        nhalf = sb("nhalf", [P, RG])
        L = sb("L", [P, TT, E])
        scratch = sb("scratch", [P, TT, E])
        oh1 = sb("oh1", [P, TT, E])
        oh2 = sb("oh2", [P, TT, E])
        incl = sb("incl", [P, TT, E])
        cmp = sb("cmp", [P, E, TT])
        m1 = sb("m1", [P, TT])
        m2 = sb("m2", [P, TT])
        r1 = sb("r1", [P, TT])
        ex = sb("ex", [P, TT])
        w0 = sb("w0", [P, TT])
        w1 = sb("w1", [P, TT])
        posf = sb("posf", [P, 2, TT])
        slot = sb("slot", [P, 2, TT], I32)
        slot_tile = sb("slot_tile", [P, 2, TT], I32)
        pos = sb("pos", [P, 2, TT], I32)
        tiles = sb("tiles", [P, E])
        tend = sb("tend", [P, E])
        base = sb("base", [P, E])
        tile_cmp = sb("tile_cmp", [1, SLOT_TILES, E])
        tile_sum = sb("tile_sum", [1, SLOT_TILES])
        tile_expert = sb("tile_expert", [1, SLOT_TILES], I32)
        slot_info = sb("slot_info", [P, SLOT_TILES, ENTRY])
        slot_ids = sb("slot_ids", [P, SLOT_TILES], I32)
        xs = sb("xs", [P, 2, D])
        xT = sb("xT", [P, DC * P])
        sg = sb("sg", [P, H])
        hs = sb("hs", [P, H])
        hT = sb("hT", [P, HC * P])
        ys = sb("ys", [P, 2, D])

        pX = pb("pX")
        pL = pb("pL")
        pG = pb("pG")
        pU = pb("pU")
        pH = pb("pH")
        pY = pb("pY")
        pC = pb("pC")

        s_const = sem("const")
        s_bias = sem("bias")
        s_w = [sem(f"w{e}") for e in range(E + 1)]
        s_fill = sem("fill")
        s_spare = sem("spare")
        s_xin = [sem(f"xin{q}") for q in range(2)]
        s_nhalf = sem("nhalf")
        s_bns = sem("bns")
        s_bna = sem("bna")
        s_ve = sem("ve")
        s_rs = sem("rs")
        s_norm = sem("norm")
        s_tr = sem("tr")
        s_xTr = sem("xTr")
        s_lg = sem("lg")
        s_L = sem("L")
        s_kept = [sem(f"kept{q}") for q in range(2)]
        s_zeros = sem("zeros")
        s_chain = sem("chain")
        s_diff = sem("diff")
        s_ex = sem("ex")
        s_oh = sem("oh")
        s_prefix = sem("prefix")
        s_pos = sem("pos")
        s_map = sem("map")
        s_entry = sem("entry")
        s_info = sem("info")
        s_ids = sem("ids")
        s_scat = sem("scat")
        s_sent = sem("sent")

        block = ctx.enter_context(nc.Block())

        def pipe(name):
            names = ("xt", "xT", "g", "u", "sg", "h", "ht", "hT", "y", "ys")
            d = {n: sem(f"{name}_{n}") for n in names}
            d["load"] = [sem(f"{name}_load{q}") for q in range(2)]
            d["store"] = [sem(f"{name}_store{q}") for q in range(2)]
            return d

        S = pipe("s")
        R = pipe("r")
        s_add = sem("add")

        def over_tiles(eng, n, step, head=2):
            for i in range(head):
                step(i, i % 2)
            pairs = (n - 1 - head) // 2
            with eng.Fori(head // 2, head // 2 + pairs) as j:
                step(j * 2, 0)
                step(j * 2 + 1, 1)
            for i in range(head + 2 * pairs, n):
                step(i, i % 2)

        @block.sync
        def _(sp):
            sp.dma_start(const[:, :], consts).then_inc(s_const, 16)
            sp.dma_start(router[:, :, :], weights["router"]).then_inc(s_bias, 16)
            sp.dma_start(bias[:, :], weights["bias"].partition_broadcast(P)).then_inc(s_bias, 16)

            def load_group(g, q):
                wait(sp, s_xin[q], (g - q) * 8)
                sp.dma_start(x_all[:, bass.ds(g * RG, RG), :], src_g[bass.ds(g, 1)].rearrange("a p t d -> p (a t) d")).then_inc(s_xin[q], 16)

            def keep_group(g, q):
                sp.wait_ge(s_norm, RG * (g + 1))
                sp.dma_start(normed_g[bass.ds(g, 1)].rearrange("a p t d -> p (a t) d"), xnb[:, q, :, :]).then_inc(s_kept[q], 16)
            load_group(0, 0)
            load_group(1, 1)
            load_group(2, 0)
            load_group(3, 1)
            with sp.Fori(0, GROUPS // 2 - 2) as j:
                keep_group(j * 2, 0)
                load_group(j * 2 + 4, 0)
                keep_group(j * 2 + 1, 1)
                load_group(j * 2 + 5, 1)
            sp.dma_start(W[:, SHARED, :], weights["moe"][SHARED]).then_inc(s_w[SHARED], 16)
            for g in range(GROUPS - 4, GROUPS):
                keep_group(g, g % 2)
            def shared_load(i, q):
                wait(sp, S["xt"], i - 1)
                sp.dma_start(xs[:, q, :], normed_t[bass.ds(i, 1)].rearrange("a p d -> p (a d)")).then_inc(S["load"][q], 16)

            def shared_store(i, q):
                sp.wait_ge(S["ys"], i + 1)
                sp.dma_start(dst_t[bass.ds(i, 1)].rearrange("a p d -> p (a d)"), ys[:, q, :]).then_inc(S["store"][q], 16)
            sp.wait_ge(s_kept[0], 16)
            shared_load(0, 0)
            shared_load(1, 1)
            for q in range(2):
                sp.wait_ge(s_kept[q], 8 * GROUPS)

            def shared(i, q):
                shared_load(i + 2, q)
                if isinstance(i, int) and i < E:
                    sp.dma_start(W[:, i, :], weights["moe"][i]).then_inc(s_w[i], 16)
                shared_store(i, q)
            over_tiles(sp, TT - 2, shared, E)
            for to, from_, s in later:
                sp.dma_start(to, from_).then_inc(s, 16)
            for i in range(TT - 2, TT):
                shared_store(i, i % 2)

        @block.gpsimd
        def _(pool):
            pool.memset(nhalf[:, :], -0.5).then_inc(s_nhalf, 1)
            pool.wait_ge(s_nhalf, 1)

            def group(g, q):
                pool.wait_ge(s_ve, g + 1)
                nc.gpsimd.tensor_tensor(rstd[:, q, :], ve[:, q, :], nhalf[:, :], ALU.pow).then_inc(s_rs, 1)
            over_tiles(pool, GROUPS, group)
            pool.wait_ge(s_const, 16)
            for k in range(K):
                nc.gpsimd.tensor_copy(entries[:, k, :, ID:ID + 1], const[:, C_TOKEN:C_TOKEN + TT].unsqueeze(2)).then_inc(s_entry, 1)
            pool.wait_ge(s_pos, 1)
            for k in range(K):
                nc.gpsimd.tensor_copy(entries[:, k, :, WEIGHT:WEIGHT + 1], (w0, w1)[k][:, :].unsqueeze(2)).then_inc(s_entry, 1)
            pool.wait_ge(s_entry, 2 * K)
            pool.wait_ge(s_fill, 16)
            for k in range(K):
                for t in range(TT):
                    nc.gpsimd.indirect_dma_start(
                        out=slots, out_offset=bass.IndirectOffsetOnAxis(ap=pos[:, k, t:t + 1], axis=0),
                        in_=entries[:, k, t, :], in_offset=None).then_inc(s_scat, 16)
            pool.wait_ge(s_scat, 16 * TT * K)
            nc.gpsimd.memset(nhalf[:, 0:1], 0.0).then_inc(s_sent, 1)

            def gather(i):
                nc.gpsimd.indirect_dma_start(
                    out=xs[:, i % 2, :], out_offset=None, in_=normed,
                    in_offset=bass.IndirectOffsetOnAxis(ap=slot_ids[:, i:i + 1], axis=0)).then_inc(R["load"][i % 2], 16)

            def add(i):
                wait(pool, s_add, 16 * i)
                pool.wait_ge(R["ys"], i + 1)
                nc.gpsimd.indirect_dma_start(
                    out=dst, out_offset=bass.IndirectOffsetOnAxis(ap=slot_ids[:, i:i + 1], axis=0),
                    in_=ys[:, i % 2, :], in_offset=None, compute_op=ALU.add).then_inc(s_add, 16)

            pool.wait_ge(s_ids, 1)
            pool.wait_ge(s_zeros, 16)
            pool.wait_ge(S["xt"], TT)
            for i in range(SLOT_TILES + LAG):
                if i < SLOT_TILES:
                    wait(pool, R["xt"], i - 1)
                    gather(i)
                if i == LAG:
                    for q in range(2):
                        pool.wait_ge(S["store"][q], 16 * TT // 2)
                    pool.wait_ge(s_spare, 16)
                if i >= LAG:
                    add(i - LAG)
            pool.wait_ge(s_add, 16 * SLOT_TILES)

        @block.scalar
        def _(act):

            def group(g, q):
                act.wait_ge(s_tr, g + 1)
                wait(act, s_lg, g - 1)
                nc.scalar.activation(xTr[:, q, :, :].rearrange("p c n -> p (c n)"), (pX, pG)[q][:, :], ACT.Copy).then_inc(s_xTr, 1)
            over_tiles(act, GROUPS, group)
            act.wait_ge(s_const, 16)
            act.dma_start(slots_p,
                          const[:, C_FILL:C_FILL + ENTRY].unsqueeze(1).broadcast_to([P, SLOT_TILES, ENTRY])).then_inc(s_fill, 16)
            act.dma_start(dst_t[TT], const[:, C_ZERO:C_ZERO + D]).then_inc(s_spare, 16)
            act.dma_start(normed_t[TT], const[:, C_ZERO:C_ZERO + D]).then_inc(s_zeros, 16)

            def silu_and_hT(Q, i):
                act.wait_ge(Q["g"], i + 1)
                wait(act, Q["h"], i)
                nc.scalar.activation(sg[:, :], pG[:, :], ACT.Silu).then_inc(Q["sg"], 1)
                act.wait_ge(Q["ht"], i + 1)
                nc.scalar.activation(hT[:, :], pH[:, :], ACT.Copy).then_inc(Q["hT"], 1)

            def shared(i, q):
                silu_and_hT(S, i)
                if isinstance(i, int) and i == EXP_TILE:
                    act.wait_ge(s_diff, 1)
                    nc.scalar.activation(ex[:, :], r1[:, :], ACT.Exp).then_inc(s_ex, 1)
            over_tiles(act, TT, shared, ROUTING_TILES)
            act.wait_ge(s_sent, 1)
            act.dma_start(slot_info[:, :, :], slots_p).then_inc(s_info, 16)
            over_tiles(act, SLOT_TILES, lambda i, q: silu_and_hT(R, i))

        @block.tensor
        def _(pe):
            pe.wait_ge(s_const, 16)
            pe.wait_ge(s_bias, 32)

            def logits(g, q):
                pe.wait_ge(s_xTr, g + 1)
                for t in range(RG):
                    for c in range(DC):
                        last = nc.tensor.matmul(pL[:, bass.ds((g * RG + t) * E, E)], xTr[:, q, c, t * P:(t + 1) * P],
                                                router[:, c, :], start=(c == 0), stop=(c == DC - 1))
                last.then_inc(s_lg, 1)

            def group(g, q):
                pe.wait_ge(s_norm, RG * (g + 1))
                wait(pe, s_xTr, g - 1)
                for c in range(DC):
                    for t in range(RG):
                        last = nc.tensor.transpose((pX, pG)[q][:, (c * RG + t) * P:(c * RG + t + 1) * P],
                                                   xnb[:, q, t, c * P:(c + 1) * P], ident)
                last.then_inc(s_tr, 1)
                if not isinstance(g, int) or g > 0:
                    logits(g - 1, 1 - q)
            over_tiles(pe, GROUPS, group)
            logits(GROUPS - 1, (GROUPS - 1) % 2)

            def prefix():
                pe.wait_ge(s_oh, 1)
                chosen = scratch[:, :, :].rearrange("p t e -> p (t e)")
                nc.tensor.matmul(pL[:, 0:TT * E], const[:, C_TRI:C_TRI + P], chosen, start=True, stop=True)
                nc.tensor.matmul(pC[:, 0:TT * E], ones, chosen, start=True, stop=True).then_inc(s_prefix, 1)

            Wf = W[:, :, :].rearrange("p e n -> p (e n)")

            def expert(e, at, n):
                return Wf[:, bass.ds(e * EXPERT + at, n)]

            def turn_x(Q, q, ready, free):
                for s, v in ready:
                    pe.wait_ge(s, v)
                for s, v in free:
                    wait(pe, s, v)
                for c in range(DC):
                    last = nc.tensor.transpose(pX[:, c * P:(c + 1) * P], xs[:, q, c * P:(c + 1) * P], ident)
                last.then_inc(Q["xt"], 1)

            def up(Q, i, e):
                pe.wait_ge(Q["xT"], i + 1)
                wait(pe, Q["h"], i)
                for bank, at, s in ((pG, 0, "g"), (pU, UP, "u")):
                    for c in range(DC):
                        last = nc.tensor.matmul(bank[:, :], xT[:, c * P:(c + 1) * P], expert(e, at + c * H, H),
                                                start=(c == 0), stop=(c == DC - 1))
                    last.then_inc(Q[s], 1)

            def down(Q, i, e):
                pe.wait_ge(Q["hT"], i + 1)
                wait(pe, Q["ys"], i)
                for k in range(HC):
                    last = nc.tensor.matmul(pY[:, 0:D], hT[:, k * P:(k + 1) * P], expert(e, 2 * UP + k * D, D),
                                            start=(k == 0), stop=(k == HC - 1))
                last.then_inc(Q["y"], 1)

            def turn_h(Q, i):
                pe.wait_ge(Q["h"], i + 1)
                wait(pe, Q["hT"], i)
                for k in range(HC):
                    last = nc.tensor.transpose(pH[:, k * P:(k + 1) * P], hs[:, k * P:(k + 1) * P], ident)
                last.then_inc(Q["ht"], 1)

            pe.wait_ge(s_w[SHARED], 16)
            turn_x(S, 0, [(S["load"][0], 16)], [])

            def shared(i, q):
                up(S, i, SHARED)
                if not isinstance(i, int) or i + 1 < TT:
                    turn_x(S, 1 - q, [(S["load"][1 - q], (i + 1 - (1 - q)) * 8 + 16)], [(S["xT"], i + 1)])
                if not isinstance(i, int) or i > 0:
                    down(S, i - 1, SHARED)
                turn_h(S, i)
                if isinstance(i, int) and i == PREFIX_TILE:
                    prefix()
            over_tiles(pe, TT, shared, ROUTING_TILES)
            down(S, TT - 1, SHARED)

            for e in range(E):
                pe.wait_ge(s_w[e], 16)
            pe.wait_ge(s_map, 1)
            turn_x(R, 0, [(R["load"][0], 16)], [(S["xT"], TT)])

            def routed(i, q):
                e = pe.value_load(tile_expert[0:1, bass.ds(i, 1)], min_val=0, max_val=E - 1)
                if isinstance(i, int) and i == 0:
                    pe.wait_ge(S["ys"], TT)
                up(R, i, e)
                if not isinstance(i, int) or i + 1 < SLOT_TILES:
                    n = (i + 1 - (1 - q)) * 8 + 16
                    turn_x(R, 1 - q, [(R["load"][1 - q], n)], [(R["xT"], i + 1)])
                if not isinstance(i, int) or i > 0:
                    before = pe.value_load(tile_expert[0:1, bass.ds(i - 1, 1)], min_val=0, max_val=E - 1)
                    down(R, i - 1, before)
                turn_h(R, i)
            over_tiles(pe, SLOT_TILES, routed)
            down(R, SLOT_TILES - 1, pe.value_load(tile_expert[0:1, SLOT_TILES - 1:SLOT_TILES], min_val=0, max_val=E - 1))

        @block.vector
        def _(dve):
            def statistics(g, q):
                for t in range(RG):
                    nc.vector.bn_stats(stats[:, q, t, :], x_all[:, bass.ds(g * RG + t, 1), :].rearrange("p a d -> p (a d)")).then_inc(s_bns, 1)

            def variance(g, q):
                for t in range(RG):
                    nc.vector.bn_aggr(mv[:, q, t, :], stats[:, q, t, :]).then_inc(s_bna, 1)
                dve.wait_ge(s_bna, RG * (g + 1))
                nc.vector.tensor_scalar(ve[:, q, :], mv[:, q, :, 1], LN_EPS, None, ALU.add).then_inc(s_ve, 1)

            def ahead(g, by):
                return not isinstance(g, int) or g + by < GROUPS

            def group(g, q):
                if ahead(g, 2):
                    dve.wait_ge(s_xin[q], (g + 2 - q) * 8 + 16)
                if ahead(g, 1):
                    dve.wait_ge(s_bns, RG * (g + 2))
                dve.wait_ge(s_rs, g + 1)
                wait(dve, s_tr, g - 1)
                wait(dve, s_kept[q], (g - q) * 8)
                wait(dve, s_norm, RG * g)
                for t in range(RG):
                    nc.vector.tensor_scalar(xnb[:, q, t, :], x_all[:, bass.ds(g * RG + t, 1), :].rearrange("p a d -> p (a d)"),
                                            mv[:, q, t, 0:1], rstd[:, q, t:t + 1], ALU.subtract, ALU.mult).then_inc(s_norm, 1)
                if ahead(g, 1):
                    variance(g + 1, 1 - q)
                if ahead(g, 2):
                    statistics(g + 2, q)
            for g in range(2):
                dve.wait_ge(s_xin[g], 16)
                statistics(g, g)
            dve.wait_ge(s_bns, RG)
            variance(0, 0)
            over_tiles(dve, GROUPS, group)
            dve.wait_ge(s_bias, 32)
            dve.wait_ge(s_lg, GROUPS)
            nc.vector.tensor_tensor(L[:, :, :], pL[:, 0:TT * E].rearrange("p (t e) -> p t e", e=E),
                                    bias[:, :].unsqueeze(1).broadcast_to([P, TT, E]), ALU.add).then_inc(s_L, 1)
            dve.wait_ge(s_const, 16)

            chained = [0]

            def link(ins):
                chained[0] += 1
                ins.then_inc(s_chain, 1)
                dve.wait_ge(s_chain, chained[0])

            v = nc.vector
            total = pC[:, 0:TT * E].rearrange("p (t e) -> p t e", e=E)
            within = pL[:, 0:TT * E].rearrange("p (t e) -> p t e", e=E)

            def per_tile(a):
                return a.unsqueeze(2).broadcast_to([P, TT, E])

            def per_expert(a):
                return a.unsqueeze(1).broadcast_to([P, TT, E])
            rank = per_expert(const[:, C_RANK:C_RANK + E])

            def first_of_max(m, onehot):
                link(v.tensor_reduce(m[:, :], L[:, :, :], X, ALU.max))
                link(v.tensor_tensor(scratch[:, :, :], L[:, :, :], per_tile(m[:, :]), ALU.is_equal))
                link(v.tensor_tensor(scratch[:, :, :], scratch[:, :, :], rank, ALU.mult))
                link(v.tensor_reduce(r1[:, :], scratch[:, :, :], X, ALU.max))
                link(v.tensor_tensor(onehot[:, :, :], scratch[:, :, :], per_tile(r1[:, :]), ALU.is_equal))

            def slot_of(k, onehot):
                link(v.tensor_tensor(onehot[:, :, :], onehot[:, :, :], incl[:, :, :], ALU.mult))
                link(v.tensor_reduce(posf[:, k, :], onehot[:, :, :], X, ALU.add))

            def routing(step):
                if step == 0:
                    dve.wait_ge(s_L, 1)
                    first_of_max(m1, oh1)
                if step == 1:
                    link(v.scalar_tensor_tensor(L[:, :, :], oh1[:, :, :], -3e38, L[:, :, :], op0=ALU.mult, op1=ALU.add))
                    first_of_max(m2, oh2)
                    v.tensor_tensor(scratch[:, :, :], oh1[:, :, :], oh2[:, :, :], ALU.add).then_inc(s_oh, 1)
                    v.tensor_tensor(r1[:, :], m2[:, :], m1[:, :], ALU.subtract).then_inc(s_diff, 1)
                if step == 3:
                    dve.wait_ge(s_prefix, 1)
                    for e in range(E):
                        last = v.tensor_tensor_scan(incl[:, :, e], ones[:, 0:TT], total[:, :, e], initial=0.0, op0=ALU.mult, op1=ALU.add)
                        if e < E - 1:
                            last.then_inc(s_chain, 1)
                            chained[0] += 1
                    link(last)
                    count = incl[:, TT - 1, :]
                    link(v.tensor_tensor(cmp[:, :, :], count.unsqueeze(2).broadcast_to([P, E, TT]),
                                         const[:, C_START:C_START + TT].unsqueeze(1).broadcast_to([P, E, TT]), ALU.is_gt))
                    link(v.tensor_reduce(tiles[:, :], cmp[:, :, :], X, ALU.add))
                if step == 4:
                    link(v.tensor_tensor_scan(tend[:, :], ones[:, 0:E], tiles[:, :], initial=0.0, op0=ALU.mult, op1=ALU.add))
                    link(v.tensor_tensor(base[:, :], tend[:, :], tiles[:, :], ALU.subtract))
                    link(v.tensor_tensor(incl[:, :, :], incl[:, :, :], total, ALU.subtract))
                    link(v.tensor_tensor(incl[:, :, :], incl[:, :, :], within, ALU.add))
                    link(v.scalar_tensor_tensor(incl[:, :, :], per_expert(base[:, :]), float(P), incl[:, :, :], op0=ALU.mult, op1=ALU.add))
                if step == 5:
                    slot_of(0, oh1)
                    slot_of(1, oh2)
                    link(v.tensor_copy(slot[:, :, :], posf[:, :, :]))
                    link(v.tensor_scalar(slot_tile[:, :, :], slot[:, :, :], P.bit_length() - 1, None, ALU.logical_shift_right))
                    link(v.tensor_scalar(slot[:, :, :], slot[:, :, :], P - 1, None, ALU.bitwise_and))
                    link(v.scalar_tensor_tensor(pos[:, :, :], slot[:, :, :], float(SLOT_TILES), slot_tile[:, :, :],
                                                op0=ALU.mult, op1=ALU.add))
                if step == 6:
                    dve.wait_ge(s_ex, 1)
                    link(v.tensor_scalar(m1[:, :], ex[:, :], 1.0, None, ALU.add))
                    link(v.reciprocal(m2[:, :], m1[:, :]))
                    link(v.tensor_scalar(w0[:, :], m2[:, :], 0.5, None, ALU.mult))
                    v.tensor_tensor(w1[:, :], w0[:, :], ex[:, :], ALU.mult).then_inc(s_pos, 1)
                if step == 7:
                    link(v.tensor_tensor(tile_cmp[:, :, :], tend[0:1, :].unsqueeze(1).broadcast_to([1, SLOT_TILES, E]),
                                         const[0:1, C_TILE:C_TILE + SLOT_TILES].unsqueeze(2).broadcast_to([1, SLOT_TILES, E]), ALU.is_le))
                    link(v.tensor_reduce(tile_sum[:, :], tile_cmp[:, :, :], X, ALU.add))
                    v.tensor_scalar(tile_expert[:, :], tile_sum[:, :], float(E - 1), None, ALU.min).then_inc(s_map, 1)

            def take_x(Q, i):
                dve.wait_ge(Q["xt"], i + 1)
                nc.vector.tensor_copy(xT[:, :], pX[:, 0:DC * P]).then_inc(Q["xT"], 1)

            def gate(Q, i):
                dve.wait_ge(Q["sg"], i + 1)
                dve.wait_ge(Q["u"], i + 1)
                nc.vector.tensor_tensor(hs[:, :], sg[:, :], pU[:, :], ALU.mult).then_inc(Q["h"], 1)

            def shared_sum(i, q):
                dve.wait_ge(S["y"], i + 1)
                wait(dve, S["store"][q], (i - q) * 8)
                nc.vector.scalar_tensor_tensor(ys[:, q, :], pY[:, 0:D], 0.5,
                                               x_all[:, bass.ds(i, 1), :].rearrange("p a d -> p (a d)"),
                                               op0=ALU.mult, op1=ALU.add).then_inc(S["ys"], 1)

            take_x(S, 0)

            def shared(i, q):
                gate(S, i)
                if not isinstance(i, int) or i + 1 < TT:
                    take_x(S, i + 1)
                if not isinstance(i, int) or i > 0:
                    shared_sum(i - 1, 1 - q)
                if isinstance(i, int) and i < ROUTING_TILES:
                    routing(i)
            over_tiles(dve, TT, shared, ROUTING_TILES)
            shared_sum(TT - 1, (TT - 1) % 2)

            def weigh(i, q):
                dve.wait_ge(R["y"], i + 1)
                wait(dve, s_add, (i - 1) * 16)
                nc.vector.tensor_scalar(ys[:, q, :], pY[:, 0:D], slot_info[:, bass.ds(i, 1), WEIGHT], None, ALU.mult).then_inc(R["ys"], 1)

            dve.wait_ge(s_info, 16)
            nc.vector.tensor_copy(slot_ids[:, :], slot_info[:, :, ID]).then_inc(s_ids, 1)
            for q in range(2):
                dve.wait_ge(S["store"][q], 16 * TT // 2)
            take_x(R, 0)

            def routed(i, q):
                gate(R, i)
                if not isinstance(i, int) or i + 1 < SLOT_TILES:
                    take_x(R, i + 1)
                if not isinstance(i, int) or i > 0:
                    weigh(i - 1, 1 - q)
            over_tiles(dve, SLOT_TILES, routed)
            weigh(SLOT_TILES - 1, (SLOT_TILES - 1) % 2)


DI = 512
EB = DI // P
N = 16
F = 704
FB = -(-F // P)
CH = 512
CT = CH // P
CHUNKS = T // CH
UNITS = N * EB
F_LAST = F - (FB - 1) * P
TURN_LAG, SUM_LAG, KEEP_LAG = 5, 7, 2
AHEAD = 2
A_BUFS, B_BUFS, H_BUFS, HT_BANKS = 4, 4, 4, 4

MAMBA_WEIGHTS = {
    "in_w": [P, DC, DI], "gate_w": [P, DC, DI], "dt_w": [P, EB, DI], "bc_w": [P, EB, 2 * N],
    "out_w": [P, EB, D], "norm1": [P, DC], "norm2": [P, DC], "dt_b": [P, EB], "A_log": [P, EB * N], "Dp": [P, EB],
}
FFN_WEIGHTS = {"fg_w": [P, DC, F], "fu_w": [P, DC, F], "fd_w": [P, FB - 1, D], "fd_last": [F_LAST, D]}


def mamba(nc, src, dst, b_rows, w, ffn, const, s_weights):
    ident = const[:, C_IDENT:C_IDENT + P]
    src_c = src[0:T, :].rearrange("(c t p) d -> c p t d", t=CT, p=P)
    dst_c = dst[0:T, :].rearrange("(c t p) d -> c p t d", t=CT, p=P)

    with phase(nc) as new, ExitStack() as ctx:
        def sb(name, shape, dt=F32):
            return ctx.enter_context(nc.sbuf_tensor(f"b_{name}", shape, dt))

        def pb(name):
            return ctx.enter_context(nc.psum_tensor(f"b_{name}", [P, 512], F32))

        def sem(name):
            return new(f"b_{name}")

        w = dict(w, **{name: sb(name, shape) for name, shape in FFN_WEIGHTS.items()})
        xf = sb("xf", [P, CT, D])
        xb = sb("xb", [P, CT, D])
        yln = sb("yln", [P, 2, CT, D])
        hrow = sb("hrow", [P, CT, D])
        hT = sb("hT", [P, DC, CH])
        z = sb("z", [P, 2, EB, CH])
        dt = sb("dt", [P, 2, EB, CH])
        dtz = sb("dtz", [P, 2, EB, CH])
        C = sb("C", [P, 2, CT, N])
        Bt = sb("Bt", [N, CH])
        Bn = sb("Bn", [P, 2, CH])
        acc = sb("acc", [P, CT, DI])
        xa = sb("xa", [P, CT, D])
        hnT = sb("hnT", [P, DC, CH])
        ff = sb("ff", [P, FB, CH])
        dA = sb("dA", [P, A_BUFS, CH])
        dB = sb("dB", [P, B_BUFS, CH])
        h = sb("h", [P, H_BUFS, EB, CH])
        eF = sb("eF", [P, CH])
        eB = sb("eB", [P, CH])
        ea = sb("ea", [P, CH])
        eo = sb("eo", [P, CH])
        el = sb("el", [P, CH])
        state = sb("state", [P, N, EB])
        negA = sb("negA", [P, EB * N])
        stats = sb("stats", [P, CT, 6])
        mv = sb("mv", [P, CT, 2])
        ve = sb("ve", [P, CT])
        rstd = sb("rstd", [P, CT])
        sq = sb("sq", [P, D])
        ssq = sb("ssq", [P, 2, CT])
        ms = sb("ms", [P, 2, CT])
        rr = sb("rr", [P, 2, CT])
        nhalf = sb("nhalf", [P, CT])

        pH = [pb(f"pH{i}") for i in range(HT_BANKS)]
        pF = [pb(f"pF{i}") for i in range(2)]
        pK = [pb(f"pK{i}") for i in range(2)]
        pY = [pK[0], pK[1], pF[0], pF[1]]
        F_USES = (3 + EB, 1 + 2 * EB)
        K_USES = 3 + FB

        s_ffn = sem("ffn")
        s_fld = sem("fld")
        s_bld = sem("bld")
        s_stored = sem("stored")
        s_bt = sem("bt")
        s_Bn = [sem(f"Bn{i}") for i in range(2)]
        s_init = sem("init")
        s_neg = sem("neg")
        s_bns = sem("bns")
        s_bna = sem("bna")
        s_ve = sem("ve")
        s_rstd = sem("rstd")
        s_ln = sem("ln")
        s_y = sem("y")
        s_sq = sem("sq")
        s_ms = [sem(f"ms{i}") for i in range(2)]
        s_rr = [sem(f"rr{i}") for i in range(2)]
        s_hrow = sem("hrow")
        s_hT = sem("hT")
        s_eF = sem("eF")
        s_lnF = sem("lnF")
        s_sigF = sem("sigF")
        s_z = sem("z")
        s_C = sem("C")
        s_Bt = sem("Bt")
        s_relu = sem("relu")
        s_ea0 = sem("ea0")
        s_ea = sem("ea")
        s_eo0 = sem("eo0")
        s_eo = sem("eo")
        s_el = sem("el")
        s_p1 = sem("p1")
        s_p2 = sem("p2")
        s_dt = sem("dt")
        s_dtz = sem("dtz")
        s_fullF = [sem(f"fullF{i}") for i in range(2)]
        s_fullK = [sem(f"fullK{i}") for i in range(2)]
        s_yT = sem("yT")
        s_ssm = sem("ssm")
        s_xa = sem("xa")
        s_base = sem("base")
        s_hn = sem("hn")
        s_hnT = sem("hnT")
        s_eB = sem("eB")
        s_lnB = sem("lnB")
        s_sigB = sem("sigB")
        s_gu = sem("gu")
        s_ff = sem("ff")
        s_x2 = sem("x2")
        s_dA = sem("dA")
        s_dB = sem("dB")
        s_scan = sem("scan")
        s_state = sem("state")
        s_ht = sem("ht")
        s_acc = sem("acc")

        block = ctx.enter_context(nc.Block())

        def chunks(eng, slots):
            slots(0, 0, True, False)
            with eng.Fori(0, CHUNKS // 2 - 1) as j:
                slots(j * 2 + 1, 1, True, True)
                slots(j * 2 + 2, 0, True, True)
            slots(CHUNKS - 1, 1, False, True)

        def of(c, q, u):
            u0 = u % UNITS
            return u0 // EB, u0 % EB, q if 0 <= u < UNITS else 1 - q, c * UNITS + u

        def squares_before(side, c):
            if side == 0:
                backs = max(c - 2, 0) if isinstance(c, int) else c - 2
                return (backs + c) * CT
            fronts = min(c + 3, CHUNKS) if isinstance(c, int) else c + 3
            return (fronts + c) * CT

        @block.sync
        def _(sp):
            def load(rows, c, s):
                sp.dma_start(rows, src_c[bass.ds(c, 1)].rearrange("a p t d -> p (a t) d")).then_inc(s, 16)

            def spread_B(c, n):
                if n == 0:
                    sp.wait_ge(s_bt, 16 * (c + 1))
                wait(sp, s_dB, (c * N + n - 1) * EB)
                sp.dma_start(Bn[:, n % 2, :], b_rows[bass.ds(c * N + n, 1)].rearrange("a m -> (a m)").partition_broadcast(P)).then_inc(s_Bn[n % 2], 16)

            def store_B(c):
                sp.wait_ge(s_Bt, c + 1)
                sp.dma_start(b_rows[bass.ds(c * N, N)], Bt[:, :]).then_inc(s_bt, 16)

            def store_rows(c):
                sp.wait_ge(s_x2, 2 * (c + 1))
                sp.dma_start(dst_c[bass.ds(c, 1)].rearrange("a p t d -> p (a t) d"), xb[:, :, :]).then_inc(s_stored, 16)
                sp.wait_ge(s_stored, 16 * (c + 1))

            def chunk(c, store, xb_load, xf_load, front):
                for n in range(N):
                    spread_B(c, n)
                    if n == 1:
                        if store:
                            store_rows(c - 2)
                        if xb_load:
                            load(xb[:, :, :], c - 1, s_bld)
                    if n == 6 and xf_load:
                        sp.wait_ge(s_y, CT * (c + 2))
                        load(xf[:, :, :], c + 2, s_fld)
                    if n == 11 and front:
                        store_B(c + 1)
            load(xf[:, :, :], 0, s_fld)
            for name in FFN_WEIGHTS:
                sp.dma_start(w[name][:], ffn[name]).then_inc(s_ffn, 16)
            sp.wait_ge(s_y, CT)
            load(xf[:, :, :], 1, s_fld)
            store_B(0)
            chunk(0, False, False, True, True)
            chunk(1, False, True, True, True)
            with sp.Fori(2, CHUNKS - 2) as c:
                chunk(c, True, True, True, True)
            chunk(CHUNKS - 2, True, True, False, True)
            chunk(CHUNKS - 1, True, True, False, False)
            store_rows(CHUNKS - 2)
            load(xb[:, :, :], CHUNKS - 1, s_bld)
            store_rows(CHUNKS - 1)

        @block.gpsimd
        def _(pool):
            g = nc.gpsimd
            g.memset(nhalf[:, :], -0.5).then_inc(s_init, 1)
            g.memset(state[:, :, :], 0.0).then_inc(s_init, 1)
            pool.wait_ge(s_init, 2)

            def rms(side, c):
                pool.wait_ge(s_ms[side], c + 1)
                g.tensor_tensor(rr[:, side, :], ms[:, side, :], nhalf[:, :], ALU.pow).then_inc(s_rr[side], 1)

            def front(u, c, q):
                if u == 2:
                    pool.wait_ge(s_ve, c + 1)
                    g.tensor_tensor(rstd[:, :], ve[:, :], nhalf[:, :], ALU.pow).then_inc(s_rstd, 1)
                if u == 7:
                    rms(0, c)
                for b in range(EB):
                    n = c * EB + b + 1
                    if u == 38 + 4 * b:
                        pool.wait_ge(s_el, n)
                        g.tensor_tensor(dt[:, q, b, :], dt[:, q, b, :], el[:, :], ALU.add).then_inc(s_p1, 1)
                    if u == 39 + 4 * b:
                        pool.wait_ge(s_eo, n)
                        g.tensor_tensor(eo[:, :], ea[:, :], eo[:, :], ALU.subtract).then_inc(s_p2, 1)
                    if u == 40 + 4 * b:
                        pool.wait_ge(s_p1, n)
                        pool.wait_ge(s_p2, n)
                        g.tensor_tensor(dt[:, q, b, :], dt[:, q, b, :], eo[:, :], ALU.add).then_inc(s_dt, 1)
                    if u == 41 + 4 * b:
                        pool.wait_ge(s_dt, n)
                        pool.wait_ge(s_z, n)
                        g.tensor_tensor(dtz[:, q, b, :], dt[:, q, b, :], z[:, q, b, :], ALU.mult).then_inc(s_dtz, 1)

            def back(u, c, q):
                for i in range(2):
                    if u == 17 + i:
                        pool.wait_ge(s_xa, 2 * (c + 1))
                        pool.wait_ge(s_bld, 16 * (c + 1))
                        g.tensor_tensor(xb[:, 2 * i:2 * i + 2, :], xb[:, 2 * i:2 * i + 2, :], xa[:, 2 * i:2 * i + 2, :], ALU.add).then_inc(s_base, 1)
                if u == 20:
                    rms(1, c)

            def input_of_scan(u, c, q):
                n, k, q, U = of(c, q, u)
                if k == 0:
                    pool.wait_ge(s_Bn[n % 2], (c * N + u // EB - n % 2) * 8 + 16)
                    pool.wait_ge(s_dtz, EB * (c + 1 + u // UNITS))
                wait(pool, s_scan, U - B_BUFS + 1)
                g.tensor_tensor(dB[:, u % B_BUFS, :], dtz[:, q, k, :], Bn[:, n % 2, :], ALU.mult).then_inc(s_dB, 1)

            def slots(c, q, has_front, has_back):
                for u in range(UNITS):
                    if u + AHEAD < UNITS or has_front:
                        input_of_scan(u + AHEAD, c, q)
                    if has_front:
                        front(u, c + 1, 1 - q)
                    if has_back:
                        back(u, c - 1, 1 - q)
            for u in range(UNITS):
                front(u, 0, 0)
            for u in range(AHEAD):
                input_of_scan(u, 0, 0)
            chunks(pool, slots)
            for u in range(UNITS):
                back(u, CHUNKS - 1, 1)

        @block.scalar
        def _(act):
            a = nc.scalar
            act.preload_act_table_set("natural_log_exp_and_others")
            act.wait_ge(s_weights, 16 * len(MAMBA_WEIGHTS))
            a.activation(negA[:, :], w["A_log"][:, :], ACT.Exp).then_inc(s_neg, 1)
            act.wait_ge(s_neg, 1)
            a.activation(negA[:, :], negA[:, :], ACT.Copy, scale=-1.0).then_inc(s_neg, 1)
            act.wait_ge(s_neg, 2)

            def squares(side, rows, before):
                for t in range(CT):
                    wait(act, s_sq, before + t)
                    a.activation(sq[:, :], rows[:, t, :], ACT.Square, accum_out=ssq[:, side, t:t + 1]).then_inc(s_sq, 1)

            def front(u, c, q):
                if u == 4:
                    act.wait_ge(s_ln, CT * (c + 1))
                    squares(0, hrow, squares_before(0, c))
                if u == 12:
                    for d in range(DC):
                        act.wait_ge(s_fullF[d], c * F_USES[d] + 1)
                        wait(act, s_fullF[1], c * F_USES[1])
                        a.activation(hT[:, d, :], pF[d][:, :], ACT.Copy, scale=w["norm1"][:, d:d + 1]).then_inc(s_hT, 1)
                for b in range(EB):
                    n = c * EB + b
                    if u == 16 + 4 * b:
                        act.wait_ge(s_fullF[1], c * F_USES[1] + 2 + b)
                        wait(act, s_z, n)
                        a.activation(eF[:, :], pF[1][:, :], ACT.Exp, scale=-1.0).then_inc(s_eF, 1)
                    if u == 17 + 4 * b:
                        act.wait_ge(s_eF, n + 1)
                        a.activation(eF[:, :], eF[:, :], ACT.Ln, bias=1.0).then_inc(s_lnF, 1)
                    if u == 18 + 4 * b:
                        act.wait_ge(s_lnF, n + 1)
                        a.activation(eF[:, :], eF[:, :], ACT.Exp, scale=-1.0).then_inc(s_sigF, 1)
                    if u == 36 + 4 * b:
                        act.wait_ge(s_fullF[1], c * F_USES[1] + 2 + EB + b)
                        wait(act, s_dt, n)
                        a.activation(ea[:, :], pF[1][:, :], ACT.Abs, bias=w["dt_b"][:, b:b + 1]).then_inc(s_ea0, 1)
                        a.activation(dt[:, q, b, :], pF[1][:, :], ACT.Relu, bias=w["dt_b"][:, b:b + 1]).then_inc(s_relu, 1)
                        act.wait_ge(s_ea0, n + 1)
                        a.activation(ea[:, :], ea[:, :], ACT.Exp, scale=-1.0).then_inc(s_ea, 1)
                    if u == 37 + 4 * b:
                        act.wait_ge(s_ea, n + 1)
                        act.wait_ge(s_relu, n + 1)
                        a.activation(el[:, :], ea[:, :], ACT.Ln, bias=1.0).then_inc(s_el, 1)
                        a.activation(eo[:, :], ea[:, :], ACT.Copy, bias=1.0).then_inc(s_eo0, 1)
                    if u == 38 + 4 * b:
                        act.wait_ge(s_eo0, n + 1)
                        a.activation(eo[:, :], eo[:, :], ACT.Copy, bias=-1.0).then_inc(s_eo, 1)
                if u == 35:
                    act.wait_ge(s_fullF[0], (c + 1) * F_USES[0])
                    wait(act, s_bt, 16 * c)
                    a.activation(Bt[:, :], pF[0][0:N, :], ACT.Copy).then_inc(s_Bt, 1)

            def back(u, c, q):
                if u == 17:
                    act.wait_ge(s_xa, 2 * (c + 1))
                    squares(1, xa, squares_before(1, c))
                if u == 23:
                    for d in range(DC):
                        act.wait_ge(s_fullK[d], c * K_USES + 2)
                        a.activation(hnT[:, d, :], pK[d][:, :], ACT.Copy, scale=w["norm2"][:, d:d + 1]).then_inc(s_hnT, 1)
                for b in range(FB):
                    m = P if b < FB - 1 else F_LAST
                    if u == 25 + 4 * b:
                        act.wait_ge(s_fullK[0], c * K_USES + 3 + b)
                        wait(act, s_gu, c * FB + b)
                        a.activation(eB[0:m, :], pK[0][0:m, :], ACT.Exp, scale=-1.0).then_inc(s_eB, 1)
                    if u == 26 + 4 * b:
                        act.wait_ge(s_eB, c * FB + b + 1)
                        a.activation(eB[0:m, :], eB[0:m, :], ACT.Ln, bias=1.0).then_inc(s_lnB, 1)
                    if u == 27 + 4 * b:
                        act.wait_ge(s_lnB, c * FB + b + 1)
                        a.activation(eB[0:m, :], eB[0:m, :], ACT.Exp, scale=-1.0).then_inc(s_sigB, 1)

            def decay(u, c, q):
                n, k, q, U = of(c, q, u)
                if k == 0:
                    act.wait_ge(s_dt, EB * (c + 1 + u // UNITS))
                wait(act, s_scan, U - A_BUFS + 1)
                a.activation(dA[:, u % A_BUFS, :], dt[:, q, k, :], ACT.Exp, scale=negA[:, k * N + n:k * N + n + 1]).then_inc(s_dA, 1)

            def keep_state(u, c):
                n, _, _, U = of(c, 0, u)
                act.wait_ge(s_scan, U + 1)
                a.activation(state[:, n, :], h[:, n % H_BUFS, :, CH - 1], ACT.Copy).then_inc(s_state, 1)

            def slots(c, q, has_front, has_back):
                for u in range(UNITS):
                    if u + AHEAD < UNITS or has_front:
                        decay(u + AHEAD, c, q)
                    kept = u - KEEP_LAG
                    if kept % EB == EB - 1 and (kept >= 0 or has_back):
                        keep_state(kept, c)
                    if has_front:
                        front(u, c + 1, 1 - q)
                    if has_back:
                        back(u, c - 1, 1 - q)
            for u in range(UNITS):
                front(u, 0, 0)
            for u in range(AHEAD):
                decay(u, 0, 0)
            chunks(act, slots)
            for u in range(UNITS):
                back(u, CHUNKS - 1, 1)

        @block.tensor
        def _(pe):
            t_ = nc.tensor

            def turn(bank, parts):
                for i, part in enumerate(parts):
                    last = t_.transpose(bank[:, i * P:(i + 1) * P], part, ident)
                return last

            def front(u, c, q):
                if u == 11:
                    pe.wait_ge(s_hrow, CT * (c + 1))
                    wait(pe, s_Bt, c)
                    wait(pe, s_ea0, EB * c)
                    wait(pe, s_relu, EB * c)
                    if not isinstance(c, int) or c > 1:
                        pe.wait_ge(s_ssm, EB * (c - 1))
                    for d in range(DC):
                        turn(pF[d], [hrow[:, t, d * P:(d + 1) * P] for t in range(CT)]).then_inc(s_fullF[d], 1)
                for b in range(EB):
                    for bank, name in ((0, "in_w"), (1, "gate_w")):
                        if u == 13 + 4 * b + 2 * bank:
                            pe.wait_ge(s_hT, DC * (c + 1))
                            wait(pe, (s_z, s_eF)[bank], c * EB + b)
                            for d in range(DC):
                                last = t_.matmul(pF[bank][:, :], w[name][:, d, b * P:(b + 1) * P], hT[:, d, :],
                                                 start=(d == 0), stop=(d == DC - 1))
                            last.then_inc(s_fullF[bank], 1)
                    for half in range(2):
                        if u == 33 + 4 * b + 2 * half:
                            if half == 0:
                                pe.wait_ge(s_z, EB * (c + 1))
                                pe.wait_ge(s_eF, EB * (c + 1))
                                wait(pe, s_ea0, c * EB + b)
                                wait(pe, s_relu, c * EB + b)
                            for d in range(half * EB // 2, (half + 1) * EB // 2):
                                last = t_.matmul(pF[1][:, :], w["dt_w"][:, d, b * P:(b + 1) * P], z[:, q, d, :],
                                                 start=(d == 0), stop=(d == EB - 1))
                            if half == 1:
                                last.then_inc(s_fullF[1], 1)
                if u == 32:
                    pe.wait_ge(s_z, EB * (c + 1))
                    for t in range(CT):
                        for d in range(EB):
                            last = t_.matmul(pF[0][:, t * N:(t + 1) * N], z[:, q, d, t * P:(t + 1) * P],
                                             w["bc_w"][:, d, N:2 * N], start=(d == 0), stop=(d == EB - 1))
                    last.then_inc(s_fullF[0], 1)
                if u == 34:
                    pe.wait_ge(s_C, c + 1)
                    for d in range(EB):
                        last = t_.matmul(pF[0][0:N, :], w["bc_w"][:, d, 0:N], z[:, q, d, :], start=(d == 0), stop=(d == EB - 1))
                    last.then_inc(s_fullF[0], 1)

            def back(u, c, q):
                if u == SUM_LAG:
                    pe.wait_ge(s_acc, UNITS * (c + 1))
                    wait(pe, s_x2, 2 * c)
                    fronts = min(c + 2, CHUNKS) if isinstance(c, int) else c + 2
                    pe.wait_ge(s_Bt, fronts)
                    pe.wait_ge(s_ea0, fronts * EB)
                    pe.wait_ge(s_relu, fronts * EB)
                    for b in range(EB):
                        last = turn(pY[b], [acc[:, t, b * P:(b + 1) * P] for t in range(CT)])
                    last.then_inc(s_yT, 1)
                for t in range(CT):
                    if u == SUM_LAG + 1 + EB + t:
                        pe.wait_ge(s_ssm, EB * (c + 1))
                        for d in range(EB):
                            last = t_.matmul(pK[t // 2][:, (t % 2) * D:(t % 2 + 1) * D], z[:, q, d, t * P:(t + 1) * P],
                                             w["out_w"][:, d, :], start=(d == 0), stop=(d == EB - 1))
                        if t % 2 == 1:
                            last.then_inc(s_fullK[t // 2], 1)
                if u == 22:
                    pe.wait_ge(s_hn, CT * (c + 1))
                    for d in range(DC):
                        turn(pK[d], [xa[:, t, d * P:(d + 1) * P] for t in range(CT)]).then_inc(s_fullK[d], 1)
                for b in range(FB):
                    m = P if b < FB - 1 else F_LAST
                    for bank, name in ((0, "fg_w"), (1, "fu_w")):
                        if u == 24 + 4 * b + 2 * bank:
                            pe.wait_ge(s_hnT, DC * (c + 1))
                            wait(pe, (s_gu, s_ff)[bank], c * FB + b)
                            for d in range(DC):
                                last = t_.matmul(pK[bank][0:m, :], w[name][:, d, b * P:b * P + m], hnT[:, d, :],
                                                 start=(d == 0), stop=(d == DC - 1))
                            last.then_inc(s_fullK[bank], 1)
                for t in range(CT):
                    for half in range(2):
                        if u == 50 + 3 * t + half:
                            pe.wait_ge(s_ff, FB * (c + 1))
                            for b in range(half * FB // 2, (half + 1) * FB // 2):
                                m = P if b < FB - 1 else F_LAST
                                rhs = w["fd_w"][:, b, :] if b < FB - 1 else w["fd_last"][:, :]
                                last = t_.matmul(pK[t // 2][:, (t % 2) * D:(t % 2 + 1) * D], ff[0:m, b, t * P:(t + 1) * P],
                                                 rhs, start=(b == 0), stop=(b == FB - 1))
                            if t % 2 == 1 and half == 1:
                                last.then_inc(s_fullK[t // 2], 1)

            def states(v, c):
                n, t, _, V = of(c, 0, v)
                pe.wait_ge(s_scan, V - t + EB)
                wait(pe, s_acc, V - HT_BANKS + 1)
                turn(pH[v % HT_BANKS], [h[:, n % H_BUFS, k, t * P:(t + 1) * P] for k in range(EB)]).then_inc(s_ht, 1)

            def slots(c, q, has_front, has_back):
                for u in range(UNITS):
                    if u >= TURN_LAG or has_back:
                        states(u - TURN_LAG, c)
                    if has_front:
                        front(u, c + 1, 1 - q)
                    if has_back:
                        back(u, c - 1, 1 - q)
            pe.wait_ge(s_weights, 16 * len(MAMBA_WEIGHTS))
            for u in range(UNITS):
                front(u, 0, 0)
            pe.wait_ge(s_ffn, 16 * len(FFN_WEIGHTS))
            chunks(pe, slots)
            for u in range(TURN_LAG):
                states(UNITS - TURN_LAG + u, CHUNKS - 1)
            for u in range(UNITS):
                back(u, CHUNKS - 1, 1)

        @block.vector
        def _(dve):
            v_ = nc.vector
            dve.wait_ge(s_weights, 16 * len(MAMBA_WEIGHTS))
            dve.wait_ge(s_init, 2)

            def mean_square(side, c):
                dve.wait_ge(s_sq, squares_before(side, c) + CT)
                v_.tensor_scalar(ms[:, side, :], ssq[:, side, :], 1.0 / D, RMS_EPS, ALU.mult, ALU.add).then_inc(s_ms[side], 1)

            def normalise(rows, s):
                for t in range(CT):
                    v_.tensor_scalar(rows[:, t, :], xf[:, t, :], mv[:, t, 0:1], rstd[:, t:t + 1],
                                     ALU.subtract, ALU.mult).then_inc(s, 1)

            def front(u, c, q):
                if u == 0:
                    dve.wait_ge(s_fld, 16 * (c + 1))
                    for t in range(CT):
                        v_.bn_stats(stats[:, t, :], xf[:, t, :]).then_inc(s_bns, 1)
                if u == 1:
                    for t in range(CT):
                        v_.bn_aggr(mv[:, t, :], stats[:, t, :]).then_inc(s_bna, 1)
                    dve.wait_ge(s_bna, CT * (c + 1))
                    v_.tensor_scalar(ve[:, :], mv[:, :, 1], LN_EPS, None, ALU.add).then_inc(s_ve, 1)
                if u == 3:
                    dve.wait_ge(s_rstd, c + 1)
                    wait(dve, s_hT, DC * c)
                    normalise(hrow, s_ln)
                if u == 6:
                    mean_square(0, c)
                if u == 8:
                    dve.wait_ge(s_rr[0], c + 1)
                    for t in range(CT):
                        v_.tensor_scalar(hrow[:, t, :], hrow[:, t, :], rr[:, 0, t:t + 1], None, ALU.mult).then_inc(s_hrow, 1)
                if u == 17:
                    if not isinstance(c, int) or c > 1:
                        dve.wait_ge(s_xa, 2 * (c - 1))
                    normalise(yln[:, q], s_y)
                for b in range(EB):
                    if u == 19 + 4 * b:
                        dve.wait_ge(s_sigF, c * EB + b + 1)
                        dve.wait_ge(s_fullF[0], c * F_USES[0] + 2 + b)
                        v_.tensor_tensor(z[:, q, b, :], eF[:, :], pF[0][:, :], ALU.mult).then_inc(s_z, 1)
                if u == 33:
                    dve.wait_ge(s_fullF[0], (c + 1) * F_USES[0] - 1)
                    v_.tensor_copy(C[:, q, :, :], pF[0][:, 0:CT * N].rearrange("p (t n) -> p t n", t=CT)).then_inc(s_C, 1)

            def back(u, c, q):
                for i, b in enumerate((2, 3, 0, 1)):
                    if u == SUM_LAG + 1 + i:
                        dve.wait_ge(s_yT, c + 1)
                        v_.scalar_tensor_tensor(z[:, q, b, :], z[:, q, b, :], w["Dp"][:, b:b + 1], pY[b][:, :],
                                                op0=ALU.mult, op1=ALU.add).then_inc(s_ssm, 1)
                for i in range(2):
                    if u == 14 + 2 * i:
                        dve.wait_ge(s_fullK[i], c * K_USES + 1)
                        v_.tensor_tensor(xa[:, 2 * i:2 * i + 2, :], yln[:, q, 2 * i:2 * i + 2, :],
                                         pK[i][:, :].rearrange("p (t d) -> p t d", t=2), ALU.add).then_inc(s_xa, 1)
                    if u == 57 + 6 * i:
                        dve.wait_ge(s_fullK[i], c * K_USES + 3 + FB)
                        v_.tensor_tensor(xb[:, 2 * i:2 * i + 2, :], xb[:, 2 * i:2 * i + 2, :],
                                         pK[i][:, :].rearrange("p (t d) -> p t d", t=2), ALU.add).then_inc(s_x2, 1)
                if u == 19:
                    mean_square(1, c)
                if u == 21:
                    dve.wait_ge(s_rr[1], c + 1)
                    dve.wait_ge(s_base, 2 * (c + 1))
                    for t in range(CT):
                        v_.tensor_scalar(xa[:, t, :], xa[:, t, :], rr[:, 1, t:t + 1], None, ALU.mult).then_inc(s_hn, 1)
                for b in range(FB):
                    if u == 28 + 4 * b:
                        m = P if b < FB - 1 else F_LAST
                        n = c * FB + b + 1
                        dve.wait_ge(s_sigB, n)
                        v_.tensor_tensor(ff[0:m, b, :], eB[0:m, :], pK[0][0:m, :], ALU.mult).then_inc(s_gu, 1)
                        dve.wait_ge(s_gu, n)
                        dve.wait_ge(s_fullK[1], c * K_USES + 3 + b)
                        v_.tensor_tensor(ff[0:m, b, :], ff[0:m, b, :], pK[1][0:m, :], ALU.mult).then_inc(s_ff, 1)

            def scan(u, c, q):
                n, k, _, U = of(c, q, u)
                dve.wait_ge(s_dA, U + 1)
                dve.wait_ge(s_dB, U + 1)
                wait(dve, s_state, c * N + n - H_BUFS + 1)
                wait(dve, s_ht, (c * N + n - H_BUFS + 1) * CT)
                v_.tensor_tensor_scan(h[:, n % H_BUFS, k, :], dA[:, u % A_BUFS, :], dB[:, u % B_BUFS, :],
                                      initial=state[:, n, k:k + 1], op0=ALU.mult, op1=ALU.add).then_inc(s_scan, 1)

            def weigh(v, c, q):
                n, t, q, V = of(c, q, v)
                dve.wait_ge(s_ht, V + 1)
                C_n = C[:, q, t, n:n + 1]
                if n == 0:
                    wait(dve, s_yT, c)
                    v_.tensor_scalar(acc[:, t, :], pH[v % HT_BANKS][:, :], C_n, None, ALU.mult).then_inc(s_acc, 1)
                else:
                    dve.wait_ge(s_acc, V - CT + 1)
                    v_.scalar_tensor_tensor(acc[:, t, :], pH[v % HT_BANKS][:, :], C_n, acc[:, t, :],
                                            op0=ALU.mult, op1=ALU.add).then_inc(s_acc, 1)

            def slots(c, q, has_front, has_back):
                for u in range(UNITS):
                    if has_front and u == 1:
                        dve.wait_ge(s_bns, CT * (c + 2))
                        dve.wait_ge(s_y, CT * (c + 1))
                    scan(u, c, q)
                    if has_back:
                        back(u, c - 1, 1 - q)
                    if u >= SUM_LAG or has_back:
                        weigh(u - SUM_LAG, c, q)
                    if has_front:
                        front(u, c + 1, 1 - q)
            for u in range(UNITS):
                if u == 1:
                    dve.wait_ge(s_bns, CT)
                front(u, 0, 0)
            chunks(dve, slots)
            for u in range(SUM_LAG):
                weigh(UNITS - SUM_LAG + u, CHUNKS - 1, 1)
            for u in range(UNITS):
                back(u, CHUNKS - 1, 1)


def macaron(nc, x, moe_w, router, bias, consts, *rest):
    out = rest[-1]
    mamba_w = dict(zip([*MAMBA_WEIGHTS, *FFN_WEIGHTS], rest))
    moe_weights = {"moe": moe_w, "router": router, "bias": bias}
    x1 = nc.dram_tensor("x1", (T + P, D), F32, kind="Internal").ap()
    x2 = nc.dram_tensor("x2", (T, D), F32, kind="Internal").ap()
    x3 = nc.dram_tensor("x3", (T + P, D), F32, kind="Internal").ap()
    normed_a, normed_c = (nc.dram_tensor(f"normed_{n}", (T + P, D), F32, kind="Internal").ap() for n in "ac")
    slots_a, slots_c = (nc.dram_tensor(f"slots_{n}", (SLOTS, ENTRY), F32, kind="Internal").ap() for n in "ac")
    b_rows = nc.dram_tensor("b_rows", (CHUNKS * N, CH), F32, kind="Internal").ap()
    with ExitStack() as ctx:
        const = ctx.enter_context(nc.sbuf_tensor("const", [P, CONSTS], F32))
        w = {n: ctx.enter_context(nc.sbuf_tensor(f"w_{n}", s, F32)) for n, s in MAMBA_WEIGHTS.items()}
        s_weights = ctx.enter_context(nc.semaphore("weights"))
        s_out = ctx.enter_context(nc.semaphore("out"))
        with nc.sbuf_tensor("Wa", [P, E + 1, EXPERT], F32) as W:
            moe(nc, "a", x, x1, normed_a, slots_a, moe_weights, consts, const, W,
                [(w[n][:], mamba_w[n], s_weights) for n in MAMBA_WEIGHTS])
        mamba(nc, x1, x2, b_rows, w, mamba_w, const, s_weights)
        with nc.sbuf_tensor("Wc", [P, E + 1, EXPERT], F32) as W:
            moe(nc, "c", x2, x3, normed_c, slots_c, moe_weights, consts, const, W)
        with nc.Block() as block:
            @block.sync
            def _(sp):
                sp.dma_start(out, x3[0:T, :]).then_inc(s_out, 16)
                sp.wait_ge(s_out, 16)


def layout(z):
    def blocks(w):
        return np.ascontiguousarray(w.reshape(w.shape[0] // P, P, -1).transpose(1, 0, 2))

    def turned(name):
        return np.ascontiguousarray(z[name].T)

    def expert(w1, w3, w2):
        return np.concatenate([blocks(w).reshape(P, -1) for w in (w1, w3, w2)], axis=1)
    f, a = "L0_ffn_", "L0_attn_"
    experts = [expert(z[f + "w1"][e], z[f + "w3"][e], z[f + "w2"][e]) for e in range(E)]
    experts.append(expert(z[f + "sw1"][0], z[f + "sw3"][0], z[f + "sw2"][0]))
    down = turned(a + "ffn_down_w")
    whole = (FB - 1) * P
    return {
        "x": z[a + "x"].reshape(T, D),
        "moe": np.stack(experts),
        "router": blocks(turned(f + "router_w")),
        "bias": z[f + "experts_bias"],
        "consts": constants(),
        "in_w": blocks(turned(a + "in_proj_w")),
        "gate_w": blocks(turned(a + "gate_proj_w")),
        "dt_w": blocks(turned(a + "dt_w")),
        "bc_w": blocks(turned(a + "x_proj_w")),
        "out_w": blocks(turned(a + "out_proj_w")),
        "norm1": z[a + "norm1_w"].reshape(DC, P).T,
        "norm2": z[a + "ffn_norm_w"].reshape(DC, P).T,
        "dt_b": z[a + "dt_b"].reshape(EB, P).T,
        "A_log": blocks(z[a + "A_log"]).reshape(P, EB * N),
        "Dp": z[a + "Dp"].reshape(EB, P).T,
        "fg_w": blocks(turned(a + "ffn_gate_w")),
        "fu_w": blocks(turned(a + "ffn_up_w")),
        "fd_w": blocks(down[:whole]),
        "fd_last": down[whole:],
    }


def kernel(**inputs):
    import concourse.bacc as _bacc
    from concourse.bass_utils import run_bass_kernel_spmd as _run

    nc = _bacc.Bacc("TRN2", target_bir_lowering=False, num_devices=1)
    arrays = {name: np.ascontiguousarray(a) for name, a in layout({n: np.asarray(v) for n, v in inputs.items()}).items()}
    args = [nc.dram_tensor(name, a.shape, mybir.dt.from_np(a.dtype), kind="ExternalInput").ap() for name, a in arrays.items()]
    args.append(nc.dram_tensor("out", (T, D), F32, kind="ExternalOutput").ap())
    macaron(nc, *args)
    r = _run(nc, [arrays], core_ids=[0])
    return r.results[0]["out"].reshape(1, T, D)
```

```python
from contextlib import ExitStack, contextmanager

import numpy as np

import concourse.bass as bass
from concourse import mybir

F32 = mybir.dt.float32
I32 = mybir.dt.int32
ALU = mybir.AluOpType
ACT = mybir.ActivationFunctionType
X = mybir.AxisListType.X

P = 128
T = 4096
D = 256
DC = D // P
TT = T // P

E = 8
K = 2
H = 512
HC = H // P
SHARED = E
UP = DC * H
EXPERT = 2 * UP + HC * D
SLOT_TILES = K * T // P + E - 1
SLOTS = SLOT_TILES * P
ENTRY = 2
ID, WEIGHT = 0, 1
LN_EPS = 1e-5
RMS_EPS = 1e-6
RG = 2
GROUPS = TT // RG
LAG = 4
SG = 4
SGROUPS = TT // SG
ROUTING_GROUPS = 4
ROUTING = {(0, 1): 0, (0, 3): 1, (1, 1): 3, (1, 2): 4, (1, 3): 5, (2, 1): 6, (2, 2): 7}
PREFIX_GROUP = EXP_GROUP = 1
EARLY = {"pe": {3: 0, 5: 1, 7: 2, 9: 3}, "act": {4: 0, 6: 1, 8: 2, 10: 3}, "dve": {5: 0, 7: 1, 9: 2, 11: 3}}
EARLY_GROUPS = 12

C_IDENT = 0
C_TRI = C_IDENT + P
C_ONES = C_TRI + P
C_TOKEN = C_ONES + P
C_START = C_TOKEN + TT
C_TILE = C_START + TT
C_RANK = C_TILE + SLOT_TILES
C_FILL = C_RANK + E
C_ZERO = C_FILL + ENTRY
CONSTS = C_ZERO + D


def constants():
    c = np.zeros((P, CONSTS), np.float32)
    p = np.arange(P)
    c[:, C_IDENT:C_IDENT + P] = np.eye(P)
    c[:, C_TRI:C_TRI + P] = p[:, None] < p[None, :]
    c[:, C_ONES:C_ONES + P] = 1.0
    c[:, C_TOKEN:C_TOKEN + TT] = np.arange(TT)[None, :] * P + p[:, None]
    c[:, C_START:C_START + TT] = np.arange(TT) * P
    c[:, C_TILE:C_TILE + SLOT_TILES] = np.arange(SLOT_TILES)
    c[:, C_RANK:C_RANK + E] = E - np.arange(E)
    c[:, C_FILL + ID] = T + p
    return c


def wait(eng, sem, value):
    if not isinstance(value, int) or value > 0:
        eng.wait_ge(sem, value)


@contextmanager
def phase(nc):
    sems = []

    def new(name):
        sems.append(nc.alloc_semaphore(name=name))
        return sems[-1]
    yield new
    nc.clear_and_free_semaphores(sems)
    nc.all_engine_barrier()


def moe(nc, tag, src, dst, normed, slots, weights, consts, const, W, later=()):
    ident = const[:, C_IDENT:C_IDENT + P]
    ones = const[:, C_ONES:C_ONES + P]
    src_g = src[0:T, :].rearrange("(g t p) d -> g p t d", t=RG, p=P)
    dst_t = dst.rearrange("(t p) d -> t p d", p=P)
    dst_g = dst[0:T, :].rearrange("(g t p) d -> g p t d", t=2, p=P)
    normed_t = normed.rearrange("(t p) d -> t p d", p=P)
    normed_g = normed[0:T, :].rearrange("(g t p) d -> g p t d", t=RG, p=P)
    slots_p = slots.rearrange("(p t) d -> p t d", t=SLOT_TILES)

    with phase(nc) as new, ExitStack() as ctx:
        def sb(name, shape, dt=F32):
            return ctx.enter_context(nc.sbuf_tensor(f"{tag}_{name}", shape, dt))

        def pb(name):
            return ctx.enter_context(nc.psum_tensor(f"{tag}_{name}", [P, 512], F32))

        def sem(name):
            return new(f"{tag}_{name}")

        bias = sb("bias", [P, E])
        router = sb("router", [P, DC, E])
        x_all = sb("x_all", [P, TT, D])
        entries = sb("entries", [P, K, TT, ENTRY])
        xnb = sb("xnb", [P, 2, RG, D])
        xTr = sb("xTr", [P, 2, DC, RG * P])
        stats = sb("stats", [P, 2, RG, 6])
        mv = sb("mv", [P, 2, RG, 2])
        ve = sb("ve", [P, 2, RG])
        rstd = sb("rstd", [P, 2, RG])
        nhalf = sb("nhalf", [P, RG])
        L = sb("L", [P, TT, E])
        scratch = sb("scratch", [P, TT, E])
        oh1 = sb("oh1", [P, TT, E])
        oh2 = sb("oh2", [P, TT, E])
        incl = sb("incl", [P, TT, E])
        cmp = sb("cmp", [P, E, TT])
        m1 = sb("m1", [P, TT])
        m2 = sb("m2", [P, TT])
        r1 = sb("r1", [P, TT])
        ex = sb("ex", [P, TT])
        w0 = sb("w0", [P, TT])
        w1 = sb("w1", [P, TT])
        posf = sb("posf", [P, 2, TT])
        slot = sb("slot", [P, 2, TT], I32)
        slot_tile = sb("slot_tile", [P, 2, TT], I32)
        pos = sb("pos", [P, 2, TT], I32)
        tiles = sb("tiles", [P, E])
        tend = sb("tend", [P, E])
        base = sb("base", [P, E])
        tile_cmp = sb("tile_cmp", [1, SLOT_TILES, E])
        tile_sum = sb("tile_sum", [1, SLOT_TILES])
        tile_expert = sb("tile_expert", [1, SLOT_TILES], I32)
        slot_info = sb("slot_info", [P, SLOT_TILES, ENTRY])
        slot_ids = sb("slot_ids", [P, SLOT_TILES], I32)
        xs = sb("xs", [P, 2, D])
        xT = sb("xT", [P, DC * P])
        hidden = sb("hidden", [P, HC, SG * P])
        ys2 = sb("ys2", [P, 2, 2, D])
        sg = sb("sg", [P, H])
        hs = sb("hs", [P, H])
        hT = sb("hT", [P, HC * P])
        ys = sb("ys", [P, 2, D])

        pX = pb("pX")
        pL = pb("pL")
        pG = pb("pG")
        pU = pb("pU")
        pH = pb("pH")
        pY = pb("pY")
        pC = pb("pC")
        pV = pb("pV")

        s_const = sem("const")
        s_bias = sem("bias")
        s_w = [sem(f"w{e}") for e in range(E + 1)]
        s_fill = sem("fill")
        s_spare = sem("spare")
        s_xin = [sem(f"xin{q}") for q in range(2)]
        s_nhalf = sem("nhalf")
        s_bns = sem("bns")
        s_bna = sem("bna")
        s_ve = sem("ve")
        s_rs = sem("rs")
        s_norm = sem("norm")
        s_tr = sem("tr")
        s_xTr = sem("xTr")
        s_xTa = sem("xTa")
        s_lg = sem("lg")
        s_L = sem("L")
        s_kept = [sem(f"kept{q}") for q in range(2)]
        s_zeros = sem("zeros")
        s_chain = sem("chain")
        s_diff = sem("diff")
        s_ex = sem("ex")
        s_oh = sem("oh")
        s_prefix = sem("prefix")
        s_pos = sem("pos")
        s_map = sem("map")
        s_entry = sem("entry")
        s_info = sem("info")
        s_ids = sem("ids")
        s_scat = sem("scat")
        s_sent = sem("sent")

        block = ctx.enter_context(nc.Block())

        Wf = W[:, :, :].rearrange("p e n -> p (e n)")
        IN_ROOM = -(-DC * T // EXPERT)
        ROOM = (E - IN_ROOM) * EXPERT

        def x_half(g, q, c):
            return Wf[:, bass.ds((g - q) * (DC * RG * P) + (ROOM + (c * SG + q * RG) * P), RG * P)]

        def x_turned(g, c, at, n):
            return Wf[:, bass.ds(g * (DC * SG * P) + (ROOM + c * SG * P + at), n)]

        S = {n: sem(f"s_{n}") for n in ("g", "u", "sg", "h", "y", "ys")}
        S["store"] = [sem(f"s_store{q}") for q in range(2)]
        R = {n: sem(f"r_{n}") for n in ("xt", "xT", "g", "u", "sg", "h", "ht", "hT", "y", "ys")}
        R["load"] = [sem(f"r_load{q}") for q in range(2)]
        s_add = sem("add")

        def over_tiles(eng, n, step, head=2):
            for i in range(head):
                step(i, i % 2)
            pairs = (n - 1 - head) // 2
            with eng.Fori(head // 2, head // 2 + pairs) as j:
                step(j * 2, 0)
                step(j * 2 + 1, 1)
            for i in range(head + 2 * pairs, n):
                step(i, i % 2)

        def gate_up(b):
            return ((pG, pU), (pH, pV))[b % 2]

        @block.sync
        def _(sp):
            sp.dma_start(const[:, :], consts).then_inc(s_const, 16)
            sp.dma_start(router[:, :, :], weights["router"]).then_inc(s_bias, 16)
            sp.dma_start(bias[:, :], weights["bias"].partition_broadcast(P)).then_inc(s_bias, 16)

            def load_group(g, q):
                wait(sp, s_xin[q], (g - q) * 8)
                sp.dma_start(x_all[:, bass.ds(g * RG, RG), :], src_g[bass.ds(g, 1)].rearrange("a p t d -> p (a t) d")).then_inc(s_xin[q], 16)

            def keep_group(g, q):
                sp.wait_ge(s_norm, RG * (g + 1))
                sp.dma_start(normed_g[bass.ds(g, 1)].rearrange("a p t d -> p (a t) d"), xnb[:, q, :, :]).then_inc(s_kept[q], 16)
            load_group(0, 0)
            load_group(1, 1)
            load_group(2, 0)
            load_group(3, 1)
            sp.dma_start(W[:, SHARED, :], weights["moe"][SHARED]).then_inc(s_w[SHARED], 16)
            with sp.Fori(0, GROUPS // 2 - 2) as j:
                keep_group(j * 2, 0)
                load_group(j * 2 + 4, 0)
                keep_group(j * 2 + 1, 1)
                load_group(j * 2 + 5, 1)
            for g in range(GROUPS - 4, GROUPS):
                keep_group(g, g % 2)
            def shared_load(i, q):
                wait(sp, S["xt"], i - 1)
                sp.dma_start(xs[:, q, :], normed_t[bass.ds(i, 1)].rearrange("a p d -> p (a d)")).then_inc(S["load"][q], 16)

            def shared_store(i, q):
                sp.wait_ge(S["ys"], i + 1)
                sp.dma_start(dst_t[bass.ds(i, 1)].rearrange("a p d -> p (a d)"), ys[:, q, :]).then_inc(S["store"][q], 16)
            for q in range(2):
                sp.wait_ge(s_kept[q], 8 * GROUPS)

            def load_expert(e):
                sp.dma_start(W[:, e, :], weights["moe"][e]).then_inc(s_w[e], 16)

            for i in range(2 * SGROUPS):
                if i % 2 == 0 and i // 2 < E - IN_ROOM:
                    load_expert(i // 2)
                sp.wait_ge(S["ys"], i + 1)
                sp.dma_start(dst_g[i], ys2[:, i % 2, :, :]).then_inc(S["store"][i % 2], 16)
                for e in range(E - IN_ROOM, E):
                    g = min((e + 1 - E + IN_ROOM) * EXPERT // (DC * SG * P), SGROUPS) - 1
                    if i == min(2 * g + 1, 2 * SGROUPS - 3):
                        sp.wait_ge(S["u"], HC * (g + 1))
                        load_expert(e)
            for to, from_, s in later:
                sp.dma_start(to, from_).then_inc(s, 16)

        @block.gpsimd
        def _(pool):
            pool.memset(nhalf[:, :], -0.5).then_inc(s_nhalf, 1)
            pool.wait_ge(s_nhalf, 1)

            def group(g, q):
                pool.wait_ge(s_ve, g + 1)
                nc.gpsimd.tensor_tensor(rstd[:, q, :], ve[:, q, :], nhalf[:, :], ALU.pow).then_inc(s_rs, 1)
            over_tiles(pool, GROUPS, group)
            pool.wait_ge(s_const, 16)
            for k in range(K):
                nc.gpsimd.tensor_copy(entries[:, k, :, ID:ID + 1], const[:, C_TOKEN:C_TOKEN + TT].unsqueeze(2)).then_inc(s_entry, 1)
            pool.wait_ge(s_pos, 1)
            for k in range(K):
                nc.gpsimd.tensor_copy(entries[:, k, :, WEIGHT:WEIGHT + 1], (w0, w1)[k][:, :].unsqueeze(2)).then_inc(s_entry, 1)
            pool.wait_ge(s_entry, 2 * K)
            pool.wait_ge(s_fill, 16)
            for k in range(K):
                for t in range(TT):
                    nc.gpsimd.indirect_dma_start(
                        out=slots, out_offset=bass.IndirectOffsetOnAxis(ap=pos[:, k, t:t + 1], axis=0),
                        in_=entries[:, k, t, :], in_offset=None).then_inc(s_scat, 16)
            pool.wait_ge(s_scat, 16 * TT * K)
            nc.gpsimd.memset(nhalf[:, 0:1], 0.0).then_inc(s_sent, 1)

            def gather(i):
                nc.gpsimd.indirect_dma_start(
                    out=xs[:, i % 2, :], out_offset=None, in_=normed,
                    in_offset=bass.IndirectOffsetOnAxis(ap=slot_ids[:, i:i + 1], axis=0)).then_inc(R["load"][i % 2], 16)

            def add(i):
                wait(pool, s_add, 16 * i)
                pool.wait_ge(R["ys"], i + 1)
                nc.gpsimd.indirect_dma_start(
                    out=dst, out_offset=bass.IndirectOffsetOnAxis(ap=slot_ids[:, i:i + 1], axis=0),
                    in_=ys[:, i % 2, :], in_offset=None, compute_op=ALU.add).then_inc(s_add, 16)

            pool.wait_ge(s_ids, 1)
            pool.wait_ge(s_zeros, 16)
            for q in range(2):
                pool.wait_ge(s_kept[q], 8 * GROUPS)
            for i in range(SLOT_TILES + LAG):
                if i < SLOT_TILES:
                    wait(pool, R["xt"], i - 1)
                    gather(i)
                if i == LAG:
                    for q in range(2):
                        pool.wait_ge(S["store"][q], 16 * SGROUPS)
                    pool.wait_ge(s_spare, 16)
                if i >= LAG:
                    add(i - LAG)
            pool.wait_ge(s_add, 16 * SLOT_TILES)

        @block.scalar
        def _(act):

            def shared_silu(g, b):
                n = g * HC + b
                act.wait_ge(S["g"], n + 1)
                wait(act, S["h"], n)
                nc.scalar.activation(sg[:, :], gate_up(b)[0][:, :], ACT.Silu).then_inc(S["sg"], 1)

            def group(g, q):
                act.wait_ge(s_tr, g + 1)
                wait(act, s_lg, g - 1)
                nc.scalar.activation(xTr[:, q, :, :].rearrange("p c n -> p (c n)"), (pX, pC)[q][:, :], ACT.Copy).then_inc(s_xTr, 1)
                for c in range(DC):
                    last = nc.scalar.activation(x_half(g, q, c), (pX, pC)[q][:, c * RG * P:(c + 1) * RG * P], ACT.Copy)
                    last.then_inc(s_xTa, 1)
                if isinstance(g, int) and g in EARLY["act"]:
                    shared_silu(0, EARLY["act"][g])
            over_tiles(act, GROUPS, group, EARLY_GROUPS)
            act.wait_ge(s_const, 16)
            act.dma_start(slots_p,
                          const[:, C_FILL:C_FILL + ENTRY].unsqueeze(1).broadcast_to([P, SLOT_TILES, ENTRY])).then_inc(s_fill, 16)
            act.dma_start(dst_t[TT], const[:, C_ZERO:C_ZERO + D]).then_inc(s_spare, 16)
            act.dma_start(normed_t[TT], const[:, C_ZERO:C_ZERO + D]).then_inc(s_zeros, 16)

            def silu_and_hT(Q, i):
                act.wait_ge(Q["g"], i + 1)
                wait(act, Q["h"], i)
                nc.scalar.activation(sg[:, :], pG[:, :], ACT.Silu).then_inc(Q["sg"], 1)
                act.wait_ge(Q["ht"], i + 1)
                nc.scalar.activation(hT[:, :], pH[:, :], ACT.Copy).then_inc(Q["hT"], 1)

            def shared(g, q):
                for b in range(HC):
                    if not isinstance(g, int) or g > 0:
                        shared_silu(g, b)
                if isinstance(g, int) and g == EXP_GROUP:
                    act.wait_ge(s_diff, 1)
                    nc.scalar.activation(ex[:, :], r1[:, :], ACT.Exp).then_inc(s_ex, 1)
            over_tiles(act, SGROUPS, shared, ROUTING_GROUPS)
            act.wait_ge(s_sent, 1)
            act.dma_start(slot_info[:, :, :], slots_p).then_inc(s_info, 16)
            over_tiles(act, SLOT_TILES, lambda i, q: silu_and_hT(R, i))

        @block.tensor
        def _(pe):
            pe.wait_ge(s_const, 16)
            pe.wait_ge(s_bias, 32)

            def logits(g, q):
                pe.wait_ge(s_xTr, g + 1)
                for t in range(RG):
                    for c in range(DC):
                        last = nc.tensor.matmul(pL[:, bass.ds((g * RG + t) * E, E)], xTr[:, q, c, t * P:(t + 1) * P],
                                                router[:, c, :], start=(c == 0), stop=(c == DC - 1))
                last.then_inc(s_lg, 1)

            def shared_up(g, b):
                wait(pe, S["h"], g * HC + b - 1)
                for bank, at, s in zip(gate_up(b), (0, UP), ("g", "u")):
                    for c in range(DC):
                        at_c = at + c * H + b * P
                        last = nc.tensor.matmul(bank[:, :], W[:, SHARED, at_c:at_c + P], x_turned(g, c, 0, SG * P),
                                                start=(c == 0), stop=(c == DC - 1))
                    last.then_inc(S[s], 1)

            def group(g, q):
                pe.wait_ge(s_norm, RG * (g + 1))
                wait(pe, s_xTa, DC * (g - 1))
                for c in range(DC):
                    for t in range(RG):
                        last = nc.tensor.transpose((pX, pC)[q][:, (c * RG + t) * P:(c * RG + t + 1) * P],
                                                   xnb[:, q, t, c * P:(c + 1) * P], ident)
                last.then_inc(s_tr, 1)
                if not isinstance(g, int) or g > 0:
                    logits(g - 1, 1 - q)
                if isinstance(g, int) and g in EARLY["pe"]:
                    if EARLY["pe"][g] == 0:
                        pe.wait_ge(s_w[SHARED], 16)
                        pe.wait_ge(s_xTa, DC * SG // RG)
                    shared_up(0, EARLY["pe"][g])
            over_tiles(pe, GROUPS, group, EARLY_GROUPS)
            logits(GROUPS - 1, (GROUPS - 1) % 2)

            def prefix():
                pe.wait_ge(s_oh, 1)
                chosen = scratch[:, :, :].rearrange("p t e -> p (t e)")
                nc.tensor.matmul(pL[:, 0:TT * E], const[:, C_TRI:C_TRI + P], chosen, start=True, stop=True)
                nc.tensor.matmul(pC[:, 0:TT * E], ones, chosen, start=True, stop=True).then_inc(s_prefix, 1)

            def expert(e, at, n):
                return Wf[:, bass.ds(e * EXPERT + at, n)]

            def turn_x(Q, q, ready, free):
                for s, v in ready:
                    pe.wait_ge(s, v)
                for s, v in free:
                    wait(pe, s, v)
                for c in range(DC):
                    last = nc.tensor.transpose(pX[:, c * P:(c + 1) * P], xs[:, q, c * P:(c + 1) * P], ident)
                last.then_inc(Q["xt"], 1)

            def up(Q, i, e):
                pe.wait_ge(Q["xT"], i + 1)
                wait(pe, Q["h"], i)
                for bank, at, s in ((pG, 0, "g"), (pU, UP, "u")):
                    for c in range(DC):
                        last = nc.tensor.matmul(bank[:, :], xT[:, c * P:(c + 1) * P], expert(e, at + c * H, H),
                                                start=(c == 0), stop=(c == DC - 1))
                    last.then_inc(Q[s], 1)

            def down(Q, i, e):
                pe.wait_ge(Q["hT"], i + 1)
                wait(pe, Q["ys"], i)
                for k in range(HC):
                    last = nc.tensor.matmul(pY[:, 0:D], hT[:, k * P:(k + 1) * P], expert(e, 2 * UP + k * D, D),
                                            start=(k == 0), stop=(k == HC - 1))
                last.then_inc(Q["y"], 1)

            def turn_h(Q, i):
                pe.wait_ge(Q["h"], i + 1)
                wait(pe, Q["hT"], i)
                for k in range(HC):
                    last = nc.tensor.transpose(pH[:, k * P:(k + 1) * P], hs[:, k * P:(k + 1) * P], ident)
                last.then_inc(Q["ht"], 1)

            pe.wait_ge(s_xTa, DC * GROUPS)

            def shared_down(g):
                pe.wait_ge(S["h"], HC * (g + 1))
                for half, bank in enumerate((pY, pX)):
                    wait(pe, S["ys"], g * 2 + half - 1)
                    for t in range(2):
                        at_t = (half * 2 + t) * P
                        for k in range(HC):
                            last = nc.tensor.matmul(bank[:, t * D:(t + 1) * D], hidden[:, k, at_t:at_t + P],
                                                    W[:, SHARED, 2 * UP + k * D:2 * UP + (k + 1) * D],
                                                    start=(k == 0), stop=(k == HC - 1))
                    last.then_inc(S["y"], 1)

            def shared(g, q):
                if isinstance(g, int) and g == 0:
                    return
                shared_up(g, 0)
                shared_down(g - 1)
                if isinstance(g, int) and g == PREFIX_GROUP:
                    prefix()
                for b in range(1, HC):
                    shared_up(g, b)
            over_tiles(pe, SGROUPS, shared, ROUTING_GROUPS)
            shared_down(SGROUPS - 1)

            for e in range(E):
                pe.wait_ge(s_w[e], 16)
            pe.wait_ge(s_map, 1)
            pe.wait_ge(S["ys"], 2 * SGROUPS)
            turn_x(R, 0, [(R["load"][0], 16)], [])

            def routed(i, q):
                e = pe.value_load(tile_expert[0:1, bass.ds(i, 1)], min_val=0, max_val=E - 1)
                up(R, i, e)
                if not isinstance(i, int) or i + 1 < SLOT_TILES:
                    n = (i + 1 - (1 - q)) * 8 + 16
                    turn_x(R, 1 - q, [(R["load"][1 - q], n)], [(R["xT"], i + 1)])
                if not isinstance(i, int) or i > 0:
                    before = pe.value_load(tile_expert[0:1, bass.ds(i - 1, 1)], min_val=0, max_val=E - 1)
                    down(R, i - 1, before)
                turn_h(R, i)
            over_tiles(pe, SLOT_TILES, routed)
            down(R, SLOT_TILES - 1, pe.value_load(tile_expert[0:1, SLOT_TILES - 1:SLOT_TILES], min_val=0, max_val=E - 1))

        @block.vector
        def _(dve):
            def statistics(g, q):
                for t in range(RG):
                    nc.vector.bn_stats(stats[:, q, t, :], x_all[:, bass.ds(g * RG + t, 1), :].rearrange("p a d -> p (a d)")).then_inc(s_bns, 1)

            def variance(g, q):
                for t in range(RG):
                    nc.vector.bn_aggr(mv[:, q, t, :], stats[:, q, t, :]).then_inc(s_bna, 1)
                dve.wait_ge(s_bna, RG * (g + 1))
                nc.vector.tensor_scalar(ve[:, q, :], mv[:, q, :, 1], LN_EPS, None, ALU.add).then_inc(s_ve, 1)

            def shared_gate(g, b):
                n = g * HC + b
                dve.wait_ge(S["sg"], n + 1)
                dve.wait_ge(S["u"], n + 1)
                wait(dve, S["y"], g * 2)
                nc.vector.tensor_tensor(hidden[:, b, :], sg[:, :], gate_up(b)[1][:, :], ALU.mult).then_inc(S["h"], 1)

            def ahead(g, by):
                return not isinstance(g, int) or g + by < GROUPS

            def group(g, q):
                if ahead(g, 2):
                    dve.wait_ge(s_xin[q], (g + 2 - q) * 8 + 16)
                if ahead(g, 1):
                    dve.wait_ge(s_bns, RG * (g + 2))
                dve.wait_ge(s_rs, g + 1)
                wait(dve, s_tr, g - 1)
                wait(dve, s_kept[q], (g - q) * 8)
                wait(dve, s_norm, RG * g)
                for t in range(RG):
                    nc.vector.tensor_scalar(xnb[:, q, t, :], x_all[:, bass.ds(g * RG + t, 1), :].rearrange("p a d -> p (a d)"),
                                            mv[:, q, t, 0:1], rstd[:, q, t:t + 1], ALU.subtract, ALU.mult).then_inc(s_norm, 1)
                if ahead(g, 1):
                    variance(g + 1, 1 - q)
                if ahead(g, 2):
                    statistics(g + 2, q)
                if isinstance(g, int) and g in EARLY["dve"]:
                    shared_gate(0, EARLY["dve"][g])
            for g in range(2):
                dve.wait_ge(s_xin[g], 16)
                statistics(g, g)
            dve.wait_ge(s_bns, RG)
            variance(0, 0)
            over_tiles(dve, GROUPS, group, EARLY_GROUPS)
            dve.wait_ge(s_bias, 32)
            dve.wait_ge(s_lg, GROUPS)
            nc.vector.tensor_tensor(L[:, :, :], pL[:, 0:TT * E].rearrange("p (t e) -> p t e", e=E),
                                    bias[:, :].unsqueeze(1).broadcast_to([P, TT, E]), ALU.add).then_inc(s_L, 1)
            dve.wait_ge(s_const, 16)

            chained = [0]

            def link(ins):
                chained[0] += 1
                ins.then_inc(s_chain, 1)
                dve.wait_ge(s_chain, chained[0])

            v = nc.vector
            total = pC[:, 0:TT * E].rearrange("p (t e) -> p t e", e=E)
            within = pL[:, 0:TT * E].rearrange("p (t e) -> p t e", e=E)

            def per_tile(a):
                return a.unsqueeze(2).broadcast_to([P, TT, E])

            def per_expert(a):
                return a.unsqueeze(1).broadcast_to([P, TT, E])
            rank = per_expert(const[:, C_RANK:C_RANK + E])

            def first_of_max(m, onehot):
                link(v.tensor_reduce(m[:, :], L[:, :, :], X, ALU.max))
                link(v.tensor_tensor(scratch[:, :, :], L[:, :, :], per_tile(m[:, :]), ALU.is_equal))
                link(v.tensor_tensor(scratch[:, :, :], scratch[:, :, :], rank, ALU.mult))
                link(v.tensor_reduce(r1[:, :], scratch[:, :, :], X, ALU.max))
                link(v.tensor_tensor(onehot[:, :, :], scratch[:, :, :], per_tile(r1[:, :]), ALU.is_equal))

            def slot_of(k, onehot):
                link(v.tensor_tensor(onehot[:, :, :], onehot[:, :, :], incl[:, :, :], ALU.mult))
                link(v.tensor_reduce(posf[:, k, :], onehot[:, :, :], X, ALU.add))

            def routing(step):
                if step == 0:
                    dve.wait_ge(s_L, 1)
                    first_of_max(m1, oh1)
                if step == 1:
                    link(v.scalar_tensor_tensor(L[:, :, :], oh1[:, :, :], -3e38, L[:, :, :], op0=ALU.mult, op1=ALU.add))
                    first_of_max(m2, oh2)
                    v.tensor_tensor(scratch[:, :, :], oh1[:, :, :], oh2[:, :, :], ALU.add).then_inc(s_oh, 1)
                    v.tensor_tensor(r1[:, :], m2[:, :], m1[:, :], ALU.subtract).then_inc(s_diff, 1)
                if step == 3:
                    dve.wait_ge(s_prefix, 1)
                    for e in range(E):
                        last = v.tensor_tensor_scan(incl[:, :, e], ones[:, 0:TT], total[:, :, e], initial=0.0, op0=ALU.mult, op1=ALU.add)
                        if e < E - 1:
                            last.then_inc(s_chain, 1)
                            chained[0] += 1
                    link(last)
                    count = incl[:, TT - 1, :]
                    link(v.tensor_tensor(cmp[:, :, :], count.unsqueeze(2).broadcast_to([P, E, TT]),
                                         const[:, C_START:C_START + TT].unsqueeze(1).broadcast_to([P, E, TT]), ALU.is_gt))
                    link(v.tensor_reduce(tiles[:, :], cmp[:, :, :], X, ALU.add))
                if step == 4:
                    link(v.tensor_tensor_scan(tend[:, :], ones[:, 0:E], tiles[:, :], initial=0.0, op0=ALU.mult, op1=ALU.add))
                    link(v.tensor_tensor(base[:, :], tend[:, :], tiles[:, :], ALU.subtract))
                    link(v.tensor_tensor(incl[:, :, :], incl[:, :, :], total, ALU.subtract))
                    link(v.tensor_tensor(incl[:, :, :], incl[:, :, :], within, ALU.add))
                    link(v.scalar_tensor_tensor(incl[:, :, :], per_expert(base[:, :]), float(P), incl[:, :, :], op0=ALU.mult, op1=ALU.add))
                if step == 5:
                    slot_of(0, oh1)
                    slot_of(1, oh2)
                    link(v.tensor_copy(slot[:, :, :], posf[:, :, :]))
                    link(v.tensor_scalar(slot_tile[:, :, :], slot[:, :, :], P.bit_length() - 1, None, ALU.logical_shift_right))
                    link(v.tensor_scalar(slot[:, :, :], slot[:, :, :], P - 1, None, ALU.bitwise_and))
                    link(v.scalar_tensor_tensor(pos[:, :, :], slot[:, :, :], float(SLOT_TILES), slot_tile[:, :, :],
                                                op0=ALU.mult, op1=ALU.add))
                if step == 6:
                    dve.wait_ge(s_ex, 1)
                    link(v.tensor_scalar(m1[:, :], ex[:, :], 1.0, None, ALU.add))
                    link(v.reciprocal(m2[:, :], m1[:, :]))
                    link(v.tensor_scalar(w0[:, :], m2[:, :], 0.5, None, ALU.mult))
                    v.tensor_tensor(w1[:, :], w0[:, :], ex[:, :], ALU.mult).then_inc(s_pos, 1)
                if step == 7:
                    link(v.tensor_tensor(tile_cmp[:, :, :], tend[0:1, :].unsqueeze(1).broadcast_to([1, SLOT_TILES, E]),
                                         const[0:1, C_TILE:C_TILE + SLOT_TILES].unsqueeze(2).broadcast_to([1, SLOT_TILES, E]), ALU.is_le))
                    link(v.tensor_reduce(tile_sum[:, :], tile_cmp[:, :, :], X, ALU.add))
                    v.tensor_scalar(tile_expert[:, :], tile_sum[:, :], float(E - 1), None, ALU.min).then_inc(s_map, 1)

            def take_x(Q, i):
                dve.wait_ge(Q["xt"], i + 1)
                nc.vector.tensor_copy(xT[:, :], pX[:, 0:DC * P]).then_inc(Q["xT"], 1)

            def gate(Q, i):
                dve.wait_ge(Q["sg"], i + 1)
                dve.wait_ge(Q["u"], i + 1)
                nc.vector.tensor_tensor(hs[:, :], sg[:, :], pU[:, :], ALU.mult).then_inc(Q["h"], 1)

            def shared_sum(g, half):
                n = g * 2 + half
                dve.wait_ge(S["y"], n + 1)
                wait(dve, S["store"][half], g * 16)
                nc.vector.scalar_tensor_tensor(
                    ys2[:, half, :, :].rearrange("p t d -> p (t d)"), (pY, pX)[half][:, :], 0.5,
                    x_all[:, bass.ds(g * SG + half * 2, 2), :].rearrange("p a d -> p (a d)"),
                    op0=ALU.mult, op1=ALU.add).then_inc(S["ys"], 1)

            def shared(g, q):
                for b in range(HC):
                    if not isinstance(g, int) or g > 0:
                        shared_gate(g, b)
                    if b == 0 and (not isinstance(g, int) or g > 0):
                        shared_sum(g - 1, 0)
                        shared_sum(g - 1, 1)
                    if isinstance(g, int) and (g, b) in ROUTING:
                        routing(ROUTING[g, b])
            over_tiles(dve, SGROUPS, shared, ROUTING_GROUPS)
            shared_sum(SGROUPS - 1, 0)
            shared_sum(SGROUPS - 1, 1)

            def weigh(i, q):
                dve.wait_ge(R["y"], i + 1)
                wait(dve, s_add, (i - 1) * 16)
                nc.vector.tensor_scalar(ys[:, q, :], pY[:, 0:D], slot_info[:, bass.ds(i, 1), WEIGHT], None, ALU.mult).then_inc(R["ys"], 1)

            dve.wait_ge(s_info, 16)
            nc.vector.tensor_copy(slot_ids[:, :], slot_info[:, :, ID]).then_inc(s_ids, 1)
            take_x(R, 0)

            def routed(i, q):
                gate(R, i)
                if not isinstance(i, int) or i + 1 < SLOT_TILES:
                    take_x(R, i + 1)
                if not isinstance(i, int) or i > 0:
                    weigh(i - 1, 1 - q)
            over_tiles(dve, SLOT_TILES, routed)
            weigh(SLOT_TILES - 1, (SLOT_TILES - 1) % 2)


DI = 512
EB = DI // P
N = 16
F = 704
FB = -(-F // P)
CH = 512
CT = CH // P
CHUNKS = T // CH
UNITS = N * EB
F_LAST = F - (FB - 1) * P
TURN_LAG, SUM_LAG, KEEP_LAG = 5, 7, 1
AT = {
    "statistics": 0, "variance": 1, "pow": 2, "layernorm": 3, "front_squares": 4, "front_mean": 7, "front_rms": 7,
    "front_row": 9, "front_turn": 14, "hT": 14, "gate": (16, 20, 24, 29), "in": (18, 22, 26, 31),
    "gate_exp": (18, 22, 26, 31), "gate_ln": (19, 23, 27, 32), "gate_sigmoid": (20, 24, 28, 33),
    "z": (21, 25, 29, 32), "residual": 20, "C": 37, "C_copy": 39, "B": 33, "B_copy": 35,
    "dt": (35, 37, 40, 42, 45, 48, 50, 53), "dt_exp": (39, 44, 50, 55), "dt_log": (40, 46, 51, 56),
    "dt_ln": (42, 47, 53, 58), "dt_low": (42, 47, 53, 58), "dt_sum": (43, 48, 54, 60), "dtz": (44, 49, 55, 60),
    "sum_turn": (5, 6, 7, 8), "ssm": (10, 11, 12, 13), "out": (14, 15, 16, 17), "xa": (18, 20),
    "back_squares": (21, 21), "base": (18, 20), "back_mean": 21, "back_rms": 21, "back_row": 24, "back_turn": 25,
    "hnT": 27, "ffn_gate_product": (29, 34, 39, 44, 49, 54), "ffn_up_product": (29, 36, 41, 46, 51, 56),
    "ffn_exp": (31, 36, 41, 46, 51, 56), "ffn_up_copy": (32, 37, 42, 47, 52, 57), "ffn_ln": (32, 37, 42, 47, 52, 57),
    "ffn_sigmoid": (33, 38, 43, 48, 53, 58), "ffn_gate": (33, 38, 43, 48, 53, 58),
    "ffn_product": (34, 39, 44, 49, 54, 59), "down": (60, 61, 62, 63, 64, 65, 66, 67), "x2": (65, 69),
}
END = max(AT["x2"]) + 1 - UNITS
AHEAD = 3
A_BUFS, B_BUFS, H_BUFS, HT_BANKS = 4, 4, 4, 4

MAMBA_WEIGHTS = {
    "in_w": [P, DC, DI], "gate_w": [P, DC, DI], "dt_w": [P, EB, DI], "bc_w": [P, EB, 2 * N],
    "out_w": [P, EB, D], "norm1": [P, DC], "norm2": [P, DC], "dt_b": [P, EB], "A_log": [P, EB * N], "Dp": [P, EB],
}
FFN_WEIGHTS = {"fg_w": [P, DC, F], "fu_w": [P, DC, F], "fd_w": [P, FB - 1, D], "fd_last": [F_LAST, D]}


def mamba(nc, src, dst, b_rows, w, ffn, const, s_weights):
    ident = const[:, C_IDENT:C_IDENT + P]
    src_c = src[0:T, :].rearrange("(c t p) d -> c p t d", t=CT, p=P)
    dst_c = dst[0:T, :].rearrange("(c t p) d -> c p t d", t=CT, p=P)

    with phase(nc) as new, ExitStack() as ctx:
        def sb(name, shape, dt=F32):
            return ctx.enter_context(nc.sbuf_tensor(f"b_{name}", shape, dt))

        def pb(name):
            return ctx.enter_context(nc.psum_tensor(f"b_{name}", [P, 512], F32))

        def sem(name):
            return new(f"b_{name}")

        w = dict(w, **{name: sb(name, shape) for name, shape in FFN_WEIGHTS.items()})
        xf = sb("xf", [P, CT, D])
        xb = sb("xb", [P, CT, D])
        yln = sb("yln", [P, 2, CT, D])
        hrow = sb("hrow", [P, CT, D])
        hT = sb("hT", [P, DC, CH])
        z = sb("z", [P, 2, EB, CH])
        dt = sb("dt", [P, 2, EB, CH])
        dtz = sb("dtz", [P, 2, EB, CH])
        C = sb("C", [P, 2, CT, N])
        Bt = sb("Bt", [2 * N, CH])
        Bn = sb("Bn", [P, 2, CH])
        acc = sb("acc", [P, CT, DI])
        xa = sb("xa", [P, CT, D])
        hnT = sb("hnT", [P, DC, CH])
        ff = sb("ff", [P, FB, CH])
        dA = sb("dA", [P, A_BUFS, CH])
        dB = sb("dB", [P, B_BUFS, CH])
        h = sb("h", [P, H_BUFS, EB, CH])
        eF = sb("eF", [P, CH])
        eB = sb("eB", [P, CH])
        ea = sb("ea", [P, CH])
        eo = sb("eo", [P, CH])
        el = sb("el", [P, CH])
        state = sb("state", [P, N, EB])
        negA = sb("negA", [P, EB * N])
        stats = sb("stats", [P, CT, 6])
        mv = sb("mv", [P, CT, 2])
        ve = sb("ve", [P, CT])
        rstd = sb("rstd", [P, CT])
        sq = sb("sq", [P, D])
        ssq = sb("ssq", [P, 2, CT])
        ms = sb("ms", [P, 2, CT])
        rr = sb("rr", [P, 2, CT])
        nhalf = sb("nhalf", [P, CT])

        pH = [pb(f"pH{i}") for i in range(HT_BANKS)]
        pF = [pb(f"pF{i}") for i in range(2)]
        pK = [pb(f"pK{i}") for i in range(2)]
        pY = [pK[0], pK[1], pF[0], pF[1]]
        def front_bank(i, b, alone):
            return pH[i] if alone and b % 2 else pF[i]

        def back_bank(i, b, alone):
            return pH[i] if alone and b % 2 else pK[i]

        F_USES = (3 + EB + EB // 2, 1 + EB + EB // 2)
        DT_BANK = [1 - b % 2 for b in range(EB)]
        K_USES = 3 + FB

        s_ffn = sem("ffn")
        s_fld = sem("fld")
        s_bld = sem("bld")
        s_stored = sem("stored")
        s_bt = sem("bt")
        s_Bn = [sem(f"Bn{i}") for i in range(2)]
        s_init = sem("init")
        s_neg = sem("neg")
        s_bns = sem("bns")
        s_bna = sem("bna")
        s_ve = sem("ve")
        s_rstd = sem("rstd")
        s_ln = sem("ln")
        s_y = sem("y")
        s_sq = sem("sq")
        s_ms = [sem(f"ms{i}") for i in range(2)]
        s_rr = [sem(f"rr{i}") for i in range(2)]
        s_hrow = sem("hrow")
        s_hT = sem("hT")
        s_eF = sem("eF")
        s_lnF = sem("lnF")
        s_sigF = sem("sigF")
        s_z = sem("z")
        s_C = sem("C")
        s_Bt = sem("Bt")
        s_relu = sem("relu")
        s_ea0 = sem("ea0")
        s_ea = sem("ea")
        s_eo = sem("eo")
        s_el = sem("el")
        s_log = sem("log")
        s_gain = sem("gain")
        s_dt = sem("dt")
        s_dtz = sem("dtz")
        s_fullF = [sem(f"fullF{i}") for i in range(2)]
        s_fullK = [sem(f"fullK{i}") for i in range(2)]
        s_yT = sem("yT")
        s_ssm = sem("ssm")
        s_xa = sem("xa")
        s_base = sem("base")
        s_hn = sem("hn")
        s_hnT = sem("hnT")
        s_eB = sem("eB")
        s_lnB = sem("lnB")
        s_sigB = sem("sigB")
        s_up = sem("up")
        s_gu = sem("gu")
        s_ff = sem("ff")
        s_x2 = sem("x2")
        s_dA = sem("dA")
        s_dB = sem("dB")
        s_scan = sem("scan")
        s_state = sem("state")
        s_ht = sem("ht")
        s_acc = sem("acc")

        block = ctx.enter_context(nc.Block())

        def chunks(eng, slots):
            slots(0, 0, True, False, False)
            slots(1, 1, True, True, False)
            with eng.Fori(1, CHUNKS // 2 - 1) as j:
                slots(j * 2, 0, True, True, True)
                slots(j * 2 + 1, 1, True, True, True)
            slots(CHUNKS - 2, 0, True, True, True)
            slots(CHUNKS - 1, 1, False, True, True)

        def of(c, q, u):
            u0 = u % UNITS
            return u0 // EB, u0 % EB, q if 0 <= u < UNITS else 1 - q, c * UNITS + u

        def squares_before(side, c):
            if side == 0:
                backs = max(c - 2, 0) if isinstance(c, int) else c - 2
                return (backs + c) * CT
            fronts = min(c + 3, CHUNKS) if isinstance(c, int) else c + 3
            return (fronts + c) * CT

        def softplus(eng, g, u, c, q):
            for b in range(EB):
                n = c * EB + b + 1
                if u == AT["dt_ln"][b]:
                    eng.wait_ge(s_el, n)
                    g.tensor_tensor(dt[:, q, b, :], dt[:, q, b, :], el[:, :], ALU.add).then_inc(s_log, 1)
                if u == AT["dt_sum"][b]:
                    eng.wait_ge(s_log, n)
                    eng.wait_ge(s_gain, n)
                    g.tensor_tensor(dt[:, q, b, :], dt[:, q, b, :], eo[:, :], ALU.subtract).then_inc(s_dt, 1)
                if u == AT["dtz"][b]:
                    eng.wait_ge(s_dt, n)
                    eng.wait_ge(s_z, n)
                    g.tensor_tensor(dtz[:, q, b, :], dt[:, q, b, :], z[:, q, b, :], ALU.mult).then_inc(s_dtz, 1)

        @block.sync
        def _(sp):
            def load(rows, c, s):
                sp.dma_start(rows, src_c[bass.ds(c, 1)].rearrange("a p t d -> p (a t) d")).then_inc(s, 16)

            def spread_B(c, n):
                if n == 0:
                    sp.wait_ge(s_bt, 16 * (c + 1))
                wait(sp, s_dB, (c * N + n - 1) * EB)
                sp.dma_start(Bn[:, n % 2, :], b_rows[bass.ds(c * N + n, 1)].rearrange("a m -> (a m)").partition_broadcast(P)).then_inc(s_Bn[n % 2], 16)

            def store_B(c):
                sp.wait_ge(s_Bt, c + 1)
                sp.dma_start(b_rows[bass.ds(c * N, N)], Bt[0:N, :]).then_inc(s_bt, 16)

            def store_rows(c):
                sp.wait_ge(s_x2, 2 * (c + 1))
                sp.dma_start(dst_c[bass.ds(c, 1)].rearrange("a p t d -> p (a t) d"), xb[:, :, :]).then_inc(s_stored, 16)
                sp.wait_ge(s_stored, 16 * (c + 1))

            def chunk(c, store, xb_load, xf_load, front):
                for n in range(N):
                    spread_B(c, n)
                    if n == 2:
                        if store:
                            store_rows(c - 2)
                        if xb_load:
                            load(xb[:, :, :], c - 1, s_bld)
                    if n == 6 and xf_load:
                        sp.wait_ge(s_y, CT * (c + 2))
                        load(xf[:, :, :], c + 2, s_fld)
                    if n == 11 and front:
                        store_B(c + 1)
            load(xf[:, :, :], 0, s_fld)
            for name in FFN_WEIGHTS:
                sp.dma_start(w[name][:], ffn[name]).then_inc(s_ffn, 16)
            sp.wait_ge(s_y, CT)
            load(xf[:, :, :], 1, s_fld)
            store_B(0)
            chunk(0, False, False, True, True)
            chunk(1, False, True, True, True)
            with sp.Fori(2, CHUNKS - 2) as c:
                chunk(c, True, True, True, True)
            chunk(CHUNKS - 2, True, True, False, True)
            chunk(CHUNKS - 1, True, True, False, False)
            store_rows(CHUNKS - 2)
            load(xb[:, :, :], CHUNKS - 1, s_bld)
            store_rows(CHUNKS - 1)

        @block.gpsimd
        def _(pool):
            g = nc.gpsimd
            g.memset(nhalf[:, :], -0.5).then_inc(s_init, 1)
            g.memset(state[:, :, :], 0.0).then_inc(s_init, 1)
            pool.wait_ge(s_init, 2)

            def rms(side, c):
                pool.wait_ge(s_ms[side], c + 1)
                g.tensor_tensor(rr[:, side, :], ms[:, side, :], nhalf[:, :], ALU.pow).then_inc(s_rr[side], 1)

            def front(u, c, q):
                if u == AT["pow"]:
                    pool.wait_ge(s_ve, c + 1)
                    g.tensor_tensor(rstd[:, :], ve[:, :], nhalf[:, :], ALU.pow).then_inc(s_rstd, 1)
                if u == AT["front_rms"]:
                    rms(0, c)

            def back(u, c, q):
                for i in range(2):
                    if u == AT["base"][i]:
                        pool.wait_ge(s_xa, 2 * c + i + 1)
                        pool.wait_ge(s_bld, 16 * (c + 1))
                        g.tensor_tensor(xb[:, 2 * i:2 * i + 2, :], xb[:, 2 * i:2 * i + 2, :], xa[:, 2 * i:2 * i + 2, :], ALU.add).then_inc(s_base, 1)
                if u == AT["back_rms"]:
                    rms(1, c)

            def input_of_scan(u, c, q):
                n, k, q, U = of(c, q, u)
                if k == 0:
                    pool.wait_ge(s_Bn[n % 2], (c * N + u // EB - n % 2) * 8 + 16)
                    pool.wait_ge(s_dtz, EB * (c + 1 + u // UNITS))
                wait(pool, s_scan, U - B_BUFS + 1)
                g.tensor_tensor(dB[:, u % B_BUFS, :], dtz[:, q, k, :], Bn[:, n % 2, :], ALU.mult).then_inc(s_dB, 1)

            def slots(c, q, has_front, has_back, has_end):
                for u in range(UNITS):
                    if u + AHEAD < UNITS or has_front:
                        input_of_scan(u + AHEAD, c, q)
                    if has_front:
                        front(u, c + 1, 1 - q)
                        softplus(pool, g, u, c + 1, 1 - q)
                    if has_back:
                        back(u, c - 1, 1 - q)
            for u in range(UNITS):
                front(u, 0, 0)
            for u in range(AHEAD):
                input_of_scan(u, 0, 0)
            chunks(pool, slots)
            for u in range(UNITS):
                back(u, CHUNKS - 1, 1)

        @block.scalar
        def _(act):
            a = nc.scalar
            act.preload_act_table_set("natural_log_exp_and_others")
            act.wait_ge(s_weights, 16 * len(MAMBA_WEIGHTS))
            a.activation(negA[:, :], w["A_log"][:, :], ACT.Exp).then_inc(s_neg, 1)
            act.wait_ge(s_neg, 1)
            a.activation(negA[:, :], negA[:, :], ACT.Copy, scale=-1.0).then_inc(s_neg, 1)
            act.wait_ge(s_neg, 2)

            def squares(side, rows, before, tiles):
                for t in tiles:
                    wait(act, s_sq, before + t)
                    a.activation(sq[:, :], rows[:, t, :], ACT.Square, accum_out=ssq[:, side, t:t + 1]).then_inc(s_sq, 1)

            def front(u, c, q, alone=False):
                if u == AT["front_squares"]:
                    act.wait_ge(s_ln, CT * (c + 1))
                    squares(0, hrow, squares_before(0, c), range(CT))
                if u == AT["front_row"]:
                    act.wait_ge(s_rr[0], c + 1)
                    for t in range(CT):
                        a.activation(hrow[:, t, :], hrow[:, t, :], ACT.Copy, scale=rr[:, 0, t:t + 1]).then_inc(s_hrow, 1)
                if u == AT["hT"]:
                    for d in range(DC):
                        act.wait_ge(s_fullF[d], c * F_USES[d] + 1)
                        wait(act, s_fullF[0], c * F_USES[0])
                        a.activation(hT[:, d, :], pF[d][:, :], ACT.Copy, scale=w["norm1"][:, d:d + 1]).then_inc(s_hT, 1)
                for b in range(EB):
                    n = c * EB + b
                    if u == AT["gate_exp"][b]:
                        act.wait_ge(s_fullF[1], c * F_USES[1] + 2 + b)
                        wait(act, s_z, n)
                        a.activation(eF[:, :], front_bank(1, b, alone)[:, :], ACT.Exp, scale=-1.0).then_inc(s_eF, 1)
                    if u == AT["gate_ln"][b]:
                        act.wait_ge(s_eF, n + 1)
                        a.activation(eF[:, :], eF[:, :], ACT.Ln, bias=1.0).then_inc(s_lnF, 1)
                    if u == AT["gate_sigmoid"][b]:
                        act.wait_ge(s_lnF, n + 1)
                        a.activation(eF[:, :], eF[:, :], ACT.Exp, scale=-1.0).then_inc(s_sigF, 1)
                    if u == AT["dt_exp"][b]:
                        bank = DT_BANK[b]
                        act.wait_ge(s_fullF[bank], (c + 1) * F_USES[bank] - EB // 2 + b // 2 + 1)
                        wait(act, s_gain, n)
                        a.activation(ea[:, :], pF[bank][:, :], ACT.Abs, bias=w["dt_b"][:, b:b + 1]).then_inc(s_ea0, 1)
                        a.activation(dt[:, q, b, :], pF[bank][:, :], ACT.Relu, bias=w["dt_b"][:, b:b + 1]).then_inc(s_relu, 1)
                        act.wait_ge(s_ea0, n + 1)
                        a.activation(ea[:, :], ea[:, :], ACT.Exp, scale=-1.0).then_inc(s_ea, 1)
                    if u == AT["dt_log"][b]:
                        act.wait_ge(s_ea, n + 1)
                        act.wait_ge(s_relu, n + 1)
                        wait(act, s_log, n)
                        a.activation(el[:, :], ea[:, :], ACT.Ln, bias=1.0).then_inc(s_el, 1)
                        wait(act, s_dt, n)
                        a.activation(eo[:, :], ea[:, :], ACT.Copy, bias=1.0).then_inc(s_eo, 1)
                if u == AT["B_copy"]:
                    act.wait_ge(s_fullF[0], (c + 1) * F_USES[0] - EB // 2 - 1)
                    wait(act, s_bt, 16 * c)
                    wait(act, s_C, c)
                    a.activation(Bt[:, :], pF[0][0:2 * N, :], ACT.Copy).then_inc(s_Bt, 1)

            def back(u, c, q, alone=False):
                for i in range(2):
                    if u == AT["back_squares"][i]:
                        act.wait_ge(s_xa, 2 * c + i + 1)
                        squares(1, xa, squares_before(1, c), range(2 * i, 2 * i + 2))
                if u == AT["back_row"]:
                    act.wait_ge(s_rr[1], c + 1)
                    act.wait_ge(s_base, 2 * (c + 1))
                    for t in range(CT):
                        a.activation(xa[:, t, :], xa[:, t, :], ACT.Copy, scale=rr[:, 1, t:t + 1]).then_inc(s_hn, 1)
                if u == AT["hnT"]:
                    for d in range(DC):
                        act.wait_ge(s_fullK[d], c * K_USES + 2)
                        a.activation(hnT[:, d, :], pK[d][:, :], ACT.Copy, scale=w["norm2"][:, d:d + 1]).then_inc(s_hnT, 1)
                for b in range(FB):
                    m = P if b < FB - 1 else F_LAST
                    if u == AT["ffn_exp"][b]:
                        act.wait_ge(s_fullK[0], c * K_USES + 3 + b)
                        wait(act, s_ff, c * FB + b)
                        a.activation(eB[0:m, :], back_bank(0, b, alone)[0:m, :], ACT.Exp, scale=-1.0).then_inc(s_eB, 1)
                    if u == AT["ffn_up_copy"][b]:
                        act.wait_ge(s_fullK[1], c * K_USES + 3 + b)
                        a.activation(ff[0:m, b, :], back_bank(1, b, alone)[0:m, :], ACT.Copy).then_inc(s_up, 1)
                    if u == AT["ffn_ln"][b]:
                        act.wait_ge(s_eB, c * FB + b + 1)
                        a.activation(eB[0:m, :], eB[0:m, :], ACT.Ln, bias=1.0).then_inc(s_lnB, 1)
                    if u == AT["ffn_sigmoid"][b]:
                        act.wait_ge(s_lnB, c * FB + b + 1)
                        a.activation(eB[0:m, :], eB[0:m, :], ACT.Exp, scale=-1.0).then_inc(s_sigB, 1)

            def decay(u, c, q):
                n, k, q, U = of(c, q, u)
                if k == 0:
                    act.wait_ge(s_dt, EB * (c + 1 + u // UNITS))
                wait(act, s_scan, U - A_BUFS + 1)
                a.activation(dA[:, u % A_BUFS, :], dt[:, q, k, :], ACT.Exp, scale=negA[:, k * N + n:k * N + n + 1]).then_inc(s_dA, 1)

            def keep_state(u, c):
                n, _, _, U = of(c, 0, u)
                act.wait_ge(s_scan, U + 1)
                a.activation(state[:, n, :], h[:, n % H_BUFS, :, CH - 1], ACT.Copy).then_inc(s_state, 1)

            def slots(c, q, has_front, has_back, has_end):
                for u in range(UNITS):
                    if u + AHEAD < UNITS or has_front:
                        decay(u + AHEAD, c, q)
                    kept = u - KEEP_LAG
                    if kept % EB == EB - 1 and (kept >= 0 or has_back):
                        keep_state(kept, c)
                    if has_front:
                        front(u, c + 1, 1 - q)
                    if has_back:
                        back(u, c - 1, 1 - q)
            for u in range(UNITS):
                front(u, 0, 0, alone=True)
            for u in range(AHEAD):
                decay(u, 0, 0)
            chunks(act, slots)
            for u in range(UNITS):
                back(u, CHUNKS - 1, 1, alone=True)

        @block.tensor
        def _(pe):
            t_ = nc.tensor

            def turn(bank, parts):
                for i, part in enumerate(parts):
                    last = t_.transpose(bank[:, i * P:(i + 1) * P], part, ident)
                return last

            def front(u, c, q, alone=False):
                if u == AT["front_turn"]:
                    pe.wait_ge(s_hrow, CT * (c + 1))
                    wait(pe, s_C, c)
                    wait(pe, s_ea0, EB * c)
                    wait(pe, s_relu, EB * c)
                    if not isinstance(c, int) or c > 1:
                        pe.wait_ge(s_ssm, EB * (c - 1))
                    for d in range(DC):
                        turn(pF[d], [hrow[:, t, d * P:(d + 1) * P] for t in range(CT)]).then_inc(s_fullF[d], 1)
                for b in range(EB):
                    for bank, name in ((0, "in_w"), (1, "gate_w")):
                        if u == (AT["in"], AT["gate"])[bank][b]:
                            pe.wait_ge(s_hT, DC * (c + 1))
                            wait(pe, (s_z, s_eF)[bank], c * EB + b - (1 if alone and b else 0))
                            for d in range(DC):
                                last = t_.matmul(front_bank(bank, b, alone)[:, :], w[name][:, d, b * P:(b + 1) * P], hT[:, d, :],
                                                 start=(d == 0), stop=(d == DC - 1))
                            last.then_inc(s_fullF[bank], 1)
                    for half in range(2):
                        if u == AT["dt"][2 * b + half]:
                            if half == 0:
                                pe.wait_ge(s_z, EB * (c + 1))
                                if b == 0:
                                    pe.wait_ge(s_eF, EB * (c + 1))
                                elif b == 1:
                                    pe.wait_ge(s_C, c + 1)
                                else:
                                    pe.wait_ge(s_ea0, c * EB + b - 1)
                                    pe.wait_ge(s_relu, c * EB + b - 1)
                            for d in range(half * EB // 2, (half + 1) * EB // 2):
                                last = t_.matmul(pF[DT_BANK[b]][:, :], w["dt_w"][:, d, b * P:(b + 1) * P], z[:, q, d, :],
                                                 start=(d == 0), stop=(d == EB - 1))
                            if half == 1:
                                last.then_inc(s_fullF[DT_BANK[b]], 1)
                if u == AT["B"]:
                    pe.wait_ge(s_z, EB * (c + 1))
                    for d in range(EB):
                        last = t_.matmul(pF[0][0:2 * N, :], w["bc_w"][:, d, :], z[:, q, d, :], start=(d == 0), stop=(d == EB - 1))
                    last.then_inc(s_fullF[0], 1)
                if u == AT["C"]:
                    for t in range(CT):
                        last = t_.transpose(pF[0][:, t * 2 * N:(t + 1) * 2 * N], Bt[:, t * P:(t + 1) * P], ident[0:2 * N, 0:2 * N])
                    last.then_inc(s_fullF[0], 1)

            def back(u, c, q, alone=False):
                for t in range(CT):
                    if u == AT["sum_turn"][t]:
                        pe.wait_ge(s_acc, UNITS * (c + 1) - CT + t + 1)
                        if t == 0:
                            wait(pe, s_x2, 2 * c)
                            fronts = min(c + 2, CHUNKS) if isinstance(c, int) else c + 2
                            pe.wait_ge(s_C, fronts)
                            pe.wait_ge(s_ea0, fronts * EB)
                            pe.wait_ge(s_relu, fronts * EB)
                        for b in range(EB):
                            last = t_.transpose(pY[b][:, t * P:(t + 1) * P], acc[:, t, b * P:(b + 1) * P], ident)
                        last.then_inc(s_yT, 1)
                for t in range(CT):
                    if u == AT["out"][t]:
                        pe.wait_ge(s_ssm, EB * (c + 1))
                        for d in range(EB):
                            last = t_.matmul(pK[t // 2][:, (t % 2) * D:(t % 2 + 1) * D], z[:, q, d, t * P:(t + 1) * P],
                                             w["out_w"][:, d, :], start=(d == 0), stop=(d == EB - 1))
                        if t % 2 == 1:
                            last.then_inc(s_fullK[t // 2], 1)
                if u == AT["back_turn"]:
                    pe.wait_ge(s_hn, CT * (c + 1))
                    for d in range(DC):
                        turn(pK[d], [xa[:, t, d * P:(d + 1) * P] for t in range(CT)]).then_inc(s_fullK[d], 1)
                for b in range(FB):
                    m = P if b < FB - 1 else F_LAST
                    for bank, name in ((0, "fg_w"), (1, "fu_w")):
                        if u == (AT["ffn_gate_product"], AT["ffn_up_product"])[bank][b]:
                            pe.wait_ge(s_hnT, DC * (c + 1))
                            used = c * FB + b - (1 if alone and b else 0)
                            wait(pe, (s_gu, s_up)[bank], used)
                            if bank == 0:
                                wait(pe, s_eB, used)
                            for d in range(DC):
                                last = t_.matmul(back_bank(bank, b, alone)[0:m, :], w[name][:, d, b * P:b * P + m], hnT[:, d, :],
                                                 start=(d == 0), stop=(d == DC - 1))
                            last.then_inc(s_fullK[bank], 1)
                for t in range(CT):
                    for half in range(2):
                        if u == AT["down"][2 * t + half]:
                            pe.wait_ge(s_ff, FB * (c + 1))
                            for b in range(half * FB // 2, (half + 1) * FB // 2):
                                m = P if b < FB - 1 else F_LAST
                                rhs = w["fd_w"][:, b, :] if b < FB - 1 else w["fd_last"][:, :]
                                last = t_.matmul(pK[t // 2][:, (t % 2) * D:(t % 2 + 1) * D], ff[0:m, b, t * P:(t + 1) * P],
                                                 rhs, start=(b == 0), stop=(b == FB - 1))
                            if t % 2 == 1 and half == 1:
                                last.then_inc(s_fullK[t // 2], 1)

            def states(v, c):
                n, t, _, V = of(c, 0, v)
                pe.wait_ge(s_scan, V - t + EB)
                wait(pe, s_acc, V - HT_BANKS + 1)
                turn(pH[v % HT_BANKS], [h[:, n % H_BUFS, k, t * P:(t + 1) * P] for k in range(EB)]).then_inc(s_ht, 1)

            def slots(c, q, has_front, has_back, has_end):
                for u in range(UNITS):
                    if has_front and u == AT["C"]:
                        pe.wait_ge(s_Bt, c + 2)
                    if u >= TURN_LAG or has_back:
                        states(u - TURN_LAG, c)
                    if has_front:
                        front(u, c + 1, 1 - q)
                    if has_end and u < END:
                        back(UNITS + u, c - 2, q)
                    if has_back:
                        back(u, c - 1, 1 - q)
            pe.wait_ge(s_weights, 16 * len(MAMBA_WEIGHTS))
            for u in range(UNITS):
                if u == AT["C"]:
                    pe.wait_ge(s_Bt, 1)
                front(u, 0, 0, alone=True)
            pe.wait_ge(s_ffn, 16 * len(FFN_WEIGHTS))
            chunks(pe, slots)
            for u in range(END):
                if u < TURN_LAG:
                    states(UNITS - TURN_LAG + u, CHUNKS - 1)
                back(UNITS + u, CHUNKS - 2, 0)
            for u in range(UNITS + END):
                back(u, CHUNKS - 1, 1, alone=True)

        @block.vector
        def _(dve):
            v_ = nc.vector
            dve.wait_ge(s_weights, 16 * len(MAMBA_WEIGHTS))
            dve.wait_ge(s_init, 2)

            def mean_square(side, c):
                dve.wait_ge(s_sq, squares_before(side, c) + CT)
                v_.tensor_scalar(ms[:, side, :], ssq[:, side, :], 1.0 / D, RMS_EPS, ALU.mult, ALU.add).then_inc(s_ms[side], 1)

            def normalise(rows, s):
                for t in range(CT):
                    v_.tensor_scalar(rows[:, t, :], xf[:, t, :], mv[:, t, 0:1], rstd[:, t:t + 1],
                                     ALU.subtract, ALU.mult).then_inc(s, 1)

            def front(u, c, q, alone=False):
                if u == AT["statistics"]:
                    dve.wait_ge(s_fld, 16 * (c + 1))
                    for t in range(CT):
                        v_.bn_stats(stats[:, t, :], xf[:, t, :]).then_inc(s_bns, 1)
                if u == AT["variance"]:
                    for t in range(CT):
                        v_.bn_aggr(mv[:, t, :], stats[:, t, :]).then_inc(s_bna, 1)
                    dve.wait_ge(s_bna, CT * (c + 1))
                    v_.tensor_scalar(ve[:, :], mv[:, :, 1], LN_EPS, None, ALU.add).then_inc(s_ve, 1)
                if u == AT["layernorm"]:
                    dve.wait_ge(s_rstd, c + 1)
                    wait(dve, s_hT, DC * c)
                    normalise(hrow, s_ln)
                if u == AT["front_mean"]:
                    mean_square(0, c)
                if u == AT["residual"]:
                    if not isinstance(c, int) or c > 1:
                        dve.wait_ge(s_xa, 2 * (c - 1))
                    normalise(yln[:, q], s_y)
                for b in range(EB):
                    if u == AT["z"][b]:
                        dve.wait_ge(s_sigF, c * EB + b + 1)
                        dve.wait_ge(s_fullF[0], c * F_USES[0] + 2 + b)
                        v_.tensor_tensor(z[:, q, b, :], eF[:, :], front_bank(0, b, alone)[:, :], ALU.mult).then_inc(s_z, 1)
                for b in range(EB):
                    if u == AT["dt_low"][b]:
                        dve.wait_ge(s_eo, c * EB + b + 1)
                        v_.scalar_tensor_tensor(eo[:, :], eo[:, :], 1.0, ea[:, :], op0=ALU.subtract, op1=ALU.subtract).then_inc(s_gain, 1)
                if u == AT["C_copy"]:
                    dve.wait_ge(s_fullF[0], (c + 1) * F_USES[0] - EB // 2)
                    v_.tensor_copy(C[:, q, :, :], pF[0][:, 0:CT * 2 * N].rearrange("p (t n) -> p t n", t=CT)[:, :, N:2 * N]).then_inc(s_C, 1)

            def back(u, c, q, alone=False):
                for i, b in enumerate((2, 3, 0, 1)):
                    if u == AT["ssm"][i]:
                        dve.wait_ge(s_yT, CT * (c + 1))
                        v_.scalar_tensor_tensor(z[:, q, b, :], z[:, q, b, :], w["Dp"][:, b:b + 1], pY[b][:, :],
                                                op0=ALU.mult, op1=ALU.add).then_inc(s_ssm, 1)
                for i in range(2):
                    if u == AT["xa"][i]:
                        dve.wait_ge(s_fullK[i], c * K_USES + 1)
                        v_.tensor_tensor(xa[:, 2 * i:2 * i + 2, :], yln[:, q, 2 * i:2 * i + 2, :],
                                         pK[i][:, :].rearrange("p (t d) -> p t d", t=2), ALU.add).then_inc(s_xa, 1)
                    if u == AT["x2"][i]:
                        dve.wait_ge(s_fullK[i], c * K_USES + 3 + FB)
                        v_.tensor_tensor(xb[:, 2 * i:2 * i + 2, :], xb[:, 2 * i:2 * i + 2, :],
                                         pK[i][:, :].rearrange("p (t d) -> p t d", t=2), ALU.add).then_inc(s_x2, 1)
                if u == AT["back_mean"]:
                    mean_square(1, c)
                for b in range(FB):
                    m = P if b < FB - 1 else F_LAST
                    n = c * FB + b + 1
                    if u == AT["ffn_gate"][b]:
                        dve.wait_ge(s_up, n)
                        dve.wait_ge(s_fullK[0], c * K_USES + 3 + b)
                        v_.tensor_tensor(ff[0:m, b, :], ff[0:m, b, :], back_bank(0, b, alone)[0:m, :], ALU.mult).then_inc(s_gu, 1)
                    if u == AT["ffn_product"][b]:
                        dve.wait_ge(s_sigB, n)
                        dve.wait_ge(s_gu, n)
                        v_.tensor_tensor(ff[0:m, b, :], ff[0:m, b, :], eB[0:m, :], ALU.mult).then_inc(s_ff, 1)

            def scan(u, c, q):
                n, k, _, U = of(c, q, u)
                dve.wait_ge(s_dA, U + 1)
                dve.wait_ge(s_dB, U + 1)
                wait(dve, s_state, c * N + n - H_BUFS + 1)
                wait(dve, s_ht, (c * N + n - H_BUFS + 1) * CT)
                v_.tensor_tensor_scan(h[:, n % H_BUFS, k, :], dA[:, u % A_BUFS, :], dB[:, u % B_BUFS, :],
                                      initial=state[:, n, k:k + 1], op0=ALU.mult, op1=ALU.add).then_inc(s_scan, 1)

            def weigh(v, c, q):
                n, t, q, V = of(c, q, v)
                dve.wait_ge(s_ht, V + 1)
                C_n = C[:, q, t, n:n + 1]
                if n == 0:
                    if not isinstance(c, int) or c > 0:
                        dve.wait_ge(s_yT, (c - 1) * CT + t + 1)
                    v_.tensor_scalar(acc[:, t, :], pH[v % HT_BANKS][:, :], C_n, None, ALU.mult).then_inc(s_acc, 1)
                else:
                    dve.wait_ge(s_acc, V - CT + 1)
                    v_.scalar_tensor_tensor(acc[:, t, :], pH[v % HT_BANKS][:, :], C_n, acc[:, t, :],
                                            op0=ALU.mult, op1=ALU.add).then_inc(s_acc, 1)

            def slots(c, q, has_front, has_back, has_end):
                for u in range(UNITS):
                    if has_front and u == AT["variance"]:
                        dve.wait_ge(s_bns, CT * (c + 2))
                        dve.wait_ge(s_y, CT * (c + 1))
                    scan(u, c, q)
                    if has_end and u < END:
                        back(UNITS + u, c - 2, q)
                    if has_back:
                        back(u, c - 1, 1 - q)
                    if u >= SUM_LAG or has_back:
                        weigh(u - SUM_LAG, c, q)
                    if has_front:
                        front(u, c + 1, 1 - q)
            for u in range(UNITS):
                if u == AT["variance"]:
                    dve.wait_ge(s_bns, CT)
                front(u, 0, 0, alone=True)
                softplus(dve, v_, u, 0, 0)
            chunks(dve, slots)
            for u in range(SUM_LAG):
                if u < END:
                    back(UNITS + u, CHUNKS - 2, 0)
                weigh(UNITS - SUM_LAG + u, CHUNKS - 1, 1)
            for u in range(UNITS + END):
                back(u, CHUNKS - 1, 1, alone=True)


def macaron(nc, x, moe_w, router, bias, consts, *rest):
    out = rest[-1]
    mamba_w = dict(zip([*MAMBA_WEIGHTS, *FFN_WEIGHTS], rest))
    moe_weights = {"moe": moe_w, "router": router, "bias": bias}
    x1 = nc.dram_tensor("x1", (T + P, D), F32, kind="Internal").ap()
    x2 = nc.dram_tensor("x2", (T, D), F32, kind="Internal").ap()
    normed_a, normed_c = (nc.dram_tensor(f"normed_{n}", (T + P, D), F32, kind="Internal").ap() for n in "ac")
    slots_a, slots_c = (nc.dram_tensor(f"slots_{n}", (SLOTS, ENTRY), F32, kind="Internal").ap() for n in "ac")
    b_rows = nc.dram_tensor("b_rows", (CHUNKS * N, CH), F32, kind="Internal").ap()
    with ExitStack() as ctx:
        const = ctx.enter_context(nc.sbuf_tensor("const", [P, CONSTS], F32))
        w = {n: ctx.enter_context(nc.sbuf_tensor(f"w_{n}", s, F32)) for n, s in MAMBA_WEIGHTS.items()}
        s_weights = ctx.enter_context(nc.semaphore("weights"))
        with nc.sbuf_tensor("Wa", [P, E + 1, EXPERT], F32) as W:
            moe(nc, "a", x, x1, normed_a, slots_a, moe_weights, consts, const, W,
                [(w[n][:], mamba_w[n], s_weights) for n in MAMBA_WEIGHTS])
        mamba(nc, x1, x2, b_rows, w, mamba_w, const, s_weights)
        with nc.sbuf_tensor("Wc", [P, E + 1, EXPERT], F32) as W:
            moe(nc, "c", x2, out, normed_c, slots_c, moe_weights, consts, const, W)


def layout(z):
    def blocks(w):
        return np.ascontiguousarray(w.reshape(w.shape[0] // P, P, -1).transpose(1, 0, 2))

    def turned(name):
        return np.ascontiguousarray(z[name].T)

    def expert(w1, w3, w2):
        return np.concatenate([blocks(w).reshape(P, -1) for w in (w1, w3, w2)], axis=1)
    f, a = "L0_ffn_", "L0_attn_"
    experts = [expert(z[f + "w1"][e], z[f + "w3"][e], z[f + "w2"][e]) for e in range(E)]
    experts.append(expert(z[f + "sw1"][0], z[f + "sw3"][0], z[f + "sw2"][0]))
    down = turned(a + "ffn_down_w")
    whole = (FB - 1) * P
    return {
        "x": z[a + "x"].reshape(T, D),
        "moe": np.stack(experts),
        "router": blocks(turned(f + "router_w")),
        "bias": z[f + "experts_bias"],
        "consts": constants(),
        "in_w": blocks(turned(a + "in_proj_w")),
        "gate_w": blocks(turned(a + "gate_proj_w")),
        "dt_w": blocks(turned(a + "dt_w")),
        "bc_w": blocks(turned(a + "x_proj_w")),
        "out_w": blocks(turned(a + "out_proj_w")),
        "norm1": z[a + "norm1_w"].reshape(DC, P).T,
        "norm2": z[a + "ffn_norm_w"].reshape(DC, P).T,
        "dt_b": z[a + "dt_b"].reshape(EB, P).T,
        "A_log": blocks(z[a + "A_log"]).reshape(P, EB * N),
        "Dp": z[a + "Dp"].reshape(EB, P).T,
        "fg_w": blocks(turned(a + "ffn_gate_w")),
        "fu_w": blocks(turned(a + "ffn_up_w")),
        "fd_w": blocks(down[:whole]),
        "fd_last": down[whole:],
    }


def kernel(**inputs):
    import concourse.bacc as _bacc
    from concourse.bass_utils import run_bass_kernel_spmd as _run

    nc = _bacc.Bacc("TRN2", target_bir_lowering=False, num_devices=1)
    arrays = {name: np.ascontiguousarray(a) for name, a in layout({n: np.asarray(v) for n, v in inputs.items()}).items()}
    args = [nc.dram_tensor(name, a.shape, mybir.dt.from_np(a.dtype), kind="ExternalInput").ap() for name, a in arrays.items()]
    args.append(nc.dram_tensor("out", (T + P, D), F32, kind="ExternalOutput").ap())
    macaron(nc, *args)
    r = _run(nc, [arrays], core_ids=[0])
    return r.results[0]["out"][:T].reshape(1, T, D)
```
